# Optimizing a Trainium2 kernel written in Bass

```python
import numpy as np
import jax
import jax.numpy as jnp

def _softmax(x, axis=-1):
    return jax.nn.softmax(x, axis=axis)

def _gelu(x):
    return jax.nn.gelu(x, approximate=True)

def _silu(x):
    return jax.nn.silu(x)

def _sigmoid(x):
    return jax.nn.sigmoid(x)

def _layernorm(x, axis=-1, eps=1e-05):
    m = jnp.mean(x, axis=axis, keepdims=True)
    v = jnp.var(x, axis=axis, keepdims=True)
    return (x - m) / jnp.sqrt(v + eps)

def _scatter_add(tgt, idx, src, axis=0):
    return tgt.at[idx].add(src)

def _segment_sum(src, seg, n):
    return jax.ops.segment_sum(src, seg, n)
kernel_name = 'mk_xattn_ffn_d2_seqx_r8_448203'

def setup_inputs(seed: int=0):
    np.random.seed(seed)
    _w = jnp.asarray

    def _rec_inputs():
        import jax
        import jax.numpy as jnp
        _rk = jax.random.key(seed)
        x = 7.22e-05 + 1 * jax.random.normal(jax.random.fold_in(_rk, 1), (8, 56, 128), jnp.float32)
        _lenS = 56 - jax.random.randint(jax.random.fold_in(_rk, 7), (8,), 0, max(1, 56 // 4) + 1, jnp.int32)
        _lenS2 = 1500 - jax.random.randint(jax.random.fold_in(_rk, 8), (8,), 0, max(1, 1500 // 4) + 1, jnp.int32)
        _ctx_1024P = jax.random.normal(jax.random.fold_in(_rk, 11), (8, 16, 128), jnp.float32)
        _ctx_1024c = jax.random.dirichlet(jax.random.fold_in(_rk, 511), 0.3 * jnp.ones((16,), jnp.float32), (8, 1500))
        _ctx_1024t = jnp.einsum('bsk,bkd->bsd', _ctx_1024c, _ctx_1024P)
        _ctx_1024t = _ctx_1024t * jax.lax.rsqrt(jnp.mean(jnp.square(_ctx_1024t)) + 1e-12) * 0.953939
        ctx_1024 = 4.13588e-05 + 0.999923 * (_ctx_1024t + 0.3 * jax.random.normal(jax.random.fold_in(_rk, 611), (8, 1500, 128), jnp.float32))
        itok_BxS_0_255 = jax.random.randint(jax.random.fold_in(_rk, 12), (8, 56), 0, 32, jnp.int32)
        return (x, ctx_1024, itok_BxS_0_255)
    x, ctx_1024, itok_BxS_0_255 = _rec_inputs()

    def _L0_xattn_setup():
        import jax, jax.numpy as jnp
        import numpy as np
        N_HEAD = 16
        key = jax.random.key(seed)
        ks = jax.random.split(key, 5)
        b, l, d = (4, 256, 128)
        dh = d // N_HEAD
        return {'q': jax.random.normal(ks[0], (b, l, d), dtype=jnp.float32), 'kv': jax.random.normal(ks[1], (b, l, d), dtype=jnp.float32), 'Wq': jax.random.normal(ks[2], (d, d), dtype=jnp.float32) * 0.02, 'Wkv': jax.random.normal(ks[3], (2 * dh, d), dtype=jnp.float32) * 0.02, 'Wc': jax.random.normal(ks[4], (d, d), dtype=jnp.float32) * 0.02}
    _L0_xattn_all = _L0_xattn_setup()
    _L0_xattn_in = {k: v for k, v in _L0_xattn_all.items() if k in ('Wq', 'Wkv', 'Wc')}
    del _L0_xattn_all

    def _L0_ffn_setup():
        import jax, jax.numpy as jnp
        import numpy as np
        ALPHA = 1.702
        LIMIT = 7.0
        EPS = 1e-05
        E = 16
        K = 4

        def _swiglu(h):
            x_glu = jnp.minimum(h[..., ::2], LIMIT)
            x_lin = jnp.clip(h[..., 1::2], LIMIT, LIMIT)
            return x_glu * jax.nn.sigmoid(ALPHA * x_glu) * (x_lin + 1.0)
        key = jax.random.key(seed)
        ks = jax.random.split(key, 7)
        B, T, H, I = (1, 256, 128, 128)
        x = jax.random.normal(ks[0], (B, T, H), jnp.float32)
        scale = jnp.ones((H,), jnp.float32)
        gate_w = jax.random.normal(ks[1], (E, H), jnp.float32) * 0.02
        gate_b = jnp.zeros((E,), jnp.float32)
        mlp1_w = jax.random.normal(ks[2], (E, 2 * I, H), jnp.float32) * 0.02
        mlp1_b = jax.random.normal(ks[3], (E, 2 * I), jnp.float32) * 0.02
        mlp2_w = jax.random.normal(ks[4], (E, H, I), jnp.float32) * 0.02
        mlp2_b = jax.random.normal(ks[5], (E, H), jnp.float32) * 0.02
        return dict(x=x, scale=scale, gate_w=gate_w, gate_b=gate_b, mlp1_w=mlp1_w, mlp1_b=mlp1_b, mlp2_w=mlp2_w, mlp2_b=mlp2_b)
    _L0_ffn_all = _L0_ffn_setup()
    _L0_ffn_in = {k: v for k, v in _L0_ffn_all.items() if k in ('scale', 'gate_w', 'gate_b', 'mlp1_w', 'mlp1_b', 'mlp2_w', 'mlp2_b')}
    del _L0_ffn_all

    def _L1_xattn_setup():
        import jax, jax.numpy as jnp
        import numpy as np
        N_LAYERS = 4
        H = 16
        LOOKBACK = 128
        EPS = 1e-06
        ROPE_BASE = 10000.0
        NEG = jnp.float32(-1e+30)

        def rmsnorm(x, w):
            return x * jax.lax.rsqrt(jnp.mean(x * x, axis=-1, keepdims=True) + EPS) * w

        def rope_cache(L, hd):
            inv = 1.0 / ROPE_BASE ** (jnp.arange(0, hd, 2, dtype=jnp.float32) / hd)
            t = jnp.arange(L, dtype=jnp.float32)
            f = t[:, None] * inv[None, :]
            emb = jnp.concatenate([f, f], axis=-1)
            return (jnp.cos(emb), jnp.sin(emb))

        def apply_rope(x, cos, sin):
            d = x.shape[-1]
            x1, x2 = (x[..., :d // 2], x[..., d // 2:])
            rot = jnp.concatenate([-x2, x1], axis=-1)
            return x * cos + rot * sin

        def split_heads(x, n_heads):
            B, L, D = x.shape
            return x.reshape(B, L, n_heads, D // n_heads).transpose(0, 2, 1, 3)

        def merge_heads(x):
            B, h, L, d = x.shape
            return x.transpose(0, 2, 1, 3).reshape(B, L, h * d)

        def sdpa(q, k, v, bias):
            scale = q.shape[-1] ** (-0.5)
            s = jnp.einsum('bhqd,bhkd->bhqk', q, k) * scale + bias
            p = jax.nn.softmax(s, axis=-1)
            return jnp.einsum('bhqk,bhkd->bhqd', p, v)

        def forward(x, memory, seg_ids, Wqkv, bqkv, Wo, bo, Wq_c, Wkv_c, Wo_c, Wg, Wu, Wd, n1, n2, n3, nf):
            B, L, D = x.shape
            S = memory.shape[1]
            hd = D // H
            cos, sin = rope_cache(L, hd)
            i = jnp.arange(L)
            causal_bias = jnp.where(i[None, :] <= i[:, None], 0.0, NEG)[None, None]
            j = jnp.arange(S)
            allowed = (j[None, None, :] <= seg_ids[:, :, None]) & (j[None, None, :] > seg_ids[:, :, None] - LOOKBACK)
            cross_bias = jnp.where(allowed, 0.0, NEG)[:, None]
            for l in range(N_LAYERS):
                h = rmsnorm(x, n1[l])
                qkv = h @ Wqkv[l].T + bqkv[l]
                q, k, v = jnp.split(qkv, 3, axis=-1)
                q = apply_rope(split_heads(q, H), cos, sin)
                k = apply_rope(split_heads(k, H), cos, sin)
                v = split_heads(v, H)
                o = merge_heads(sdpa(q, k, v, causal_bias)) @ Wo[l].T + bo[l]
                x = x + o
                h2 = rmsnorm(x, n2[l])
                qc = split_heads(h2 @ Wq_c[l].T, H)
                kv = memory @ Wkv_c[l].T
                kc, vc = jnp.split(kv, 2, axis=-1)
                kc, vc = (split_heads(kc, H), split_heads(vc, H))
                oc = merge_heads(sdpa(qc, kc, vc, cross_bias)) @ Wo_c[l].T
                x = x + oc
                h3 = rmsnorm(x, n3[l])
                x = x + jax.nn.silu(h3 @ Wg[l].T) * (h3 @ Wu[l].T) @ Wd[l].T
            return rmsnorm(x, nf)
        key = jax.random.key(seed)
        ks = jax.random.split(key, 16)
        B, L, S, D, F = (2, 256, 32, 128, 512)
        w = 0.02
        inp = {'x': jax.random.normal(ks[0], (B, L, D), jnp.float32), 'memory': jax.random.normal(ks[1], (B, S, D), jnp.float32), 'seg_ids': jnp.sort(jax.random.randint(ks[2], (B, L), 0, S), axis=-1), 'Wqkv': jax.random.normal(ks[3], (N_LAYERS, 3 * D, D), jnp.float32) * w, 'bqkv': jnp.zeros((N_LAYERS, 3 * D), jnp.float32), 'Wo': jax.random.normal(ks[4], (N_LAYERS, D, D), jnp.float32) * w, 'bo': jnp.zeros((N_LAYERS, D), jnp.float32), 'Wq_c': jax.random.normal(ks[5], (N_LAYERS, D, D), jnp.float32) * w, 'Wkv_c': jax.random.normal(ks[6], (N_LAYERS, 2 * D, D), jnp.float32) * w, 'Wo_c': jax.random.normal(ks[7], (N_LAYERS, D, D), jnp.float32) * w, 'Wg': jax.random.normal(ks[8], (N_LAYERS, F, D), jnp.float32) * w, 'Wu': jax.random.normal(ks[9], (N_LAYERS, F, D), jnp.float32) * w, 'Wd': jax.random.normal(ks[10], (N_LAYERS, D, F), jnp.float32) * w, 'n1': jnp.ones((N_LAYERS, D), jnp.float32), 'n2': jnp.ones((N_LAYERS, D), jnp.float32), 'n3': jnp.ones((N_LAYERS, D), jnp.float32), 'nf': jnp.ones((D,), jnp.float32)}
        return inp
    _L1_xattn_all = _L1_xattn_setup()
    _L1_xattn_in = {k: v for k, v in _L1_xattn_all.items() if k in ('Wqkv', 'bqkv', 'Wo', 'bo', 'Wq_c', 'Wkv_c', 'Wo_c', 'Wg', 'Wu', 'Wd', 'n1', 'n2', 'n3', 'nf')}
    del _L1_xattn_all

    def _L1_ffn_setup():
        import jax, jax.numpy as jnp
        import numpy as np
        EPS = 1e-08

        def _ste(x, q):
            return x + jax.lax.stop_gradient(q - x)

        def quant_act_uint8(x):
            s = jax.lax.stop_gradient(jnp.maximum(jnp.max(x), EPS)) / 255.0
            q = jnp.clip(jnp.round(x / s), 0.0, 255.0) * s
            return (_ste(x, q), s)

        def quant_weight_int8_perchannel(w):
            s = jax.lax.stop_gradient(jnp.maximum(jnp.max(jnp.abs(w), axis=1, keepdims=True), EPS)) / 127.0
            q = jnp.clip(jnp.round(w / s), -128.0, 127.0) * s
            return (_ste(w, q), s[:, 0])

        def quant_bias_int32(b, s_in, s_w):
            s = jax.lax.stop_gradient(s_in * s_w)
            q = jnp.round(b / s) * s
            return _ste(b, q)

        def quant_linear(x, w, b):
            xq, s_in = quant_act_uint8(x)
            wq, s_w = quant_weight_int8_perchannel(w)
            bq = quant_bias_int32(b, s_in, s_w)
            return jnp.einsum('btd,fd->btf', xq, wq) + bq
        key = jax.random.key(seed)
        k1, k2, k3, k4, k5 = jax.random.split(key, 5)
        B, S, D, F = (4, 256, 128, 512)
        return {'x': jax.random.normal(k1, (B, S, D), dtype=jnp.float32), 'w1': jax.random.normal(k2, (F, D), dtype=jnp.float32) * (1.0 / np.sqrt(D)), 'b1': jax.random.normal(k3, (F,), dtype=jnp.float32) * 0.01, 'w2': jax.random.normal(k4, (D, F), dtype=jnp.float32) * (1.0 / np.sqrt(F)), 'b2': jax.random.normal(k5, (D,), dtype=jnp.float32) * 0.01}
    _L1_ffn_all = _L1_ffn_setup()
    _L1_ffn_in = {k: v for k, v in _L1_ffn_all.items() if k in ('w1', 'b1', 'w2', 'b2')}
    del _L1_ffn_all
    return {'x': x, 'ctx_1024': ctx_1024, 'itok_BxS_0_255': itok_BxS_0_255, 'L0_xattn_Wq': _L0_xattn_in['Wq'], 'L0_xattn_Wkv': _L0_xattn_in['Wkv'], 'L0_xattn_Wc': _L0_xattn_in['Wc'], 'L0_ffn_scale': _L0_ffn_in['scale'], 'L0_ffn_gate_w': _L0_ffn_in['gate_w'], 'L0_ffn_gate_b': _L0_ffn_in['gate_b'], 'L0_ffn_mlp1_w': _L0_ffn_in['mlp1_w'], 'L0_ffn_mlp1_b': _L0_ffn_in['mlp1_b'], 'L0_ffn_mlp2_w': _L0_ffn_in['mlp2_w'], 'L0_ffn_mlp2_b': _L0_ffn_in['mlp2_b'], 'L1_xattn_Wqkv': _L1_xattn_in['Wqkv'], 'L1_xattn_bqkv': _L1_xattn_in['bqkv'], 'L1_xattn_Wo': _L1_xattn_in['Wo'], 'L1_xattn_bo': _L1_xattn_in['bo'], 'L1_xattn_Wq_c': _L1_xattn_in['Wq_c'], 'L1_xattn_Wkv_c': _L1_xattn_in['Wkv_c'], 'L1_xattn_Wo_c': _L1_xattn_in['Wo_c'], 'L1_xattn_Wg': _L1_xattn_in['Wg'], 'L1_xattn_Wu': _L1_xattn_in['Wu'], 'L1_xattn_Wd': _L1_xattn_in['Wd'], 'L1_xattn_n1': _L1_xattn_in['n1'], 'L1_xattn_n2': _L1_xattn_in['n2'], 'L1_xattn_n3': _L1_xattn_in['n3'], 'L1_xattn_nf': _L1_xattn_in['nf'], 'L1_ffn_w1': _L1_ffn_in['w1'], 'L1_ffn_b1': _L1_ffn_in['b1'], 'L1_ffn_w2': _L1_ffn_in['w2'], 'L1_ffn_b2': _L1_ffn_in['b2']}

def reference(x, ctx_1024, itok_BxS_0_255, L0_xattn_Wq, L0_xattn_Wkv, L0_xattn_Wc, L0_ffn_scale, L0_ffn_gate_w, L0_ffn_gate_b, L0_ffn_mlp1_w, L0_ffn_mlp1_b, L0_ffn_mlp2_w, L0_ffn_mlp2_b, L1_xattn_Wqkv, L1_xattn_bqkv, L1_xattn_Wo, L1_xattn_bo, L1_xattn_Wq_c, L1_xattn_Wkv_c, L1_xattn_Wo_c, L1_xattn_Wg, L1_xattn_Wu, L1_xattn_Wd, L1_xattn_n1, L1_xattn_n2, L1_xattn_n3, L1_xattn_nf, L1_ffn_w1, L1_ffn_b1, L1_ffn_w2, L1_ffn_b2):
    import jax
    import jax.numpy as jnp

    def _L0_xattn_ref(q, kv, Wq, Wkv, Wc):
        import jax, jax.numpy as jnp
        import numpy as np
        N_HEAD = 16
        b, l, d = q.shape
        h = N_HEAD
        dh = d // h
        qp = jnp.einsum('bld,ed->ble', q, Wq)
        scores = jnp.einsum('bld,bmd->blm', qp, kv)
        idx = jnp.argmax(scores, axis=-1)
        mem = jnp.take_along_axis(kv, idx[..., None], axis=1)
        mkv = jnp.einsum('bld,ed->ble', mem, Wkv)
        mk, mv = jnp.split(mkv, 2, axis=-1)
        qh = qp.reshape(b, l, h, dh).transpose(0, 2, 1, 3)
        scale = 1.0 / np.sqrt(dh).astype(np.float32)
        logits = jnp.einsum('bhld,bmd->bhlm', qh, mk) * scale
        attn = jax.nn.softmax(logits, axis=-1)
        out = jnp.einsum('bhlm,bmd->bhld', attn, mv)
        out = out.transpose(0, 2, 1, 3).reshape(b, l, d)
        return jnp.einsum('bld,ed->ble', out, Wc)

    def _L0_ffn_ref(x, scale, gate_w, gate_b, mlp1_w, mlp1_b, mlp2_w, mlp2_b):
        import jax, jax.numpy as jnp
        import numpy as np
        ALPHA = 1.702
        LIMIT = 7.0
        EPS = 1e-05
        E = 16
        K = 4

        def _swiglu(h):
            x_glu = jnp.minimum(h[..., ::2], LIMIT)
            x_lin = jnp.clip(h[..., 1::2], LIMIT, LIMIT)
            return x_glu * jax.nn.sigmoid(ALPHA * x_glu) * (x_lin + 1.0)
        t = x * jax.lax.rsqrt(jnp.mean(x * x, axis=-1, keepdims=True) + EPS) * scale
        g = jnp.einsum('bth,eh->bte', t, gate_w) + gate_b
        vals, idx = jax.lax.top_k(g, K)
        w = jax.nn.softmax(vals, axis=-1)
        route = jnp.sum(jax.nn.one_hot(idx, E, dtype=t.dtype) * w[..., None], axis=-2)
        route_e = jnp.moveaxis(route, -1, 0)

        def step(acc, p):
            w1, b1, w2, b2, r = p
            h = jnp.einsum('bth,ih->bti', t, w1) + b1
            s = _swiglu(h)
            y = jnp.einsum('bti,hi->bth', s, w2) + b2
            return (acc + r[..., None] * y, None)
        acc, _ = jax.lax.scan(step, jnp.zeros_like(x), (mlp1_w, mlp1_b, mlp2_w, mlp2_b, route_e))
        return x + acc

    def _L1_xattn_ref(x, memory, seg_ids, Wqkv, bqkv, Wo, bo, Wq_c, Wkv_c, Wo_c, Wg, Wu, Wd, n1, n2, n3, nf):
        import jax, jax.numpy as jnp
        import numpy as np
        N_LAYERS = 4
        H = 16
        LOOKBACK = 128
        EPS = 1e-06
        ROPE_BASE = 10000.0
        NEG = jnp.float32(-1e+30)

        def rmsnorm(x, w):
            return x * jax.lax.rsqrt(jnp.mean(x * x, axis=-1, keepdims=True) + EPS) * w

        def rope_cache(L, hd):
            inv = 1.0 / ROPE_BASE ** (jnp.arange(0, hd, 2, dtype=jnp.float32) / hd)
            t = jnp.arange(L, dtype=jnp.float32)
            f = t[:, None] * inv[None, :]
            emb = jnp.concatenate([f, f], axis=-1)
            return (jnp.cos(emb), jnp.sin(emb))

        def apply_rope(x, cos, sin):
            d = x.shape[-1]
            x1, x2 = (x[..., :d // 2], x[..., d // 2:])
            rot = jnp.concatenate([-x2, x1], axis=-1)
            return x * cos + rot * sin

        def split_heads(x, n_heads):
            B, L, D = x.shape
            return x.reshape(B, L, n_heads, D // n_heads).transpose(0, 2, 1, 3)

        def merge_heads(x):
            B, h, L, d = x.shape
            return x.transpose(0, 2, 1, 3).reshape(B, L, h * d)

        def sdpa(q, k, v, bias):
            scale = q.shape[-1] ** (-0.5)
            s = jnp.einsum('bhqd,bhkd->bhqk', q, k) * scale + bias
            p = jax.nn.softmax(s, axis=-1)
            return jnp.einsum('bhqk,bhkd->bhqd', p, v)

        def forward(x, memory, seg_ids, Wqkv, bqkv, Wo, bo, Wq_c, Wkv_c, Wo_c, Wg, Wu, Wd, n1, n2, n3, nf):
            B, L, D = x.shape
            S = memory.shape[1]
            hd = D // H
            cos, sin = rope_cache(L, hd)
            i = jnp.arange(L)
            causal_bias = jnp.where(i[None, :] <= i[:, None], 0.0, NEG)[None, None]
            j = jnp.arange(S)
            allowed = (j[None, None, :] <= seg_ids[:, :, None]) & (j[None, None, :] > seg_ids[:, :, None] - LOOKBACK)
            cross_bias = jnp.where(allowed, 0.0, NEG)[:, None]
            for l in range(N_LAYERS):
                h = rmsnorm(x, n1[l])
                qkv = h @ Wqkv[l].T + bqkv[l]
                q, k, v = jnp.split(qkv, 3, axis=-1)
                q = apply_rope(split_heads(q, H), cos, sin)
                k = apply_rope(split_heads(k, H), cos, sin)
                v = split_heads(v, H)
                o = merge_heads(sdpa(q, k, v, causal_bias)) @ Wo[l].T + bo[l]
                x = x + o
                h2 = rmsnorm(x, n2[l])
                qc = split_heads(h2 @ Wq_c[l].T, H)
                kv = memory @ Wkv_c[l].T
                kc, vc = jnp.split(kv, 2, axis=-1)
                kc, vc = (split_heads(kc, H), split_heads(vc, H))
                oc = merge_heads(sdpa(qc, kc, vc, cross_bias)) @ Wo_c[l].T
                x = x + oc
                h3 = rmsnorm(x, n3[l])
                x = x + jax.nn.silu(h3 @ Wg[l].T) * (h3 @ Wu[l].T) @ Wd[l].T
            return rmsnorm(x, nf)
        return forward(x, memory, seg_ids, Wqkv, bqkv, Wo, bo, Wq_c, Wkv_c, Wo_c, Wg, Wu, Wd, n1, n2, n3, nf)

    def _L1_ffn_ref(x, w1, b1, w2, b2):
        import jax, jax.numpy as jnp
        import numpy as np
        EPS = 1e-08

        def _ste(x, q):
            return x + jax.lax.stop_gradient(q - x)

        def quant_act_uint8(x):
            s = jax.lax.stop_gradient(jnp.maximum(jnp.max(x), EPS)) / 255.0
            q = jnp.clip(jnp.round(x / s), 0.0, 255.0) * s
            return (_ste(x, q), s)

        def quant_weight_int8_perchannel(w):
            s = jax.lax.stop_gradient(jnp.maximum(jnp.max(jnp.abs(w), axis=1, keepdims=True), EPS)) / 127.0
            q = jnp.clip(jnp.round(w / s), -128.0, 127.0) * s
            return (_ste(w, q), s[:, 0])

        def quant_bias_int32(b, s_in, s_w):
            s = jax.lax.stop_gradient(s_in * s_w)
            q = jnp.round(b / s) * s
            return _ste(b, q)

        def quant_linear(x, w, b):
            xq, s_in = quant_act_uint8(x)
            wq, s_w = quant_weight_int8_perchannel(w)
            bq = quant_bias_int32(b, s_in, s_w)
            return jnp.einsum('btd,fd->btf', xq, wq) + bq
        h = jax.nn.relu(quant_linear(x, w1, b1))
        return quant_linear(h, w2, b2)
    x = x + _L0_xattn_ref(_layernorm(x, axis=-1), ctx_1024, L0_xattn_Wq, L0_xattn_Wkv, L0_xattn_Wc)
    x = x + _L0_ffn_ref(_layernorm(x, axis=-1), L0_ffn_scale, L0_ffn_gate_w, L0_ffn_gate_b, L0_ffn_mlp1_w, L0_ffn_mlp1_b, L0_ffn_mlp2_w, L0_ffn_mlp2_b)
    x = x + _L1_xattn_ref(_layernorm(x, axis=-1), ctx_1024, itok_BxS_0_255, L1_xattn_Wqkv, L1_xattn_bqkv, L1_xattn_Wo, L1_xattn_bo, L1_xattn_Wq_c, L1_xattn_Wkv_c, L1_xattn_Wo_c, L1_xattn_Wg, L1_xattn_Wu, L1_xattn_Wd, L1_xattn_n1, L1_xattn_n2, L1_xattn_n3, L1_xattn_nf)
    x = x + _L1_ffn_ref(_layernorm(x, axis=-1), L1_ffn_w1, L1_ffn_b1, L1_ffn_w2, L1_ffn_b2)
    return x

_drawn_inputs = setup_inputs


def setup_inputs(seed=0):
    import zlib

    import numpy as np

    out = dict(_drawn_inputs(seed))
    spreads = {'L0_ffn_scale': (1.0, 0.6),
     'L0_ffn_gate_b': (0.0, 0.1),
     'L1_xattn_bqkv': (0.0, 0.51),
     'L1_xattn_bo': (0.0, 0.1),
     'L1_xattn_n1': (1.0, 0.6),
     'L1_xattn_n2': (1.0, 0.6),
     'L1_xattn_n3': (1.0, 0.6),
     'L1_xattn_nf': (1.0, 0.2)}
    factors = {'L0_xattn_Wq': 5.299,
     'L0_ffn_mlp1_b': 8.0,
     'L0_ffn_mlp2_b': 8.0,
     'L1_xattn_Wqkv': 4.765,
     'L1_xattn_Wo': 2.862,
     'L1_xattn_Wq_c': 8.0,
     'L1_xattn_Wkv_c': 2.814,
     'L1_xattn_Wo_c': 2.868,
     'L1_xattn_Wg': 6.379,
     'L1_xattn_Wu': 6.341,
     'L1_xattn_Wd': 6.303,
     'L1_ffn_b1': 8.0,
     'L1_ffn_b2': 8.0}
    for name, (base, spread) in spreads.items():
        noise = np.random.default_rng([zlib.crc32(name.encode()), seed]).standard_normal(out[name].shape)
        drawn = base * np.exp(spread * noise) if base else spread * noise
        out[name] = jnp.asarray(drawn.astype(out[name].dtype))
    for name, factor in factors.items():
        out[name] = (out[name] * factor).astype(out[name].dtype)
    return out
```

```python
from contextlib import ExitStack

import numpy as np

import concourse.bass as bass
from concourse import mybir

F32 = mybir.dt.float32
BF16 = mybir.dt.bfloat16
I32 = mybir.dt.int32
U32 = mybir.dt.uint32
ALU = mybir.AluOpType
ACT = mybir.ActivationFunctionType
AX = mybir.AxisListType

D = 128
B = 8
L = 56
T = B * L
H = 16
DH = D // H
GR = 4
HG = H // GR
S = 1500
NL = 4
E = 16
TOPK = 4
FF = 512
FC = FF // D
HV = 2 * DH
CO = HV + 1
NEAR = 32
LOOKBACK = 128
KC = 125
NK = S // KC
SB = 500
UNITS = 4
PB = 2 * L
SCALE = float(1.0 / np.sqrt(np.float32(DH)))
WARM_SQ = 6
WARM_NORM = 9
NEG = -1e30
MAGIC = 12582912.0
LIMIT = 7.0
ALPHA = 1.702

WQ, WQR, WK, WKR, WV, WO, WQC, WKC, WVC, WOC = (i * D for i in range(10))
WATT = 10 * D
WG, WU, WD = 0, FF, 2 * FF
WFFN = 3 * FF
BQ, BQR, BK, BKR, BV, BO, N1, N2, N3 = range(9)
NP_ = 9
NDVE = 16
V_SCALE, V_NF, V_B2 = 0, 1, 2
V_B1 = 3
V_SEL = V_B1 + FC
V_ROW = V_SEL + HG
V_BASE = V_ROW + 2
V_B1G = V_BASE + UNITS
V_B1L = V_B1G + E
V_HEAD = V_B1L + E
NV = V_HEAD + H


class Chain:

    def __init__(self, eng, sem, start=0):
        self.eng, self.sem, self.start, self.n = eng, sem, start, 0

    def __call__(self, ins):
        self.n += 1
        ins.then_inc(self.sem, 1)
        self.eng.wait_ge(self.sem, self.start + self.n)

    def mark(self, ins):
        self.n += 1
        ins.then_inc(self.sem, 1)
        return self.start + self.n


def build(nc, a, out):
    ctx = ExitStack()
    with ctx:
        def sb(name, shape, dt=F32):
            return ctx.enter_context(nc.sbuf_tensor(name, shape, dt))

        def sem(name):
            return ctx.enter_context(nc.semaphore(name))

        ctxT = sb("ctxT", [D, B * S])
        arena = [0]

        def carve(*shape):
            n = int(np.prod(shape))
            assert arena[0] + n <= B * S
            flat = ctxT[:, arena[0]:arena[0] + n]
            arena[0] += n
            if len(shape) == 1:
                return flat
            names = "abcde"[:len(shape)]
            return flat.rearrange("p (" + " ".join(names) + ") -> p " + " ".join(names),
                                  **{c: m for c, m in zip(names[1:], shape[1:])})

        xin = sb("xin", [D, T])
        xc = sb("xc", [D, T])
        sq = sb("sq", [D, T])
        rs = sb("rs", [D, T])
        xh = sb("xh", [D, T])
        h = sb("h", [D, T])
        x1 = sb("x1", [D, T])
        x2 = sb("x2", [D, T])
        xl = sb("xl", [D, T])
        wa0 = sb("wa0", [D, 4 * D])
        wA = sb("wA", [D, WATT])
        wF = sb("wF", [D, WFFN])
        par = sb("par", [D, NL, NP_])
        pl = sb("pl", [D, NP_])
        vec = sb("vec", [D, NV])
        cs = sb("cs", [D, 2, T])
        seg = sb("seg", [PB, B], I32)
        segrow = sb("segrow", [1, T], I32)
        segrf = sb("segrf", [1, T])
        lim = sb("lim", [1, 4])
        near_i = sb("near_i", [1, 1], I32)
        fmx = sb("fmx", [L, 3])
        segf = sb("segf", [PB, 2, B])
        ident = sb("ident", [D, D])
        identb = sb("identb", [D, D], BF16)
        warm = sb("warm", [D, 8 * L], BF16)
        onesD = sb("onesD", [D, D])
        ones1 = sb("ones1", [1, D])
        eps = sb("eps", [D, 2])
        causal = sb("causal", [PB, 8, L], BF16)
        frow = sb("frow", [L, SB])
        cz = sb("cz", [PB, 4, L])
        krow = sb("krow", [PB, NEAR], I32)
        krowf = sb("krowf", [PB, NEAR])
        xm = sb("xm", [PB, 2, NEAR])
        qpT = sb("qpT", [D, T + 8])
        mx8 = sb("mx8", [D, 8])
        idx8 = sb("idx8", [D, 8], U32)
        rows = sb("rows", [D, UNITS], U32)
        mem = sb("mem", [D, UNITS, D])
        tq = sb("tq", [D, 2, T])
        memD = tq[:, :, :].rearrange("p a t -> p (a t)").rearrange("p (b k l) -> p b k l", b=B, k=2)
        Q4 = sb("Q4", [D, B, HG, L])
        Kz = sb("Kz", [D, B, GR, L])
        VB = sb("VB", [PB, B, 2, 2, 2, HV + 1])
        O = sb("O", [PB, 2, 2, D])
        rcp = sb("rcp", [PB, 2, 16])
        wgt = sb("wgt", [PB, 2, 16, 2])
        fold = sb("fold", [PB, L])
        P = sb("P", [PB, 2, 2, 8, L])
        PT = sb("PT", [PB, 2, 2, 4, PB])
        mxs = sb("mxs", [PB, 2, 16])
        o = sb("o", [D, T])
        Kc = sb("Kc", [D, B, GR, NEAR])
        Vc = sb("Vc", [D, B, 2, GR, HV + 1])
        near = sb("near", [D, B, NEAR])
        bo2 = sb("bo2", [D, 1])
        gw = sb("gw", [D, E])
        gb = sb("gb", [PB, E])
        gl = sb("gl", [PB, UNITS, E])
        gm8 = sb("gm8", [PB, UNITS, 8])
        gi8 = sb("gi8", [PB, UNITS, 8], U32)
        gif = sb("gif", [PB, UNITS, TOPK])
        eio = sb("eio", [PB, E], I32)
        eiof = sb("eiof", [PB, E])
        eq = sb("eq", [PB, UNITS, E, TOPK])
        ge = sb("ge", [PB, UNITS, E])
        gsum = sb("gsum", [PB, UNITS])
        b2e = sb("b2e", [E, D])
        RING = 4
        ew = sb("ew", [D, RING, 3 * D])
        wn = sb("wn", [D, 2, FF])
        w1n = wn[:, 0, :].rearrange("p (c d) -> p c d", c=FC)
        w2n = wn[:, 1, :]
        wt = wn
        wqb = sb("wqb", [D, 2, FF], BF16)
        w1qT = sb("w1qT", [D, FF], BF16)
        w2qT = sb("w2qT", [D, FC, D], BF16)
        sw = sb("sw", [D, 8])
        swi = sb("swi", [D, 8])
        ss = sb("ss", [D, 8])
        bq = sb("bq", [D, 8])
        s11 = sb("s11", [D, 12])
        yt = sb("yt", [D, T])
        yq = sb("yq", [D, T], BF16)
        def bf16(ap):
            return ap.bitcast(BF16)

        sel = bf16(carve(E * D // 2)[0:96]).rearrange("p (e d) -> p e d", e=E)
        rpart = carve(2, T)[0:E]
        routeT = carve(T)[0:E]
        rmid = bf16(carve(T // 2)[0:E])
        rb = bf16(carve(T // 2)[0:96])
        xg, sg, l1, l2, vv, ww, zz = (carve(2, T) for _ in range(7))
        arena[0] = 0
        Q4c = carve(B, HG, L)
        Pc = carve(UNITS, 16, NEAR)[0:PB]
        PTc = carve(UNITS, 4, PB)
        sl = carve(FC, T)
        mm = sl
        hd = carve(B, 2, L)
        near4 = carve(B, GR, NEAR)
        tk = carve(2, T)
        qk = carve(2, T)
        xbias = bf16(carve(B * GR * NEAR // 2)[0:PB]).rearrange("p (b k) -> p b k", b=B)
        x3 = x1
        arena[0] = 0
        gx = carve(S)
        gk = carve(S)
        gv = carve(S)
        gV = carve(NK, D)[0:KC]
        gp = carve(S)[0:L]
        gPT = carve(NK, L)[0:KC]
        assert arena[0] <= 8320
        gb_ = P[:, :, :, :, :].rearrange("p a b c l -> p (a b c l)")[0:L, 0:S]
        gi = PT[:, :, :, :, :].rearrange("p a b c l -> p (a b c l)")[0:L, 0:S]
        gq, gqz = tk[:, 0, 0:L], tk[:, 0, 64:64 + L]
        gO, gOc = qk[0:L, 0, 0:D], qk[0:L, 1, 0:D]
        arena[0] = 0
        sq2 = carve(T)
        hh = carve(FC, T)
        ht = carve(FC, T)
        hq = carve(FC * T // 2).bitcast(BF16).rearrange("p (c t) -> p c t", c=FC)

        PS = ctx.enter_context(nc.psum_tensor("PS", [D, 8, 512], F32))

        names = """warm_ready d_x d_vec d_wa0 d_ctx0 d_ctx1 d_ctx2 d_ctx3 d_gw d_seg d_cs d_par d_wA d_wF d_wq d_b2e
        ln_done on_ready ot_done oc_part con_ready cot_done hd_ready near_ready d_segrow near_known far_step d_gx far_kv gk_ready gv_ready far_vt gV_ready gq_ready fs_ready fm_ready fe_ready ft_ready fpt_ready fo_ready fO_ready ff_ready dve_fb dve_fh dve_c ww_ready x_ready xbias_ready bo_ready d_near d_ew0 d_ew1 d_ew2 d_ew3 d_out g0 g1 g2 g3
        consts pool_own dve_a dve_b dve_l dve_d act_a act_b act_l act_d pool_b
        mean_ready xc_ready sq_ready ms_ready rstd_ready norm_ready
        qp_done qp_copied cand_scores rows_ready mem_turned memT_ready kv_done
        proj_done q4_ready k_ready kz_ready vb_ready s_ready sub_done exp_done turned pt_ready pv_done o_ready
        wo_done res_ready ckv_done ckv_ready cv_half qc_done q4c_ready cs_ready csub_done cexp_done cturned cpt_ready cpv_done oc_ready
        woc_done resc_ready g_done u_done silu_done m_ready d_done layer_done pl_ready
        gate_done route_ready gexp_in gexp_done route_turned rb_ready
        e_glr xg_ready sg_ready l1_ready l2_ready vv_ready zz_ready y_done b_done
        wq_ready wq_turned wqT_ready max_in max_turned s_one s_bcast yq_ready up_done relu_done hq_ready down_done out_scaled out_ready""".split()
        s = {n: sem(n) for n in names}

        ctx.enter_context(nc.allow_non_contiguous_dma(reason="small vectors"))
        block = ctx.enter_context(nc.Block())

        def colv(c, n=1, p=D):
            return vec[0:p, c:c + n]

        def heads3(ap):
            return ap.rearrange("p (b l) -> p b l", b=B)

        @block.sync
        def _(sp):
            sp.dma_start(xin[:, :], a["xT"]).then_inc(s["d_x"], 16)
            sp.dma_start(vec[:, :], a["vec"]).then_inc(s["d_vec"], 16)
            sp.dma_start(wa0[:, :], a["wa0"]).then_inc(s["d_wa0"], 16)
            for u in range(UNITS):
                sp.dma_start(ctxT[:, u * 2 * S:(u + 1) * 2 * S],
                             a["ctxT"][:, u * 2 * S:(u + 1) * 2 * S]).then_inc(s[f"d_ctx{u}"], 16)
            sp.dma_start(gw[:, :], a["gw"]).then_inc(s["d_gw"], 16)
            sp.dma_start(gb[:, :], a["gb"]).then_inc(s["d_gw"], 16)
            sp.dma_start(b2e[:, :], a["b2e"]).then_inc(s["d_b2e"], 16)
            for e in range(RING):
                sp.dma_start(ew[:, e, :], a["ew"][:, e * 3 * D:(e + 1) * 3 * D]).then_inc(s[f"d_ew{e}"], 16)
            sp.dma_start(seg[:, :], a["seg"]).then_inc(s["d_seg"], 16)
            sp.dma_start(segrow[:, :], a["segrow"]).then_inc(s["d_segrow"], 16)
            sp.dma_start(near[:, :, :], a["ctxT"].rearrange("p (b s) -> p b s", b=B)[:, :, 0:NEAR]).then_inc(s["d_near"], 16)
            sp.dma_start(w1n[:, :, :], a["w1n"]).then_inc(s["d_wq"], 16)
            sp.dma_start(w2n[:, :], a["w2n"]).then_inc(s["d_wq"], 16)
            sp.dma_start(cs[:, :, :], a["cs"]).then_inc(s["d_cs"], 16)
            sp.dma_start(par[:, :, :], a["par"]).then_inc(s["d_par"], 16)
            sp.dma_start(wA[:, :], a["wA"][:, 0:WATT]).then_inc(s["d_wA"], 16)
            sp.dma_start(wF[:, :], a["wF"][:, 0:WFFN]).then_inc(s["d_wF"], 16)
            with sp.Fori(0, E // RING - 1) as i:
                for k in range(RING):
                    sp.wait_ge(s["y_done"], i * RING + (k + 1))
                    sp.dma_start(ew[:, k, :], a["ew"][:, bass.ds((i + 1) * (RING * 3 * D) + k * 3 * D, 3 * D)])\
                        .then_inc(s[f"d_ew{k}"], 16)
            sp.wait_ge(s["near_known"], 1)
            short = sp.value_load(near_i[0:1, 0:1], min_val=0, max_val=1)

            def contexts(l):
                with sp.If(short == 0):
                    with sp.Fori(0, B) as b:
                        sp.wait_ge(s["far_step"], l * (B + 1) + b + 1)
                        sp.dma_start(gx, a["ctxT"][:, bass.ds(b * S, S)]).then_inc(s["d_gx"], 16)

            with sp.Fori(0, NL - 1) as l:
                contexts(l)
                sp.wait_ge(s["woc_done"], l + 1)
                sp.dma_start(wA[:, :], a["wA"][:, bass.ds((l + 1) * WATT, WATT)]).then_inc(s["d_wA"], 16)
                sp.wait_ge(s["d_done"], l + 1)
                sp.dma_start(wF[:, :], a["wF"][:, bass.ds((l + 1) * WFFN, WFFN)]).then_inc(s["d_wF"], 16)
            contexts(NL - 1)
            sp.wait_ge(s["out_ready"], 1)
            sp.dma_start(out, yt[:, :]).then_inc(s["d_out"], 16)
            sp.wait_ge(s["d_out"], 16)


        @block.gpsimd
        def _(pool):
            own = Chain(pool, s["pool_own"])
            pool.memset(onesD[:, :], 1.0 / D).then_inc(s["consts"], 1)
            pool.memset(eps[:, 0:1], 1e-5).then_inc(s["consts"], 1)
            pool.memset(eps[:, 1:2], 1e-6).then_inc(s["consts"], 1)
            pool.memset(ones1[:, :], 1.0).then_inc(s["consts"], 1)
            pool.memset(warm[:, :], 1.0).then_inc(s["warm_ready"], 1)
            own(pool.memset(ident[:, :], 0.0))
            pool.affine_select(out=ident[:, :], in_=ident[:, :], compare_op=ALU.not_equal, fill=1.0,
                               base=0, pattern=[[-1, D]], channel_multiplier=1).then_inc(s["consts"], 1)
            pool.wait_ge(s["consts"], 5)
            pool.tensor_copy(identb[:, :], ident[:, :]).then_inc(s["consts"], 1)
            pool.memset(qpT[:, T:T + 8], 0.0).then_inc(s["consts"], 1)
            pool.memset(Kz[:, :, :, :], 0.0).then_inc(s["consts"], 1)
            own(pool.memset(VB[:, :, :, :, :, :], 0.0))
            pool.wait_ge(s["d_vec"], 16)
            for gg in range(2):
                pool.tensor_copy(VB[:, :, :, :, gg, HV:CO].rearrange("p b g j c -> p (b g j) c"),
                                 vec[0:PB, V_ROW + gg:V_ROW + gg + 1].unsqueeze(1).broadcast_to([PB, 4 * B, 1]))\
                    .then_inc(s["consts"], 1)
            own(pool.memset(fold[:, :], 0.0))
            for k in range(2):
                pool.affine_select(out=fold[:, :], in_=fold[:, :], compare_op=ALU.not_equal, fill=1.0, base=-k * L,
                                   pattern=[[-1, L]], channel_multiplier=1).then_inc(s["consts"], 1)
                pool.wait_ge(s["consts"], 11 + k)
            for u in range(UNITS):
                pool.wait_ge(s["rows_ready"], u + 1)
                pool.indirect_dma_start(out=mem[:, u, :], out_offset=None, in_=a["ctx"],
                                        in_offset=bass.IndirectOffsetOnAxis(ap=rows[:, u:u + 1], axis=0))\
                    .then_inc(s[f"g{u}"], 16)
            for u in range(UNITS):
                pool.wait_ge(s[f"g{u}"], 16)
            own(pool.memset(sel[:, :, :], 0.0))
            own(pool.memset(rb[:, :], 0.0))
            for k in range(3):
                own(pool.affine_select(out=sel[32 * k:32 * k + E, :, :], in_=sel[32 * k:32 * k + E, :, :],
                                       compare_op=ALU.not_equal, fill=1.0, base=0,
                                       pattern=[[-1, E], [0, D]], channel_multiplier=1))
            own(pool.iota(eio[:, :], pattern=[[1, E]], base=0, channel_multiplier=0))
            pool.tensor_copy(eiof[:, :], eio[:, :]).then_inc(s["consts"], 1)
            own(pool.memset(causal[:, :, :], 0.0))
            own(pool.memset(Kc[:, :, :, :], 0.0))
            own(pool.memset(Vc[:, :, :, :, :], 0.0))
            for g in range(GR):
                own(pool.memset(Vc[32 * g:32 * g + 32, :, :, g, HV:CO], 1.0))
            own(pool.iota(frow[:, :], pattern=[[1, SB]], base=0, channel_multiplier=0,
                          allow_small_or_imprecise_dtypes=True))
            own(pool.iota(krow[:, :], pattern=[[1, NEAR]], base=0, channel_multiplier=0))
            pool.tensor_copy(krowf[:, :], krow[:, :]).then_inc(s["consts"], 1)
            own(pool.memset(cz[:, :, :], 0.0))
            own(pool.affine_select(out=cz[:, 0, :], in_=cz[:, 0, :], compare_op=ALU.is_ge, fill=NEG,
                                   base=0, pattern=[[-1, L]], channel_multiplier=1))
            own(pool.affine_select(out=cz[:, 1, :], in_=cz[:, 1, :], compare_op=ALU.is_ge, fill=NEG,
                                   base=-L, pattern=[[-1, L]], channel_multiplier=1))
            own(pool.tensor_scalar(cz[:, 2, :], cz[:, 1, :], vec[0:PB, V_ROW + 1:V_ROW + 2], None, ALU.mult))
            own(pool.tensor_tensor(cz[:, 3, :], cz[:, 0, :], cz[:, 2, :], ALU.add))
            pool.tensor_copy(causal[:, :, :], cz[:, 3, :].unsqueeze(1).broadcast_to([PB, 8, L]))\
                .then_inc(s["consts"], 1)

            pool.wait_ge(s["d_near"], 16)
            pool.wait_ge(s["x_ready"], 2)
            pool.tensor_copy(near4[:, :, :, :], near[:, :, :].unsqueeze(2).broadcast_to([D, B, GR, NEAR]))\
                .then_inc(s["near_ready"], 1)

        @block.tensor
        def _(pe):
            def mm1(dst, w, x, start=True, stop=True):
                return nc.tensor.matmul(dst, w, x, start=start, stop=stop)

            def stay_warm(n):
                for _ in range(n):
                    mm1(PS[:, 5, 0:8 * L], identb[:, :], warm[:, :])

            def mean(i, src):
                mm1(PS[:, 6, 0:T], onesD[:, :], src).then_inc(s["mean_ready"], 1)

            def mean_square(i):
                stay_warm(WARM_SQ)
                pe.wait_ge(s["sq_ready"], i + 1)
                mm1(PS[:, 7, 0:T], onesD[:, :], sq[:, :]).then_inc(s["ms_ready"], 1)
                stay_warm(WARM_NORM)

            def attention(r, masked):
                def scores(u):
                    if u == 0:
                        pe.wait_ge(s["q4_ready"], r + 1)
                        pe.wait_ge(s["kz_ready"], r + 1)
                    if u >= 2:
                        pe.wait_ge(s["sub_done"], r * UNITS + (u - 1))
                    for k in range(2):
                        b, bank = 2 * u + k, 2 * (u % 2) + k
                        if masked:
                            mm1(PS[0:PB, bank, 0:8 * L], identb[0:PB, 0:PB],
                                causal[:, :, :].rearrange("p c l -> p (c l)"), stop=False)
                        for jp in range(2):
                            last = mm1(PS[0:PB, bank, jp * GR * L:(jp + 1) * GR * L],
                                       Q4[:, b, 2 * jp:2 * jp + 2, :].rearrange("p j l -> p (j l)"),
                                       Kz[:, b, :, :].rearrange("p g l -> p (g l)"),
                                       start=not masked, stop=not masked or jp == 1)
                    last.then_inc(s["s_ready"], 1)

                def turn(u):
                    pe.wait_ge(s["exp_done"], r * UNITS + (u + 1))
                    if u >= 1:
                        pe.wait_ge(s["pt_ready"], r * UNITS + u)
                    for k in range(2):
                        for jp in range(2):
                            for G in range(2):
                                src = P[:, u % 2, k, jp * GR + 2 * G:jp * GR + 2 * G + 2, :]
                                last = nc.tensor.transpose(PS[0:PB, 4 + k, (jp * 2 + G) * PB:(jp * 2 + G + 1) * PB],
                                                           src.rearrange("p g l -> p (g l)"), ident[0:PB, 0:PB])
                    last.then_inc(s["turned"], 1)

                def values(u):
                    pe.wait_ge(s["pt_ready"], r * UNITS + (u + 1))
                    if u == 0:
                        pe.wait_ge(s["vb_ready"], r + 1)
                    if u >= 2:
                        pe.wait_ge(s["o_ready"], r * UNITS + (u - 1))
                    for k in range(2):
                        for G in range(2):
                            for jp in range(2):
                                at = (k * 2 * GR + G * GR + jp) * CO
                                last = mm1(PS[0:PB, 6 + u % 2, at:at + 4 * CO]
                                           .rearrange("p (g j c) -> p g j c", g=2, j=2)[:, :, 0, :],
                                           PT[:, u % 2, k, jp * 2 + G, :], VB[:, 2 * u + k, G, jp, :, :])
                    last.then_inc(s["pv_done"], 1)

                def turn_back(u):
                    pe.wait_ge(s["on_ready"], r * UNITS + (u + 1))
                    for k in range(2):
                        last = mm1(PS[:, 6 + u % 2, 300 + k * L:300 + (k + 1) * L], O[:, u % 2, k, :], fold[:, :])
                    last.then_inc(s["ot_done"], 1)

                scores(0)
                scores(1)
                scores(2)
                turn(0)
                values(0)
                scores(3)
                turn(1)
                values(1)
                turn_back(0)
                turn(2)
                values(2)
                turn_back(1)
                turn(3)
                values(3)
                turn_back(2)
                turn_back(3)

            pe.wait_ge(s["consts"], 6)
            pe.wait_ge(s["warm_ready"], 1)
            pe.wait_ge(s["d_x"], 16)
            mean(0, xin[:, :])
            mean_square(0)
            pe.wait_ge(s["norm_ready"], 1)
            pe.wait_ge(s["d_wa0"], 16)
            mm1(PS[:, 2, 0:T], wa0[:, 0:D], xh[:, :]).then_inc(s["qp_done"], 1)
            for u in range(UNITS):
                if u == 0:
                    pe.wait_ge(s["consts"], 7)
                    pe.wait_ge(s["qp_copied"], 1)
                pe.wait_ge(s[f"d_ctx{u}"], 16)
                if u >= 2:
                    pe.wait_ge(s["rows_ready"], u - 1)
                for c in range(3):
                    n = min(512, S - c * 512)
                    for k in range(2):
                        b = 2 * u + k
                        last = mm1(PS[64 * k:64 * k + 64, 3 * (u % 2) + c, 0:n], qpT[:, b * L:b * L + 64],
                                   ctxT[:, b * S + c * 512:b * S + c * 512 + n])
                last.then_inc(s["cand_scores"], 1)
            for u in range(UNITS):
                pe.wait_ge(s[f"g{u}"], 16)
                last = nc.tensor.transpose(PS[:, 6, u * D:(u + 1) * D], mem[:, u, :], ident[:, :])
            last.then_inc(s["mem_turned"], 1)
            pe.wait_ge(s["memT_ready"], 1)
            mm1(PS[:, 7, 0:T], wa0[:, D:2 * D], memD[:, :, 0, :]).then_inc(s["kv_done"], 1)
            pe.wait_ge(s["rows_ready"], UNITS)
            for b in range(B):
                last = mm1(PS[0:PB, 4 + b // 4, (b % 4) * D:(b % 4 + 1) * D], memD[:, b, :, :].rearrange("p k l -> p (k l)"),
                           wa0[:, 2 * D:3 * D])
            last.then_inc(s["kv_done"], 1)
            attention(0, False)
            pe.wait_ge(s["o_ready"], UNITS)
            mm1(PS[:, 0, 0:T], wa0[:, 3 * D:4 * D], o[:, :]).then_inc(s["wo_done"], 1)

            pe.wait_ge(s["x_ready"], 1)
            mean(1, x1[:, :])
            mean_square(1)
            mean_square(2)
            pe.wait_ge(s["norm_ready"], 3)
            pe.wait_ge(s["d_gw"], 32)
            for u in range(UNITS):
                last = mm1(PS[0:PB, 0, u * E:(u + 1) * E], h[:, u * PB:(u + 1) * PB], gw[:, :])
            last.then_inc(s["gate_done"], 1)
            pe.wait_ge(s["route_ready"], 1)
            for u in range(UNITS):
                last = nc.tensor.transpose(PS[0:E, 1, u * PB:(u + 1) * PB], ge[:, u, :], ident[0:PB, 0:PB])
            last.then_inc(s["route_turned"], 1)
            pe.wait_ge(s["rb_ready"], 1)
            pe.wait_ge(s["d_b2e"], 16)
            mm1(PS[:, 6, 0:T], b2e[:, :], routeT[:, :], stop=False)

            def expert_up(e, k, i, first):
                bank = 3 * (k % 2)
                pe.wait_ge(s[f"d_ew{k % RING}"], (i + 1) * 16)
                if not first or k >= 2:
                    pe.wait_ge(s["ww_ready"], e - 1)
                mm1(PS[:, bank, 0:T], ew[:, k % RING, 0:D], h[:, :])
                mm1(PS[:, bank + 1, 0:T], ew[:, k % RING, D:2 * D], h[:, :])
                mm1(PS[:, bank + 2, 0:T], sel[:, bass.ds(e, 1), :].rearrange("p e d -> p (e d)"), rb[:, :])\
                    .then_inc(s["e_glr"], 1)

            def expert_down(e, k, stop=False):
                pe.wait_ge(s["zz_ready"], e + 1)
                mm1(PS[:, 6, 0:T], ew[:, k, 2 * D:3 * D], zz[:, k % 2, :], start=False, stop=stop)\
                    .then_inc(s["y_done"], 1)

            expert_up(0, 0, 0, True)
            for k in range(RING):
                if k + 1 < RING:
                    expert_up(k + 1, k + 1, 0, True)
                else:
                    expert_up(RING, 0, 1, False)
                expert_down(k, k)
            with pe.Fori(1, E // RING - 1) as i:
                for k in range(RING):
                    if k + 1 < RING:
                        expert_up(i * RING + (k + 1), k + 1, i, False)
                    else:
                        expert_up(i * RING + RING, 0, i + 1, False)
                    expert_down(i * RING + k, k)
            for k in range(RING):
                e = E - RING + k
                if k + 1 < RING:
                    expert_up(e + 1, k + 1, E // RING - 1, False)
                expert_down(e, k, stop=e == E - 1)

            pe.wait_ge(s["x_ready"], 2)
            mean(2, x2[:, :])
            mean_square(3)
            pe.wait_ge(s["consts"], 15)
            pe.wait_ge(s["near_ready"], 1)
            pe.wait_ge(s["xbias_ready"], 1)
            pe.wait_ge(s["near_known"], 1)
            short = pe.value_load(near_i[0:1, 0:1], min_val=0, max_val=1)

            def cross_long(l):
                with pe.Fori(0, B) as b:
                    pe.wait_ge(s["far_step"], l * (B + 1) + b + 1)
                    lb = l * B + b
                    pe.wait_ge(s["d_gx"], (lb + 1) * 16)
                    for c in range(3):
                        mm1(PS[:, c, 0:SB], wA[:, WKC:WKC + D], gx[:, c * SB:(c + 1) * SB])
                        last = mm1(PS[:, 3 + c, 0:SB], wA[:, WVC:WVC + D], gx[:, c * SB:(c + 1) * SB])
                    last.then_inc(s["far_kv"], 1)
                    pe.wait_ge(s["gv_ready"], lb + 1)
                    for c in range(NK):
                        last = nc.tensor.transpose(PS[0:KC, 3 + c // 4, (c % 4) * D:(c % 4 + 1) * D],
                                                   gv[:, c * KC:(c + 1) * KC], ident[:, :])
                    last.then_inc(s["far_vt"], 1)
                    with pe.Fori(0, H) as hh_:
                        t = lb * H + hh_
                        pe.wait_ge(s["gq_ready"], t + 1)
                        for c in range(3):
                            last = mm1(PS[0:L, c, 0:SB], gqz, gk[:, c * SB:(c + 1) * SB])
                        last.then_inc(s["fs_ready"], 1)
                        pe.wait_ge(s["fe_ready"], t + 1)
                        for c in range(NK):
                            last = mm1(PS[0:KC, 6 + c // 8, (c % 8) * 64:(c % 8) * 64 + L],
                                       gp[:, c * KC:(c + 1) * KC], ident[0:L, 0:L])
                        last.then_inc(s["ft_ready"], 1)
                        pe.wait_ge(s["gV_ready"], lb + 1)
                        pe.wait_ge(s["fpt_ready"], t + 1)
                        for c in range(NK):
                            last = mm1(PS[0:L, 3, 0:DH], gPT[:, c, :], gV[:, c, bass.ds(hh_ * DH, DH)],
                                       start=c == 0, stop=c == NK - 1)
                        last.then_inc(s["fo_ready"], 1)
                    pe.wait_ge(s["fO_ready"], lb + 1)
                    mm1(PS[:, 4, 0:L], gOc, ident[0:L, 0:L]).then_inc(s["ff_ready"], 1)

            def cross_near(l):
                pe.wait_ge(s["q4c_ready"], l + 1)
                for u in range(UNITS):
                    mm1(PS[0:PB, u, :], identb[0:PB, 0:PB],
                        xbias[:, 2 * u:2 * u + 2, :].unsqueeze(2).broadcast_to([PB, 2, 2, GR * NEAR]), stop=False)
                    for k in range(2):
                        for jp in range(2):
                            b, col = 2 * u + k, (2 * k + jp) * GR * NEAR
                            last = mm1(PS[0:PB, u, col:col + GR * NEAR],
                                       Q4c[:, b, 2 * jp:2 * jp + 2, :].rearrange("p j l -> p (j l)"),
                                       Kc[:, b, :, :].rearrange("p g k -> p (g k)"),
                                       start=False, stop=k + jp == 2)
                    last.then_inc(s["cs_ready"], 1)

                def turn_near(u):
                    pe.wait_ge(s["cexp_done"], l * UNITS + (u + 1))
                    if u >= 2:
                        pe.wait_ge(s["cpt_ready"], l * UNITS + (u - 1))
                    for c in range(4):
                        last = nc.tensor.transpose(PS[:, 4 + u % 2, c * PB:(c + 1) * PB],
                                                   Pc[:, u, GR * c:GR * c + GR, :].rearrange("p g k -> p (g k)"),
                                                   ident[0:PB, 0:PB])
                    last.then_inc(s["cturned"], 1)

                def values_near(u):
                    pe.wait_ge(s["cpt_ready"], l * UNITS + (u + 1))
                    if u >= 2:
                        pe.wait_ge(s["oc_part"], l * UNITS + (u - 1))
                    for k in range(2):
                        for jp in range(2):
                            at = (k * 2 * GR + jp) * CO
                            last = mm1(PS[0:PB, 6 + u % 2, at - jp * CO:at - jp * CO + 8 * CO]
                                       .rearrange("p (g j c) -> p g j c", g=GR, j=2)[:, :, jp, :],
                                       PTc[:, u, 2 * k + jp, :], Vc[:, 2 * u + k, jp, :, :])
                    last.then_inc(s["cpv_done"], 1)

                def turn_back_near(u):
                    pe.wait_ge(s["con_ready"], l * UNITS + (u + 1))
                    for k in range(2):
                        last = mm1(PS[:, 6 + u % 2, 300 + k * L:300 + (k + 1) * L], O[:, u % 2, k, :], fold[:, :])
                    last.then_inc(s["cot_done"], 1)

                turn_near(0)
                turn_near(1)
                values_near(0)
                turn_near(2)
                values_near(1)
                turn_back_near(0)
                turn_near(3)
                values_near(2)
                turn_back_near(1)
                values_near(3)
                turn_back_near(2)
                turn_back_near(3)

            with pe.Fori(0, NL) as l:
                mean_square(l * 3 + 4)
                pe.wait_ge(s["norm_ready"], l * 3 + 5)
                pe.wait_ge(s["d_wA"], (l + 1) * 16)
                for i, w in enumerate((WQ, WQR, WK, WKR)):
                    mm1(PS[:, i, 0:T], wA[:, w:w + D], h[:, :]).then_inc(s["proj_done"], 1)
                pe.wait_ge(s["hd_ready"], l + 1)
                for b in range(B):
                    last = mm1(PS[0:PB, 4 + b // 4, (b % 4) * D:(b % 4 + 1) * D],
                               hd[:, b, :, :].rearrange("p k l -> p (k l)"), wA[:, WV:WV + D])
                last.then_inc(s["proj_done"], 1)
                mm1(PS[:, 6, 0:1], wA[:, WO:WO + D], pl[:, BV:BV + 1])
                mm1(PS[:, 6, 128:128 + B * NEAR], wA[:, WKC:WKC + D],
                    near[:, :, :].rearrange("p b k -> p (b k)")).then_inc(s["ckv_done"], 1)
                pe.wait_ge(s["vb_ready"], l + 2)
                for b in range(B):
                    last = mm1(PS[:, 4 + b // 4, (b % 4) * D:(b % 4 + 1) * D],
                               near4[:, b, :, :].rearrange("p g k -> p (g k)"), wA[:, WVC:WVC + D])
                last.then_inc(s["ckv_done"], 1)
                pe.wait_ge(s["ckv_ready"], l + 1)
                pe.wait_ge(s["bo_ready"], l + 1)
                attention(l + 1, True)
                pe.wait_ge(s["o_ready"], (l + 1) * UNITS + UNITS)
                mm1(PS[:, 0, 0:T], wA[:, WO:WO + D], o[:, :]).then_inc(s["wo_done"], 1)
                mean_square(l * 3 + 5)
                pe.wait_ge(s["norm_ready"], l * 3 + 6)
                mm1(PS[:, 1, 0:T], wA[:, WQC:WQC + D], h[:, :]).then_inc(s["qc_done"], 1)
                with pe.If(short == 1):
                    cross_near(l)
                with pe.If(short == 0):
                    cross_long(l)
                pe.wait_ge(s["oc_ready"], l + 1)
                mm1(PS[:, 0, 0:T], wA[:, WOC:WOC + D], o[:, :]).then_inc(s["woc_done"], 1)
                mean_square(l * 3 + 6)
                pe.wait_ge(s["norm_ready"], l * 3 + 7)
                pe.wait_ge(s["d_wF"], (l + 1) * 16)

                def ffn_up(c):
                    if c >= 2:
                        pe.wait_ge(s["m_ready"], l * FC + (c - 1))
                    bank = 2 * (c % 2)
                    mm1(PS[:, bank, 0:T], wF[:, WG + c * D:WG + (c + 1) * D], h[:, :]).then_inc(s["g_done"], 1)
                    mm1(PS[:, bank + 1, 0:T], wF[:, WU + c * D:WU + (c + 1) * D], h[:, :]).then_inc(s["u_done"], 1)

                def ffn_down(c):
                    pe.wait_ge(s["m_ready"], l * FC + (c + 1))
                    return mm1(PS[:, 4, 0:T], wF[:, WD + c * D:WD + (c + 1) * D], mm[:, c, :],
                               start=c == 0, stop=c == FC - 1)

                ffn_up(0)
                ffn_up(1)
                ffn_down(0)
                ffn_up(2)
                ffn_down(1)
                ffn_up(3)
                ffn_down(2)
                ffn_down(3).then_inc(s["d_done"], 1)
            mean_square(4 + 3 * NL)

            pe.wait_ge(s["wq_ready"], 1)
            for c in range(FC):
                nc.tensor.transpose(PS[:, 0, c * 64:(c + 1) * 64].bitcast(BF16), wqb[:, 0, c * D:(c + 1) * D],
                                    identb[:, :])
            for c in range(FC):
                last = nc.tensor.transpose(PS[:, 1, c * 64:(c + 1) * 64].bitcast(BF16),
                                           wqb[:, 1, c * D:(c + 1) * D], identb[:, :])
            last.then_inc(s["wq_turned"], 1)

            pe.wait_ge(s["x_ready"], 3 + 3 * NL)
            mean(3, x3[:, :])
            mean_square(5 + 3 * NL)

            def largest(i):
                pe.wait_ge(s["max_in"], i + 1)
                nc.tensor.transpose(PS[0:1, 5, 0:D], s11[:, 0:1], ident[:, :]).then_inc(s["max_turned"], 1)
                pe.wait_ge(s["s_one"], i + 1)
                mm1(PS[:, 4, 0:1], ones1[:, :], s11[0:1, 2:3]).then_inc(s["s_bcast"], 1)

            largest(0)
            pe.wait_ge(s["yq_ready"], 1)
            pe.wait_ge(s["wqT_ready"], 1)
            for c in range(FC):
                mm1(PS[:, c, 0:T], w1qT[:, c * D:(c + 1) * D], yq[:, :]).then_inc(s["up_done"], 1)
            largest(1)
            pe.wait_ge(s["hq_ready"], 1)
            for c in range(FC):
                last = mm1(PS[:, 6, 0:T], w2qT[:, c, :], hq[:, c, :], start=c == 0, stop=c == FC - 1)
            last.then_inc(s["down_done"], 1)

        @block.scalar
        def _(act):
            def fn(dst, src, f, **kw):
                return nc.scalar.activation(dst, src, f, **kw)

            def norm(i, src, e):
                fn(sq[:, :], src, ACT.Square).then_inc(s["sq_ready"], 1)
                act.wait_ge(s["ms_ready"], i + 1)
                fn(rs[:, :], PS[:, 7, 0:T], ACT.Ln, bias=eps[:, e:e + 1]).then_inc(s["ln_done"], 1)
                act.wait_ge(s["ln_done"], i + 1)
                fn(rs[:, :], rs[:, :], ACT.Exp, scale=-0.5).then_inc(s["rstd_ready"], 1)

            def values_out(r):
                v = PS[0:PB, 4:6, :].rearrange("p k (b c) -> p (k b) c", c=D)
                for gg in range(2):
                    last = fn(VB[:, :, :, :, gg, 0:HV].rearrange("p b g j c -> p (b g) j c"),
                              v.rearrange("p b (g h c) -> p (b g) h c", g=2, h=4)[:, :, 2 * gg:2 * gg + 2, :],
                              ACT.Copy, scale=vec[0:PB, V_ROW + gg:V_ROW + gg + 1])
                last.then_inc(s["vb_ready"], 1)

            def keys_out(src):
                for g in range(GR):
                    last = fn(Kz[32 * g:32 * g + 32, :, g, :], heads3(src[32 * g:32 * g + 32]), ACT.Copy)
                last.then_inc(s["kz_ready"], 1)

            def attention(r):
                def exps(u):
                    act.wait_ge(s["sub_done"], r * UNITS + (u + 1))
                    v = P[:, u % 2, :, :, :].rearrange("p k c l -> p (k c l)")
                    fn(v, v, ACT.Exp, scale=SCALE).then_inc(s["exp_done"], 1)

                def evac(u):
                    act.wait_ge(s["turned"], r * UNITS + (u + 1))
                    if u >= 2:
                        act.wait_ge(s["pv_done"], r * UNITS + (u - 1))
                    fn(PT[:, u % 2, :, :, :].rearrange("p k c q -> p k (c q)"), PS[0:PB, 4:6, 0:4 * PB],
                       ACT.Copy).then_inc(s["pt_ready"], 1)

                def out_part(u):
                    act.wait_ge(s["ot_done"], r * UNITS + (u + 1))
                    fn(o[:, 2 * u * L:2 * (u + 1) * L], PS[:, 6 + u % 2, 300:300 + 2 * L], ACT.Copy)\
                        .then_inc(s["o_ready"], 1)

                exps(0)
                exps(1)
                evac(0)
                exps(2)
                evac(1)
                exps(3)
                out_part(0)
                evac(2)
                out_part(1)
                evac(3)
                out_part(2)
                out_part(3)

            act.preload_act_table_set("natural_log_exp_and_others")
            act.wait_ge(s["consts"], 6)
            act.wait_ge(s["xc_ready"], 1)
            norm(0, xc[:, :], 0)
            act.wait_ge(s["qp_done"], 1)
            fn(qpT[:, 0:T], PS[:, 2, 0:T], ACT.Copy).then_inc(s["qp_copied"], 1)
            act.wait_ge(s["mem_turned"], 1)
            fn(memD[:, :, :, :], PS[:, 6, :].rearrange("p (b l) -> p b l", b=B)[:, :, 0:L].unsqueeze(2)
               .broadcast_to([D, B, 2, L]), ACT.Copy).then_inc(s["memT_ready"], 1)
            act.wait_ge(s["consts"], 12)
            act.wait_ge(s["d_vec"], 16)
            act.wait_ge(s["kv_done"], 1)
            keys_out(PS[:, 7, 0:T])
            act.wait_ge(s["kv_done"], 2)
            values_out(0)
            attention(0)
            act.wait_ge(s["xc_ready"], 2)
            norm(1, xc[:, :], 0)
            act.wait_ge(s["norm_ready"], 2)
            norm(2, xh[:, :], 0)
            act.wait_ge(s["gexp_in"], 1)
            fn(ge[:, :, :], ge[:, :, :], ACT.Exp).then_inc(s["gexp_done"], 1)

            def expert(e, k, first):
                bank = 3 * (k % 2)
                act.wait_ge(s["e_glr"], e + 1)
                if not first or k >= 2:
                    act.wait_ge(s["zz_ready"], e - 1)
                fn(l1[:, k % 2, :], PS[:, bank + 1, 0:T], ACT.Identity,
                   bias=vec[:, bass.ds(e + V_B1L, 1)]).then_inc(s["l1_ready"], 1)
                act.wait_ge(s["xg_ready"], e + 1)
                fn(sg[:, k % 2, :], xg[:, k % 2, :], ACT.Sigmoid, scale=ALPHA).then_inc(s["sg_ready"], 1)

            for k in range(RING):
                expert(k, k, True)
            with act.Fori(1, E // RING) as i:
                for k in range(RING):
                    expert(i * RING + k, k, False)
            act.preload_act_table_set("natural_log_exp_and_others")
            act.wait_ge(s["xc_ready"], 3)
            norm(3, xc[:, :], 0)
            act.wait_ge(s["near_known"], 1)
            short = act.value_load(near_i[0:1, 0:1], min_val=0, max_val=1)

            def cross_near(l):
                def exps_near(u):
                    act.wait_ge(s["csub_done"], l * UNITS + (u + 1))
                    v = Pc[:, u, :, :].rearrange("p c k -> p (c k)")
                    fn(v, v, ACT.Exp, scale=SCALE).then_inc(s["cexp_done"], 1)

                def evac_near(u):
                    act.wait_ge(s["cturned"], l * UNITS + (u + 1))
                    fn(PTc[:, u, :, :].rearrange("p c q -> p (c q)"), PS[:, 4 + u % 2, 0:4 * PB],
                       ACT.Copy).then_inc(s["cpt_ready"], 1)

                def out_part_near(u):
                    act.wait_ge(s["cot_done"], l * UNITS + (u + 1))
                    fn(o[:, 2 * u * L:2 * (u + 1) * L], PS[:, 6 + u % 2, 300:300 + 2 * L], ACT.Copy)\
                        .then_inc(s["oc_part"], 1)

                exps_near(0)
                exps_near(1)
                evac_near(0)
                exps_near(2)
                evac_near(1)
                exps_near(3)
                evac_near(2)
                out_part_near(0)
                evac_near(3)
                out_part_near(1)
                out_part_near(2)
                out_part_near(3)

            def cross_long(l):
                with act.Fori(0, B) as b:
                    lb = l * B + b
                    act.wait_ge(s["far_kv"], lb + 1)
                    fn(gv.rearrange("p (c n) -> p c n", c=3), PS[:, 3:6, 0:SB], ACT.Copy).then_inc(s["gv_ready"], 1)
                    act.wait_ge(s["far_vt"], lb + 1)
                    fn(gV.rearrange("p c d -> p (c d)"), PS[0:KC, 3:6, :].rearrange("p k c -> p (k c)"), ACT.Copy)\
                        .then_inc(s["gV_ready"], 1)
                    with act.Fori(0, H) as hh_:
                        t = lb * H + hh_
                        act.wait_ge(s["fm_ready"], t + 1)
                        fn(gp, gp, ACT.Exp, scale=SCALE, accum_out=fmx[:, 2:3])\
                            .then_inc(s["fe_ready"], 1)
                        act.wait_ge(s["ft_ready"], t + 1)
                        fn(gPT, PS[0:KC, 6:8, :].rearrange("p k (c n) -> p (k c) n", n=64)[:, 0:NK, 0:L], ACT.Copy)\
                            .then_inc(s["fpt_ready"], 1)

            with act.Fori(0, NL) as l:
                act.preload_act_table_set("natural_log_exp_and_others")
                act.wait_ge(s["norm_ready"], l * 3 + 4)
                act.wait_ge(s["x_ready"], l * 3 + 2)
                norm(l * 3 + 4, xl[:, :], 1)
                act.wait_ge(s["norm_ready"], l * 3 + 5)
                fn(hd[:, :, :, :], heads3(h[:, :]).unsqueeze(2).broadcast_to([D, B, 2, L]), ACT.Copy)\
                    .then_inc(s["hd_ready"], 1)
                act.wait_ge(s["proj_done"], l * 5 + 5)
                values_out(l + 1)
                act.wait_ge(s["ckv_done"], l * 2 + 1)
                for g in range(GR):
                    fn(Kc[32 * g:32 * g + 32, :, g, :],
                       PS[32 * g:32 * g + 32, 6, 128:128 + B * NEAR].rearrange("p (b k) -> p b k", b=B), ACT.Copy)
                act.wait_ge(s["ckv_done"], l * 2 + 2)
                v = PS[:, 4:6, :].rearrange("p k (b c) -> p (k b) c", c=D)
                for g in range(GR):
                    last = fn(Vc[32 * g:32 * g + 32, :, :, g, 0:HV],
                              v[32 * g:32 * g + 32, :, 32 * g:32 * g + 32].rearrange("p b (j c) -> p b j c", j=2),
                              ACT.Copy)
                last.then_inc(s["ckv_ready"], 1)
                act.wait_ge(s["k_ready"], l + 1)
                keys_out(qk[:, 1, :])
                attention(l + 1)
                act.wait_ge(s["x_ready"], l * 3 + 3)
                norm(l * 3 + 5, xl[:, :], 1)

                with act.If(short == 1):
                    cross_near(l)
                with act.If(short == 0):
                    cross_long(l)
                act.wait_ge(s["x_ready"], l * 3 + 4)
                norm(l * 3 + 6, xl[:, :], 1)
                for c in range(FC):
                    act.wait_ge(s["g_done"], l * FC + (c + 1))
                    fn(sl[:, c, :], PS[:, 2 * (c % 2), 0:T], ACT.Silu).then_inc(s["silu_done"], 1)
            act.preload_act_table_set("natural_log_exp_and_others")
            act.wait_ge(s["x_ready"], 2 + 3 * NL)
            norm(4 + 3 * NL, xl[:, :], 1)
            act.wait_ge(s["xc_ready"], 4)
            norm(5 + 3 * NL, xc[:, :], 0)
            for c in range(FC):
                act.wait_ge(s["up_done"], c + 1)
                fn(hh[:, c, :], PS[:, c, 0:T], ACT.Relu, bias=bq[:, c:c + 1], scale=ss[:, c:c + 1])\
                    .then_inc(s["relu_done"], 1)
            act.wait_ge(s["down_done"], 1)
            fn(yt[:, :], PS[:, 6, 0:T], ACT.Identity, bias=bq[:, 4:5], scale=ss[:, 4:5]).then_inc(s["out_scaled"], 1)

        @block.vector
        def _(dve):
            v_ = nc.vector

            def layer_norm(i, k, src, dst):
                dve.wait_ge(s["mean_ready"], i + 1)
                v_.tensor_tensor(xc[:, :], src, PS[:, 6, 0:T], ALU.subtract).then_inc(s["xc_ready"], 1)
                dve.wait_ge(s["xc_ready"], i + 1)
                dve.wait_ge(s["rstd_ready"], k + 1)
                v_.tensor_tensor(dst, xc[:, :], rs[:, :], ALU.mult).then_inc(s["norm_ready"], 1)

            def rms_norm(k, src, w, dst):
                dve.wait_ge(s["rstd_ready"], k + 1)
                v_.scalar_tensor_tensor(dst, src, w, rs[:, :], ALU.mult, ALU.mult).then_inc(s["norm_ready"], 1)

            def queries_out(dst, src, ready):
                for j in range(HG):
                    last = v_.tensor_scalar(dst[:, :, j, :], heads3(src), colv(V_SEL + j), None, ALU.mult)
                last.then_inc(s[ready], 1)

            def normalise(u, own, done, n, back, ready):
                dve.wait_ge(s[done], n + (u + 1))
                v = PS[0:PB, 6 + u % 2, 0:16 * CO].rearrange("p (c x) -> p c x", x=CO)
                own(v_.reciprocal(rcp[:, u % 2, :].unsqueeze(2), v[:, :, HV:CO]))
                own(v_.tensor_tensor(wgt[:, u % 2, :, :], rcp[:, u % 2, :].unsqueeze(2).broadcast_to([PB, 16, 2]),
                                     vec[0:PB, V_ROW:V_ROW + 2].unsqueeze(1).broadcast_to([PB, 16, 2]), ALU.mult))
                if u >= 2:
                    dve.wait_ge(s[back], n + (u - 1))
                v_.tensor_tensor(O[:, u % 2, :, :].rearrange("p k (c j d) -> p (k c) j d", j=2, d=DH),
                                 v[:, :, 0:HV].rearrange("p c (j d) -> p c j d", j=2),
                                 wgt[:, u % 2, :, :].unsqueeze(3).broadcast_to([PB, 16, 2, DH]), ALU.mult)\
                    .then_inc(s[ready], 1)

            def attention(r, own):
                def softmax(u):
                    dve.wait_ge(s["s_ready"], r * UNITS + (u + 1))
                    src = PS[0:PB, 2 * (u % 2):2 * (u % 2) + 2, 0:8 * L].rearrange("p k (c l) -> p k c l", l=L)
                    m = mxs[:, u % 2, :].rearrange("p (k c) -> p k c", k=2)
                    own(v_.tensor_reduce(m, src, AX.X, ALU.max))
                    if u >= 2:
                        dve.wait_ge(s["turned"], r * UNITS + (u - 1))
                    v_.tensor_tensor(P[:, u % 2, :, :, :], src, m.unsqueeze(3).broadcast_to([PB, 2, 8, L]),
                                     ALU.subtract).then_inc(s["sub_done"], 1)

                def out(u):
                    normalise(u, own, "pv_done", r * UNITS, "ot_done", "on_ready")

                softmax(0)
                softmax(1)
                softmax(2)
                out(0)
                softmax(3)
                out(1)
                out(2)
                out(3)

            own = Chain(dve, s["dve_a"])
            dve.wait_ge(s["d_x"], 16)
            dve.wait_ge(s["d_vec"], 16)
            layer_norm(0, 0, xin[:, :], xh[:, :])
            dve.wait_ge(s["qp_copied"], 1)
            queries_out(Q4, qpT[:, 0:T], "q4_ready")
            for u in range(UNITS):
                dve.wait_ge(s["cand_scores"], u + 1)
                src = PS[:, 3 * (u % 2):3 * (u % 2) + 3, :].rearrange("p k c -> p (k c)")[:, 0:S]
                own(v_.max(mx8[:, :], src))
                own(v_.max_index(idx8[:, :], mx8[:, :], src))
                v_.tensor_tensor(rows[:, u:u + 1], idx8[:, 0:1], colv(V_BASE + u), ALU.add)\
                    .then_inc(s["rows_ready"], 1)
            dve.wait_ge(s["d_wq"], 32)
            v_.tensor_reduce(sw[:, 0:FC], w1n[:, :, :], AX.X, ALU.max, apply_absolute_value=True)
            own(v_.tensor_reduce(sw[:, FC:FC + 1], w2n[:, :], AX.X, ALU.max, apply_absolute_value=True))
            own(v_.tensor_scalar(sw[:, 0:5], sw[:, 0:5], 1e-8, 1.0 / 127.0, ALU.max, ALU.mult))
            own(v_.reciprocal(swi[:, 0:5], sw[:, 0:5]))
            for c in range(FC):
                v_.tensor_scalar(wt[:, 0, c * D:(c + 1) * D], w1n[:, c, :], swi[:, c:c + 1], MAGIC, ALU.mult, ALU.add)
            own(v_.tensor_scalar(wt[:, 1, :], w2n[:, :], swi[:, FC:FC + 1], MAGIC, ALU.mult, ALU.add))
            own(v_.tensor_scalar(wt[:, :, :], wt[:, :, :], -MAGIC, -128.0, ALU.add, ALU.max))
            v_.tensor_scalar(wqb[:, :, :], wt[:, :, :], 127.0, None, ALU.min).then_inc(s["wq_ready"], 1)
            attention(0, own)
            dve.wait_ge(s["wo_done"], 1)
            v_.tensor_tensor(x1[:, :], xin[:, :], PS[:, 0, 0:T], ALU.add).then_inc(s["x_ready"], 1)

            layer_norm(1, 1, x1[:, :], xh[:, :])
            dve.wait_ge(s["norm_ready"], 2)
            rms_norm(2, xh[:, :], colv(V_SCALE), h[:, :])
            dve.wait_ge(s["gate_done"], 1)
            dve.wait_ge(s["d_gw"], 32)
            own(v_.tensor_tensor(gl[:, :, :], PS[0:PB, 0, 0:UNITS * E].rearrange("p (u e) -> p u e", e=E),
                                 gb[:, :].unsqueeze(1).broadcast_to([PB, UNITS, E]), ALU.add))
            for u in range(UNITS):
                v = v_.max(gm8[:, u, :], gl[:, u, :])
            own(v)
            for u in range(UNITS):
                v = v_.max_index(gi8[:, u, :], gm8[:, u, :], gl[:, u, :])
            own(v)
            dve.wait_ge(s["consts"], 13)
            own(v_.tensor_copy(gif[:, :, :], gi8[:, :, 0:TOPK]))
            v_.tensor_tensor(ge[:, :, :], gl[:, :, :], gm8[:, :, 0:1].broadcast_to([PB, UNITS, E]), ALU.subtract)\
                .then_inc(s["gexp_in"], 1)
            own(v_.tensor_tensor(eq[:, :, :, :],
                                 eiof[:, :].unsqueeze(1).unsqueeze(3).broadcast_to([PB, UNITS, E, TOPK]),
                                 gif[:, :, :].unsqueeze(2).broadcast_to([PB, UNITS, E, TOPK]), ALU.is_equal))
            own(v_.tensor_reduce(gl[:, :, :], eq[:, :, :, :], AX.X, ALU.add))
            dve.wait_ge(s["gexp_done"], 1)
            own(v_.tensor_tensor(gl[:, :, :], gl[:, :, :], ge[:, :, :], ALU.mult))
            own(v_.tensor_reduce(gsum[:, :], gl[:, :, :], AX.X, ALU.add))
            own(v_.reciprocal(gsum[:, :], gsum[:, :]))
            v_.tensor_tensor(ge[:, :, :], gl[:, :, :], gsum[:, :].unsqueeze(2).broadcast_to([PB, UNITS, E]),
                             ALU.mult).then_inc(s["route_ready"], 1)
            dve.wait_ge(s["route_turned"], 1)
            ps = PS[0:E, 1, 0:T]
            own(v_.tensor_copy(rb[0:E, :], ps))
            own(v_.tensor_tensor(rpart[:, 0, :], ps, rb[0:E, :], ALU.subtract))
            v_.tensor_copy(routeT[:, :], ps)
            v_.tensor_copy(rb[32:32 + E, :], rpart[:, 0, :])
            own(v_.tensor_copy(rmid[:, :], rpart[:, 0, :]))
            own(v_.tensor_tensor(rpart[:, 1, :], rpart[:, 0, :], rmid[:, :], ALU.subtract))
            v_.tensor_copy(rb[64:64 + E, :], rpart[:, 1, :]).then_inc(s["rb_ready"], 1)

            def expert(e, k, first):
                bank = 3 * (k % 2)
                dve.wait_ge(s["e_glr"], e + 1)
                v_.tensor_scalar(xg[:, k % 2, :], PS[:, bank, 0:T], vec[:, bass.ds(e + V_B1G, 1)], LIMIT,
                                 ALU.add, ALU.min).then_inc(s["xg_ready"], 1)
                dve.wait_ge(s["l1_ready"], e + 1)
                v_.tensor_scalar(l2[:, k % 2, :], l1[:, k % 2, :], LIMIT, LIMIT, ALU.max, ALU.min)\
                    .then_inc(s["l2_ready"], 1)
                dve.wait_ge(s["l2_ready"], e + 1)
                v_.scalar_tensor_tensor(ww[:, k % 2, :], l2[:, k % 2, :], 1.0, PS[:, bank + 2, 0:T],
                                        ALU.add, ALU.mult).then_inc(s["ww_ready"], 1)
                dve.wait_ge(s["sg_ready"], e + 1)
                v_.tensor_tensor(vv[:, k % 2, :], xg[:, k % 2, :], sg[:, k % 2, :], ALU.mult)\
                    .then_inc(s["vv_ready"], 1)
                dve.wait_ge(s["ww_ready"], e + 1)
                dve.wait_ge(s["vv_ready"], e + 1)
                if not first or k >= 2:
                    dve.wait_ge(s["y_done"], e - 1)
                v_.tensor_tensor(zz[:, k % 2, :], ww[:, k % 2, :], vv[:, k % 2, :], ALU.mult)\
                    .then_inc(s["zz_ready"], 1)

            for k in range(RING):
                expert(k, k, True)
            with dve.Fori(1, E // RING) as i:
                for k in range(RING):
                    expert(i * RING + k, k, False)
            own(v_.tensor_tensor(x2[:, :], x1[:, :], xh[:, :], ALU.add))
            dve.wait_ge(s["y_done"], E)
            v_.tensor_tensor(x2[:, :], x2[:, :], PS[:, 6, 0:T], ALU.add).then_inc(s["x_ready"], 1)

            layer_norm(2, 3, x2[:, :], xl[:, :])
            dve.wait_ge(s["d_seg"], 16)
            dve.wait_ge(s["consts"], 15)
            own(v_.tensor_copy(segf[:, 0, :], seg[:, :]))
            own(v_.tensor_scalar(segf[:, 1, :], segf[:, 0, :], -float(LOOKBACK), None, ALU.add))
            for b in range(B):
                v_.tensor_scalar(xm[:, 0, :], krowf[:, :], segf[:, 0, b:b + 1], NEG, ALU.is_gt, ALU.mult)
                own(v_.tensor_scalar(xm[:, 1, :], krowf[:, :], segf[:, 1, b:b + 1], NEG, ALU.is_le, ALU.mult))
                last = v_.tensor_tensor(xbias[:, b, :].rearrange("p (g k) -> p g k", g=GR),
                                        xm[:, 0, :].unsqueeze(1).broadcast_to([PB, GR, NEAR]),
                                        xm[:, 1, :].unsqueeze(1).broadcast_to([PB, GR, NEAR]), ALU.add)
                own(last)
            v_.tensor_copy(cz[:, 0, 0:B], segf[:, 0, :]).then_inc(s["xbias_ready"], 1)
            dve.wait_ge(s["d_par"], 16)
            dve.wait_ge(s["d_cs"], 16)
            dve.wait_ge(s["d_segrow"], 16)
            own(v_.tensor_copy(segrf[:, :], segrow[:, :]))
            own(v_.tensor_reduce(lim[:, 0:1], segrf[:, :], AX.X, ALU.max))
            own(v_.tensor_reduce(lim[:, 1:2], segrf[:, :], AX.X, ALU.min))
            own(v_.tensor_scalar(lim[:, 2:3], lim[:, 0:1], NEAR - 0.5, None, ALU.is_lt))
            own(v_.tensor_scalar(lim[:, 3:4], lim[:, 1:2], 0.0, lim[:, 2:3], ALU.is_ge, ALU.mult))
            v_.tensor_copy(near_i[:, :], lim[:, 3:4]).then_inc(s["near_known"], 1)
            dve.wait_ge(s["near_known"], 1)
            short = dve.value_load(near_i[0:1, 0:1], min_val=0, max_val=1)

            def cross_near(l):
                own_c = Chain(dve, s["dve_c"], l * (3 * UNITS))
                dve.wait_ge(s["qc_done"], l + 1)
                queries_out(Q4c, PS[:, 1, 0:T], "q4c_ready")

                def softmax(u):
                    dve.wait_ge(s["cs_ready"], l * UNITS + (u + 1))
                    src = PS[0:PB, u, :].rearrange("p (c k) -> p c k", k=NEAR)
                    own_c(v_.tensor_reduce(mxs[:, u % 2, :], src, AX.X, ALU.max))
                    v_.tensor_tensor(Pc[:, u, :, :], src, mxs[:, u % 2, :].unsqueeze(2).broadcast_to([PB, 16, NEAR]),
                                     ALU.subtract).then_inc(s["csub_done"], 1)

                def out(u):
                    normalise(u, own_c, "cpv_done", l * UNITS, "cot_done", "con_ready")

                softmax(0)
                softmax(1)
                softmax(2)
                out(0)
                softmax(3)
                out(1)
                out(2)
                out(3)
                dve.wait_ge(s["oc_part"], l * UNITS + UNITS)
                v_.tensor_copy(tq[:, 1, 0:1], o[:, 0:1]).then_inc(s["oc_ready"], 1)

            def cross_long(l):
                dve.wait_ge(s["qc_done"], l + 1)
                v_.tensor_copy(tq[:, 0, :], PS[:, 1, 0:T]).then_inc(s["far_step"], 1)
                with dve.Fori(0, B) as b:
                    lb = l * B + b
                    fb = Chain(dve, s["dve_fb"], lb * 7)
                    dve.wait_ge(s["far_step"], l * (B + 1) + b + 1)
                    fb(v_.tensor_copy(gq, tq[:, 0, bass.ds(b * L, L)]))
                    for k in range(3):
                        fb(v_.tensor_scalar(gi[:, k * SB:(k + 1) * SB], frow[:, :], float(k * SB), None, ALU.add))
                    fb(v_.tensor_scalar(gb_, gi, segf[0:L, 0, bass.ds(b, 1)], NEG, ALU.is_gt, ALU.mult))
                    fb(v_.tensor_scalar(gi, gi, segf[0:L, 1, bass.ds(b, 1)], NEG, ALU.is_le, ALU.mult))
                    fb(v_.tensor_tensor(gb_, gb_, gi, ALU.add))
                    dve.wait_ge(s["far_kv"], lb + 1)
                    v_.tensor_copy(gk.rearrange("p (c n) -> p c n", c=3), PS[:, 0:3, 0:SB]).then_inc(s["gk_ready"], 1)
                    with dve.Fori(0, H) as hh_:
                        t = lb * H + hh_
                        fh = Chain(dve, s["dve_fh"], t * 4)
                        dve.wait_ge(s["gk_ready"], lb + 1)
                        v_.tensor_scalar(gqz, gq, vec[:, bass.ds(hh_ + V_HEAD, 1)], None, ALU.mult)\
                            .then_inc(s["gq_ready"], 1)
                        dve.wait_ge(s["fs_ready"], t + 1)
                        fh(v_.tensor_tensor(gp.rearrange("p (c n) -> p c n", c=3), PS[0:L, 0:3, 0:SB],
                                            gb_.rearrange("p (c n) -> p c n", c=3), ALU.add))
                        fh(v_.tensor_reduce(fmx[:, 0:1], gp, AX.X, ALU.max))
                        v_.tensor_scalar(gp, gp, fmx[:, 0:1], None, ALU.subtract).then_inc(s["fm_ready"], 1)
                        dve.wait_ge(s["fo_ready"], t + 1)
                        fh(v_.reciprocal(fmx[:, 0:1], fmx[:, 2:3]))
                        fh(v_.tensor_scalar(gO[:, bass.ds(hh_ * DH, DH)], PS[0:L, 3, 0:DH], fmx[:, 0:1], None,
                                            ALU.mult))
                    v_.tensor_copy(gOc, gO).then_inc(s["fO_ready"], 1)
                    dve.wait_ge(s["ff_ready"], lb + 1)
                    v_.tensor_copy(o[:, bass.ds(b * L, L)], PS[:, 4, 0:L]).then_inc(s["far_step"], 1)
                dve.wait_ge(s["far_step"], l * (B + 1) + (B + 1))
                v_.tensor_copy(tq[:, 1, 0:1], o[:, 0:1]).then_inc(s["oc_ready"], 1)

            with dve.Fori(0, NL) as l:
                own = Chain(dve, s["dve_l"], l * NDVE)
                own(v_.tensor_copy(pl[:, :], par[:, bass.ds(l, 1), :].rearrange("p l n -> p (l n)")))
                dve.wait_ge(s["norm_ready"], l * 3 + 4)
                dve.wait_ge(s["x_ready"], l * 3 + 2)
                rms_norm(l * 3 + 4, xl[:, :], pl[:, N1:N1 + 1], h[:, :])
                for i, (t, b1, b2) in enumerate(((tq, BQ, BQR), (tk, BK, BKR))):
                    dve.wait_ge(s["proj_done"], l * 5 + (2 * i + 1))
                    v_.scalar_tensor_tensor(t[:, 0, :], PS[:, 2 * i, 0:T], pl[:, b1:b1 + 1], cs[:, 0, :],
                                            ALU.add, ALU.mult)
                    dve.wait_ge(s["proj_done"], l * 5 + (2 * i + 2))
                    own(v_.scalar_tensor_tensor(t[:, 1, :], PS[:, 2 * i + 1, 0:T], pl[:, b2:b2 + 1], cs[:, 1, :],
                                                ALU.add, ALU.mult))
                    add = v_.tensor_tensor(qk[:, i, :], t[:, 0, :], t[:, 1, :], ALU.add)
                    if i == 1:
                        add.then_inc(s["k_ready"], 1)
                    else:
                        own(add)
                        queries_out(Q4, qk[:, 0, :], "q4_ready")
                dve.wait_ge(s["ckv_ready"], l + 1)
                v_.tensor_tensor(bo2[:, :], pl[:, BO:BO + 1], PS[:, 6, 0:1], ALU.add).then_inc(s["bo_ready"], 1)
                dve.wait_ge(s["bo_ready"], l + 1)
                attention(l + 1, own)
                dve.wait_ge(s["wo_done"], l + 2)
                v_.scalar_tensor_tensor(xl[:, :], PS[:, 0, 0:T], bo2[:, 0:1], xl[:, :], ALU.add, ALU.add)\
                    .then_inc(s["x_ready"], 1)
                dve.wait_ge(s["x_ready"], l * 3 + 3)
                rms_norm(l * 3 + 5, xl[:, :], pl[:, N2:N2 + 1], h[:, :])
                with dve.If(short == 1):
                    cross_near(l)
                with dve.If(short == 0):
                    cross_long(l)
                dve.wait_ge(s["woc_done"], l + 1)
                v_.tensor_tensor(xl[:, :], xl[:, :], PS[:, 0, 0:T], ALU.add).then_inc(s["x_ready"], 1)
                dve.wait_ge(s["x_ready"], l * 3 + 4)
                rms_norm(l * 3 + 6, xl[:, :], pl[:, N3:N3 + 1], h[:, :])
                for c in range(FC):
                    dve.wait_ge(s["silu_done"], l * FC + (c + 1))
                    dve.wait_ge(s["u_done"], l * FC + (c + 1))
                    v_.tensor_tensor(mm[:, c, :], sl[:, c, :], PS[:, 2 * (c % 2) + 1, 0:T], ALU.mult)\
                        .then_inc(s["m_ready"], 1)
                dve.wait_ge(s["d_done"], l + 1)
                v_.tensor_tensor(xl[:, :], xl[:, :], PS[:, 4, 0:T], ALU.add).then_inc(s["x_ready"], 1)
                assert own.n == NDVE, own.n
            own = Chain(dve, s["dve_d"])
            dve.wait_ge(s["x_ready"], 2 + 3 * NL)
            rms_norm(4 + 3 * NL, xl[:, :], colv(V_NF), h[:, :])
            dve.wait_ge(s["norm_ready"], 5 + 3 * NL)
            v_.tensor_tensor(x3[:, :], x2[:, :], h[:, :], ALU.add).then_inc(s["x_ready"], 1)
            dve.wait_ge(s["x_ready"], 3 + 3 * NL)

            dve.wait_ge(s["wq_turned"], 1)
            v_.tensor_copy(w1qT[:, :], PS[:, 0, 0:256].bitcast(BF16))
            v_.tensor_copy(w2qT[:, :, :].rearrange("p c d -> p (c d)"), PS[:, 1, 0:256].bitcast(BF16))\
                .then_inc(s["wqT_ready"], 1)
            layer_norm(3, 5 + 3 * NL, x3[:, :], yt[:, :])
            dve.wait_ge(s["norm_ready"], 6 + 3 * NL)

            def scale_of(i, c):
                dve.wait_ge(s["max_turned"], i + 1)
                own(v_.tensor_reduce(s11[0:1, 1:2], PS[0:1, 5, 0:D], AX.X, ALU.max))
                v_.tensor_scalar(s11[0:1, 2:3], s11[0:1, 1:2], 1e-8, 1.0 / 255.0, ALU.max, ALU.mult)\
                    .then_inc(s["s_one"], 1)
                dve.wait_ge(s["s_bcast"], i + 1)
                own(v_.tensor_copy(s11[:, c:c + 1], PS[:, 4, 0:1]))
                own(v_.reciprocal(s11[:, c + 1:c + 2], s11[:, c:c + 1]))

            def bias_of(c0, n, src, sc):
                own(v_.tensor_scalar(ss[:, c0:c0 + n], sw[:, c0:c0 + n], s11[:, sc:sc + 1], None, ALU.mult))
                own(v_.reciprocal(swi[:, c0:c0 + n], ss[:, c0:c0 + n]))
                own(v_.tensor_tensor(bq[:, c0:c0 + n], src, swi[:, c0:c0 + n], ALU.mult))
                own(v_.tensor_scalar(bq[:, c0:c0 + n], bq[:, c0:c0 + n], MAGIC, -MAGIC, ALU.add, ALU.add))
                own(v_.tensor_tensor(bq[:, c0:c0 + n], bq[:, c0:c0 + n], ss[:, c0:c0 + n], ALU.mult))

            v_.tensor_reduce(s11[:, 0:1], yt[:, :], AX.X, ALU.max).then_inc(s["max_in"], 1)
            scale_of(0, 3)
            own(v_.tensor_scalar(sq2[:, :], yt[:, :], s11[:, 4:5], MAGIC, ALU.mult, ALU.add))
            own(v_.tensor_scalar(sq2[:, :], sq2[:, :], -MAGIC, 0.0, ALU.add, ALU.max))
            own(v_.tensor_scalar(yq[:, :], sq2[:, :], 255.0, None, ALU.min))
            bias_of(0, FC, colv(V_B1, FC), 3)
            v_.tensor_copy(s11[:, 5:6], s11[:, 3:4]).then_inc(s["yq_ready"], 1)
            for c in range(FC):
                dve.wait_ge(s["relu_done"], c + 1)
                v = v_.tensor_reduce(s11[:, 8 + c:9 + c], hh[:, c, :], AX.X, ALU.max)
            own(v)
            v_.tensor_reduce(s11[:, 0:1], s11[:, 8:8 + FC], AX.X, ALU.max).then_inc(s["max_in"], 1)
            scale_of(1, 6)
            own(v_.tensor_scalar(ht[:, :, :], hh[:, :, :], s11[:, 7:8], MAGIC, ALU.mult, ALU.add))
            own(v_.tensor_scalar(ht[:, :, :], ht[:, :, :], -MAGIC, 0.0, ALU.add, ALU.max))
            own(v_.tensor_scalar(hq[:, :, :], ht[:, :, :], 255.0, None, ALU.min))
            bias_of(FC, 1, colv(V_B2), 6)
            v_.tensor_copy(s11[:, 5:6], s11[:, 6:7]).then_inc(s["hq_ready"], 1)
            dve.wait_ge(s["out_scaled"], 1)
            v_.tensor_tensor(yt[:, :], yt[:, :], x3[:, :], ALU.add).then_inc(s["out_ready"], 1)


def kernel(**inputs):
    import concourse.bacc as _bacc
    from concourse.bass_utils import run_bass_kernel_spmd as _run

    g = {n: np.asarray(v) for n, v in inputs.items()}
    f32 = np.float32
    x, ctxt = g["x"], g["ctx_1024"]
    arr = {}
    arr["xT"] = x.reshape(T, D).T
    arr["ctx"] = ctxt.reshape(B * S, D)
    arr["ctxT"] = ctxt.reshape(B * S, D).T
    wkv = g["L0_xattn_Wkv"]
    arr["wa0"] = np.concatenate([g["L0_xattn_Wq"].T, np.tile(wkv[:DH], (H, 1)).T, np.tile(wkv[DH:], (H, 1)).T,
                                 g["L0_xattn_Wc"].T], axis=1)
    arr["gw"] = g["L0_ffn_gate_w"].T
    arr["gb"] = np.tile(g["L0_ffn_gate_b"][None], (PB, 1))
    m1, m1b = g["L0_ffn_mlp1_w"], g["L0_ffn_mlp1_b"]
    arr["ew"] = np.concatenate([m1[:, ::2].transpose(2, 0, 1), m1[:, 1::2].transpose(2, 0, 1),
                                g["L0_ffn_mlp2_w"].transpose(2, 0, 1)], axis=2).reshape(D, E * 3 * D)
    arr["b2e"] = g["L0_ffn_mlp2_b"]
    seg = g["itok_BxS_0_255"]
    arr["seg"] = np.tile(seg.T, (2, 1)).astype(np.int32)
    arr["segrow"] = seg.reshape(1, T).astype(np.int32)
    arr["w1n"] = g["L1_ffn_w1"].reshape(FC, D, D).transpose(1, 0, 2)
    arr["w2n"] = g["L1_ffn_w2"]
    inv = (1.0 / f32(10000.0) ** (np.arange(0, DH, 2, dtype=f32) / f32(DH))).astype(f32)
    ang = np.arange(L, dtype=f32)[:, None] * inv[None]
    half = DH // 2
    dim = np.arange(D) % DH
    cos, sin = np.cos(ang).astype(f32)[:, dim % half].T, np.sin(ang).astype(f32)[:, dim % half].T
    sin = np.where(dim[:, None] < half, -sin, sin)
    arr["cs"] = np.stack([np.tile(cos, (1, B)), np.tile(sin, (1, B))], axis=1).astype(f32)
    swap = np.arange(D) - dim + (dim + half) % DH
    wqkv, bqkv = g["L1_xattn_Wqkv"], g["L1_xattn_bqkv"]
    wq, wk, wv = wqkv[:, 0:D], wqkv[:, D:2 * D], wqkv[:, 2 * D:]
    bq_, bk_, bv_ = bqkv[:, 0:D], bqkv[:, D:2 * D], bqkv[:, 2 * D:]
    wkvc = g["L1_xattn_Wkv_c"]
    blocks = [wq, wq[:, swap], wk, wk[:, swap], wv, g["L1_xattn_Wo"], g["L1_xattn_Wq_c"], wkvc[:, :D], wkvc[:, D:],
              g["L1_xattn_Wo_c"]]
    arr["wA"] = np.concatenate([w.transpose(2, 0, 1) for w in blocks], axis=2).reshape(D, NL * WATT)
    down = g["L1_xattn_Wd"].reshape(NL, D, FC, D).transpose(3, 0, 2, 1).reshape(D, NL, FF)
    arr["wF"] = np.concatenate([g["L1_xattn_Wg"].transpose(2, 0, 1), g["L1_xattn_Wu"].transpose(2, 0, 1), down],
                               axis=2).reshape(D, NL * WFFN)
    arr["par"] = np.stack([bq_, bq_[:, swap], bk_, bk_[:, swap], bv_, g["L1_xattn_bo"], g["L1_xattn_n1"],
                           g["L1_xattn_n2"], g["L1_xattn_n3"]], axis=0).transpose(2, 1, 0)
    p = np.arange(D)
    sel = (p[:, None] // DH % HG == np.arange(HG)[None]).astype(f32)
    row = np.stack([p < L, (p >= L) & (p < PB)], axis=1).astype(f32)
    base = (2 * np.arange(UNITS)[None] + p[:, None] // 64).astype(f32) * f32(S)
    heads = (p[:, None] // DH == np.arange(H)[None]).astype(f32)
    arr["vec"] = np.concatenate([g["L0_ffn_scale"][:, None], g["L1_xattn_nf"][:, None], g["L1_ffn_b2"][:, None],
                                 g["L1_ffn_b1"].reshape(FC, D).T, sel, row, base, m1b[:, ::2].T, m1b[:, 1::2].T,
                                 heads], axis=1)
    nc = _bacc.Bacc("TRN2", target_bir_lowering=False, num_devices=1)
    feed, aps = {}, {}
    for name, v in arr.items():
        v = np.ascontiguousarray(v)
        feed[f"in_{name}"] = v
        aps[name] = nc.dram_tensor(f"in_{name}", v.shape, mybir.dt.from_np(v.dtype), kind="ExternalInput").ap()
    out = nc.dram_tensor("out_0", (D, T), F32, kind="ExternalOutput").ap()
    build(nc, aps, out)
    r = _run(nc, [feed], core_ids=[0])
    return r.results[0]["out_0"].T.reshape(B, L, D)
```

```python
from contextlib import ExitStack

import numpy as np

import concourse.bass as bass
from concourse import mybir

F32 = mybir.dt.float32
BF16 = mybir.dt.bfloat16
I32 = mybir.dt.int32
U32 = mybir.dt.uint32
ALU = mybir.AluOpType
ACT = mybir.ActivationFunctionType
AX = mybir.AxisListType

D = 128
B = 8
L = 56
T = B * L
H = 16
DH = D // H
GR = 4
HG = H // GR
S = 1500
NL = 4
E = 16
TOPK = 4
FF = 512
FC = FF // D
HV = 2 * DH
CO = HV + 1
NEAR = 32
LOOKBACK = 128
KC = 125
NK = S // KC
SB = 500
UNITS = 4
PB = 2 * L
SCALE = float(1.0 / np.sqrt(np.float32(DH)))
WARM_SQ = 6
WARM_NORM = 9
NEG = -1e30
MAGIC = 12582912.0
LIMIT = 7.0
ALPHA = 1.702

WQ, WQR, WK, WKR, WV, WO, WQC, WKC, WVC, WOC = (i * D for i in range(10))
WATT = 10 * D
WG, WU, WD = 0, FF, 2 * FF
WFFN = 3 * FF
BQ, BQR, BK, BKR, BV, BO, N1, N2, N3 = range(9)
NP_ = 9
HT = T // 2
HB = B // 2
NDVE_LONG = 27
NDVE = 42
V_SCALE, V_NF, V_B2 = 0, 1, 2
V_B1 = 3
V_SEL = V_B1 + FC
V_ROW = V_SEL + HG
V_BASE = V_ROW + 2
V_B1G = V_BASE + UNITS
V_B1L = V_B1G + E
V_HEAD = V_B1L + E
NV = V_HEAD + H


class Chain:

    def __init__(self, eng, sem, start=0):
        self.eng, self.sem, self.start, self.n = eng, sem, start, 0

    def __call__(self, ins):
        self.n += 1
        ins.then_inc(self.sem, 1)
        self.eng.wait_ge(self.sem, self.start + self.n)

    def mark(self, ins):
        self.n += 1
        ins.then_inc(self.sem, 1)
        return self.start + self.n


def build(nc, a, out):
    ctx = ExitStack()
    with ctx:
        def sb(name, shape, dt=F32):
            return ctx.enter_context(nc.sbuf_tensor(name, shape, dt))

        def sem(name):
            return ctx.enter_context(nc.semaphore(name))

        ctxT = sb("ctxT", [D, B * S])
        arena = [0]

        def carve(*shape):
            n = int(np.prod(shape))
            assert arena[0] + n <= B * S
            flat = ctxT[:, arena[0]:arena[0] + n]
            arena[0] += n
            if len(shape) == 1:
                return flat
            names = "abcde"[:len(shape)]
            return flat.rearrange("p (" + " ".join(names) + ") -> p " + " ".join(names),
                                  **{c: m for c, m in zip(names[1:], shape[1:])})

        xin = sb("xin", [D, T])
        xc = sb("xc", [D, T])
        sq = sb("sq", [D, T])
        rs = sb("rs", [D, T])
        xh = sb("xh", [D, T])
        h = sb("h", [D, T])
        x1 = sb("x1", [D, T])
        x2 = sb("x2", [D, T])
        xl = sb("xl", [D, T])
        wa0 = sb("wa0", [D, 4 * D])
        wA = sb("wA", [D, WATT])
        wF = sb("wF", [D, WFFN])
        par = sb("par", [D, NL, NP_])
        pl = sb("pl", [D, NP_])
        vec = sb("vec", [D, NV])
        cs = sb("cs", [D, 2, T])
        seg = sb("seg", [PB, B], I32)
        segrow = sb("segrow", [1, T], I32)
        segrf = sb("segrf", [1, T])
        lim = sb("lim", [1, 4])
        near_i = sb("near_i", [1, 1], I32)
        fmx = sb("fmx", [L, 3])
        segf = sb("segf", [PB, 2, B])
        ident = sb("ident", [D, D])
        identb = sb("identb", [D, D], BF16)
        warm = sb("warm", [D, 8 * L], BF16)
        onesD = sb("onesD", [D, D])
        ones1 = sb("ones1", [1, D])
        eps = sb("eps", [D, 2])
        causal = sb("causal", [PB, 8, L], BF16)
        frow = sb("frow", [L, SB])
        cz = sb("cz", [PB, 4, L])
        krow = sb("krow", [PB, NEAR], I32)
        krowf = sb("krowf", [PB, NEAR])
        xm = sb("xm", [PB, 2, NEAR])
        qpT = sb("qpT", [D, T + 8])
        mx8 = sb("mx8", [D, 8])
        idx8 = sb("idx8", [D, 8], U32)
        rows = sb("rows", [D, UNITS], U32)
        mem = sb("mem", [D, UNITS, D])
        tq = sb("tq", [D, 2, T])
        memD = tq[:, :, :].rearrange("p a t -> p (a t)").rearrange("p (b k l) -> p b k l", b=B, k=2)
        Q4 = sb("Q4", [D, B, HG, L])
        Kz = sb("Kz", [D, B, GR, L])
        VB = sb("VB", [PB, B, 2, 2, 2, HV + 1])
        O = sb("O", [PB, 2, 2, D])
        rcp = sb("rcp", [PB, 2, 16])
        wgt = sb("wgt", [PB, 2, 16, 2])
        fold = sb("fold", [PB, L])
        P = sb("P", [PB, 2, 2, 8, L])
        PT = sb("PT", [PB, 2, 2, 4, PB])
        mxs = sb("mxs", [PB, 2, 16])
        o = sb("o", [D, T])
        Kc = sb("Kc", [D, B, GR, NEAR])
        Vc = sb("Vc", [D, B, 2, GR, HV + 1])
        near = sb("near", [D, B, NEAR])
        bo2 = sb("bo2", [D, 1])
        gw = sb("gw", [D, E])
        gb = sb("gb", [PB, E])
        gl = sb("gl", [PB, UNITS, E])
        gm8 = sb("gm8", [PB, UNITS, 8])
        gi8 = sb("gi8", [PB, UNITS, 8], U32)
        gif = sb("gif", [PB, UNITS, TOPK])
        eio = sb("eio", [PB, E], I32)
        eiof = sb("eiof", [PB, E])
        eq = sb("eq", [PB, UNITS, E, TOPK])
        ge = sb("ge", [PB, UNITS, E])
        gsum = sb("gsum", [PB, UNITS])
        b2e = sb("b2e", [E, D])
        RING = 4
        ew = sb("ew", [D, RING, 3 * D])
        wn = sb("wn", [D, 2, FF])
        w1n = wn[:, 0, :].rearrange("p (c d) -> p c d", c=FC)
        w2n = wn[:, 1, :]
        wt = wn
        wqb = sb("wqb", [D, 2, FF], BF16)
        w1qT = sb("w1qT", [D, FF], BF16)
        w2qT = sb("w2qT", [D, FC, D], BF16)
        sw = sb("sw", [D, 8])
        swi = sb("swi", [D, 8])
        ss = sb("ss", [D, 8])
        bq = sb("bq", [D, 8])
        s11 = sb("s11", [D, 12])
        yt = sb("yt", [D, T])
        yq = sb("yq", [D, T], BF16)
        def bf16(ap):
            return ap.bitcast(BF16)

        sel = bf16(carve(E * D // 2)[0:96]).rearrange("p (e d) -> p e d", e=E)
        rpart = carve(2, T)[0:E]
        routeT = carve(T)[0:E]
        rmid = bf16(carve(T // 2)[0:E])
        rb = bf16(carve(T // 2)[0:96])
        xg, sg, l1, l2, vv, ww, zz = (carve(2, T) for _ in range(7))
        arena[0] = 0
        Q4c = carve(B, HG, L)
        Pc = carve(UNITS, 16, NEAR)[0:PB]
        PTc = carve(UNITS, 4, PB)
        sl = carve(FC, T)
        mm = sl
        hd = carve(B, 2, L)
        near4 = carve(B, GR, NEAR)
        tk = carve(2, T)
        qk = carve(2, T)
        xbias = bf16(carve(B * GR * NEAR // 2)[0:PB]).rearrange("p (b k) -> p b k", b=B)
        x3 = x1
        arena[0] = 0
        gx = carve(S)
        gk = carve(S)
        gv = carve(S)
        gV = carve(NK, D)[0:KC]
        gp = carve(S)[0:L]
        gPT = carve(NK, L)[0:KC]
        assert arena[0] <= 8320
        gb_ = P[:, :, :, :, :].rearrange("p a b c l -> p (a b c l)")[0:L, 0:S]
        gi = PT[:, :, :, :, :].rearrange("p a b c l -> p (a b c l)")[0:L, 0:S]
        gq, gqz = tk[:, 0, 0:L], tk[:, 0, 64:64 + L]
        gO, gOc = qk[0:L, 0, 0:D], qk[0:L, 1, 0:D]
        arena[0] = 0
        sq2 = carve(T)
        hh = carve(FC, T)
        ht = carve(FC, T)
        hq = carve(FC * T // 2).bitcast(BF16).rearrange("p (c t) -> p c t", c=FC)

        PS = ctx.enter_context(nc.psum_tensor("PS", [D, 8, 512], F32))

        names = """n_x n_sq n_ms n_rs n_h n_hd n_proj n_k n_wo n_qc n_woc n_q4c n_up n_silu n_m n_down
        layers_done n_ln ln_last sq_last ms_last rs_last yt_ready n_dve warm_ready d_x d_vec d_wa0 d_ctx0 d_ctx1 d_ctx2 d_ctx3 d_gw d_seg d_cs d_par d_wA d_wF d_wq d_b2e
        ln_done on_ready ot_done con_ready cot_done near_out near_ready d_segrow near_known far_step d_gx far_kv gk_ready gv_ready far_vt gV_ready gq_ready fs_ready fm_ready fe_ready ft_ready fpt_ready fo_ready fO_ready ff_ready dve_fb dve_fh ww_ready x_ready xbias_ready bo_ready d_near d_ew0 d_ew1 d_ew2 d_ew3 d_out g0 g1 g2 g3
        consts pool_own dve_a dve_l dve_d         mean_ready xc_ready sq_ready ms_ready rstd_ready norm_ready
        qp_done qp_copied cand_scores rows_ready mem_turned memT_ready kv_done
        proj_done q4_ready k_ready kz_ready vb_ready s_ready sub_done exp_done turned pt_ready pv_done o_ready
        wo_done ckv_done ckv_ready qc_done cs_ready csub_done cexp_done cturned cpt_ready cpv_done oc_ready
        woc_done g_done u_done silu_done m_ready d_done pl_ready
        gate_done route_ready gexp_in gexp_done route_turned rb_ready
        e_glr xg_ready sg_ready l1_ready l2_ready vv_ready zz_ready y_done         wq_ready wq_turned wqT_ready max_in max_turned s_one s_bcast yq_ready up_done relu_done hq_ready down_done out_scaled out_ready""".split()
        s = {n: sem(n) for n in names}

        ctx.enter_context(nc.allow_non_contiguous_dma(reason="small vectors"))
        block = ctx.enter_context(nc.Block())

        def colv(c, n=1, p=D):
            return vec[0:p, c:c + n]

        def heads3(ap):
            return ap.rearrange("p (b l) -> p b l", b=B)

        @block.sync
        def _(sp):
            sp.dma_start(xin[:, :], a["xT"]).then_inc(s["d_x"], 16)
            sp.dma_start(vec[:, :], a["vec"]).then_inc(s["d_vec"], 16)
            sp.dma_start(wa0[:, :], a["wa0"]).then_inc(s["d_wa0"], 16)
            for u in range(UNITS):
                sp.dma_start(ctxT[:, u * 2 * S:(u + 1) * 2 * S],
                             a["ctxT"][:, u * 2 * S:(u + 1) * 2 * S]).then_inc(s[f"d_ctx{u}"], 16)
            sp.dma_start(gw[:, :], a["gw"]).then_inc(s["d_gw"], 16)
            sp.dma_start(gb[:, :], a["gb"]).then_inc(s["d_gw"], 16)
            sp.dma_start(b2e[:, :], a["b2e"]).then_inc(s["d_b2e"], 16)
            for e in range(RING):
                sp.dma_start(ew[:, e, :], a["ew"][:, e * 3 * D:(e + 1) * 3 * D]).then_inc(s[f"d_ew{e}"], 16)
            sp.dma_start(seg[:, :], a["seg"]).then_inc(s["d_seg"], 16)
            sp.dma_start(segrow[:, :], a["segrow"]).then_inc(s["d_segrow"], 16)
            sp.dma_start(near[:, :, :], a["ctxT"].rearrange("p (b s) -> p b s", b=B)[:, :, 0:NEAR]).then_inc(s["d_near"], 16)
            sp.dma_start(w1n[:, :, :], a["w1n"]).then_inc(s["d_wq"], 16)
            sp.dma_start(w2n[:, :], a["w2n"]).then_inc(s["d_wq"], 16)
            sp.dma_start(cs[:, :, :], a["cs"]).then_inc(s["d_cs"], 16)
            sp.dma_start(par[:, :, :], a["par"]).then_inc(s["d_par"], 16)
            sp.dma_start(wA[:, :], a["wA"][:, 0:WATT]).then_inc(s["d_wA"], 16)
            sp.dma_start(wF[:, :], a["wF"][:, 0:WFFN]).then_inc(s["d_wF"], 16)
            with sp.Fori(0, E // RING - 1) as i:
                for k in range(RING):
                    sp.wait_ge(s["y_done"], i * RING + (k + 1))
                    sp.dma_start(ew[:, k, :], a["ew"][:, bass.ds((i + 1) * (RING * 3 * D) + k * 3 * D, 3 * D)])\
                        .then_inc(s[f"d_ew{k}"], 16)
            sp.wait_ge(s["near_known"], 1)
            short = sp.value_load(near_i[0:1, 0:1], min_val=0, max_val=1)

            def contexts(l):
                with sp.Fori(0, B) as b:
                    sp.wait_ge(s["far_step"], l * (B + 1) + b + 1)
                    sp.dma_start(gx, a["ctxT"][:, bass.ds(b * S, S)]).then_inc(s["d_gx"], 16)

            def next_weights(l, attention_done, ffn_done, n):
                sp.wait_ge(s[attention_done], (l + 1) * n)
                sp.dma_start(wA[:, :], a["wA"][:, bass.ds((l + 1) * WATT, WATT)]).then_inc(s["d_wA"], 16)
                sp.wait_ge(s[ffn_done], (l + 1) * n)
                sp.dma_start(wF[:, :], a["wF"][:, bass.ds((l + 1) * WFFN, WFFN)]).then_inc(s["d_wF"], 16)

            with sp.If(short == 1):
                with sp.Fori(0, NL - 1) as l:
                    next_weights(l, "n_woc", "n_down", 2)
            with sp.If(short == 0):
                with sp.Fori(0, NL - 1) as l:
                    contexts(l)
                    next_weights(l, "woc_done", "d_done", 1)
                contexts(NL - 1)
            sp.wait_ge(s["out_ready"], 1)
            sp.dma_start(out, yt[:, :]).then_inc(s["d_out"], 16)
            sp.wait_ge(s["d_out"], 16)


        @block.gpsimd
        def _(pool):
            own = Chain(pool, s["pool_own"])
            pool.memset(onesD[:, :], 1.0 / D).then_inc(s["consts"], 1)
            pool.memset(eps[:, 0:1], 1e-5).then_inc(s["consts"], 1)
            pool.memset(eps[:, 1:2], 1e-6).then_inc(s["consts"], 1)
            pool.memset(ones1[:, :], 1.0).then_inc(s["consts"], 1)
            pool.memset(warm[:, :], 1.0).then_inc(s["warm_ready"], 1)
            own(pool.memset(ident[:, :], 0.0))
            pool.affine_select(out=ident[:, :], in_=ident[:, :], compare_op=ALU.not_equal, fill=1.0,
                               base=0, pattern=[[-1, D]], channel_multiplier=1).then_inc(s["consts"], 1)
            pool.wait_ge(s["consts"], 5)
            pool.tensor_copy(identb[:, :], ident[:, :]).then_inc(s["consts"], 1)
            pool.memset(qpT[:, T:T + 8], 0.0).then_inc(s["consts"], 1)
            pool.memset(Kz[:, :, :, :], 0.0).then_inc(s["consts"], 1)
            own(pool.memset(VB[:, :, :, :, :, :], 0.0))
            pool.wait_ge(s["d_vec"], 16)
            for gg in range(2):
                pool.tensor_copy(VB[:, :, :, :, gg, HV:CO].rearrange("p b g j c -> p (b g j) c"),
                                 vec[0:PB, V_ROW + gg:V_ROW + gg + 1].unsqueeze(1).broadcast_to([PB, 4 * B, 1]))\
                    .then_inc(s["consts"], 1)
            own(pool.memset(fold[:, :], 0.0))
            for k in range(2):
                pool.affine_select(out=fold[:, :], in_=fold[:, :], compare_op=ALU.not_equal, fill=1.0, base=-k * L,
                                   pattern=[[-1, L]], channel_multiplier=1).then_inc(s["consts"], 1)
                pool.wait_ge(s["consts"], 11 + k)
            for u in range(UNITS):
                pool.wait_ge(s["rows_ready"], u + 1)
                pool.indirect_dma_start(out=mem[:, u, :], out_offset=None, in_=a["ctx"],
                                        in_offset=bass.IndirectOffsetOnAxis(ap=rows[:, u:u + 1], axis=0))\
                    .then_inc(s[f"g{u}"], 16)
            for u in range(UNITS):
                pool.wait_ge(s[f"g{u}"], 16)
            own(pool.memset(sel[:, :, :], 0.0))
            own(pool.memset(rb[:, :], 0.0))
            for k in range(3):
                own(pool.affine_select(out=sel[32 * k:32 * k + E, :, :], in_=sel[32 * k:32 * k + E, :, :],
                                       compare_op=ALU.not_equal, fill=1.0, base=0,
                                       pattern=[[-1, E], [0, D]], channel_multiplier=1))
            own(pool.iota(eio[:, :], pattern=[[1, E]], base=0, channel_multiplier=0))
            pool.tensor_copy(eiof[:, :], eio[:, :]).then_inc(s["consts"], 1)
            own(pool.memset(causal[:, :, :], 0.0))
            own(pool.memset(Kc[:, :, :, :], 0.0))
            own(pool.memset(Vc[:, :, :, :, :], 0.0))
            for g in range(GR):
                own(pool.memset(Vc[32 * g:32 * g + 32, :, :, g, HV:CO], 1.0))
            own(pool.iota(frow[:, :], pattern=[[1, SB]], base=0, channel_multiplier=0,
                          allow_small_or_imprecise_dtypes=True))
            own(pool.iota(krow[:, :], pattern=[[1, NEAR]], base=0, channel_multiplier=0))
            pool.tensor_copy(krowf[:, :], krow[:, :]).then_inc(s["consts"], 1)
            own(pool.memset(cz[:, :, :], 0.0))
            own(pool.affine_select(out=cz[:, 0, :], in_=cz[:, 0, :], compare_op=ALU.is_ge, fill=NEG,
                                   base=0, pattern=[[-1, L]], channel_multiplier=1))
            own(pool.affine_select(out=cz[:, 1, :], in_=cz[:, 1, :], compare_op=ALU.is_ge, fill=NEG,
                                   base=-L, pattern=[[-1, L]], channel_multiplier=1))
            own(pool.tensor_scalar(cz[:, 2, :], cz[:, 1, :], vec[0:PB, V_ROW + 1:V_ROW + 2], None, ALU.mult))
            own(pool.tensor_tensor(cz[:, 3, :], cz[:, 0, :], cz[:, 2, :], ALU.add))
            pool.tensor_copy(causal[:, :, :], cz[:, 3, :].unsqueeze(1).broadcast_to([PB, 8, L]))\
                .then_inc(s["consts"], 1)

            pool.wait_ge(s["d_near"], 16)
            pool.wait_ge(s["x_ready"], 2)
            pool.tensor_copy(near4[:, :, :, :], near[:, :, :].unsqueeze(2).broadcast_to([D, B, GR, NEAR]))\
                .then_inc(s["near_ready"], 1)

        @block.tensor
        def _(pe):
            def mm1(dst, w, x, start=True, stop=True):
                return nc.tensor.matmul(dst, w, x, start=start, stop=stop)

            def stay_warm(n):
                for _ in range(n):
                    mm1(PS[:, 5, 0:8 * L], identb[:, :], warm[:, :])

            def mean(i, src):
                mm1(PS[:, 6, 0:T], onesD[:, :], src).then_inc(s["mean_ready"], 1)

            def mean_square(i):
                stay_warm(WARM_SQ)
                pe.wait_ge(s["sq_ready"], i + 1)
                mm1(PS[:, 7, 0:T], onesD[:, :], sq[:, :]).then_inc(s["ms_ready"], 1)
                stay_warm(WARM_NORM)

            def scores(r, b, masked):
                if b >= 2:
                    pe.wait_ge(s["sub_done"], r * B + (b - 1))
                if masked:
                    mm1(PS[0:PB, b % 2, 0:8 * L], identb[0:PB, 0:PB],
                        causal[:, :, :].rearrange("p c l -> p (c l)"), stop=False)
                for jp in range(2):
                    last = mm1(PS[0:PB, b % 2, jp * GR * L:(jp + 1) * GR * L],
                               Q4[:, b, 2 * jp:2 * jp + 2, :].rearrange("p j l -> p (j l)"),
                               Kz[:, b, :, :].rearrange("p g l -> p (g l)"),
                               start=not masked, stop=not masked or jp == 1)
                last.then_inc(s["s_ready"], 1)

            def turn(r, b):
                if b == 0:
                    pe.wait_ge(s["vb_ready"], r + 1)
                pe.wait_ge(s["exp_done"], r * B + (b + 1))
                if b >= 2:
                    pe.wait_ge(s["pt_ready"], r * B + (b - 1))
                for jp in range(2):
                    for G in range(2):
                        src = P[:, b // 2 % 2, b % 2, jp * GR + 2 * G:jp * GR + 2 * G + 2, :]
                        last = nc.tensor.transpose(PS[0:PB, 2 + b % 2, (jp * 2 + G) * PB:(jp * 2 + G + 1) * PB],
                                                   src.rearrange("p g l -> p (g l)"), ident[0:PB, 0:PB])
                last.then_inc(s["turned"], 1)

            def values(r, b):
                pe.wait_ge(s["pt_ready"], r * B + (b + 1))
                if b >= 2:
                    pe.wait_ge(s["o_ready"], r * B + (b - 1))
                for G in range(2):
                    for jp in range(2):
                        at = (G * GR + jp) * CO
                        last = mm1(PS[0:PB, 4 + b % 2, at - jp * CO:at - jp * CO + 4 * CO]
                                   .rearrange("p (g j c) -> p g j c", g=2, j=2)[:, :, jp, :],
                                   PT[:, b // 2 % 2, b % 2, jp * 2 + G, :], VB[:, b, G, jp, :, :])
                last.then_inc(s["pv_done"], 1)

            def turn_back(r, b):
                pe.wait_ge(s["on_ready"], r * B + (b + 1))
                mm1(PS[:, 4 + b % 2, 300:300 + L], O[:, b // 2 % 2, b % 2, :], fold[:, :]).then_inc(s["ot_done"], 1)

            def attention_start(r, masked):
                scores(r, 0, masked)
                scores(r, 1, masked)
                turn(r, 0)
                scores(r, 2, masked)
                turn(r, 1)
                values(r, 0)
                scores(r, 3, masked)
                turn(r, 2)
                values(r, 1)
                turn_back(r, 0)
                scores(r, 4, masked)
                turn(r, 3)
                values(r, 2)
                turn_back(r, 1)
                scores(r, 5, masked)
                turn(r, 4)
                values(r, 3)
                turn_back(r, 2)
                scores(r, 6, masked)
                turn(r, 5)
                values(r, 4)
                turn_back(r, 3)
                scores(r, 7, masked)
                turn(r, 6)
                values(r, 5)
                turn_back(r, 4)

            def attention(r, masked):
                attention_start(r, masked)
                turn(r, 7)
                values(r, 6)
                turn_back(r, 5)
                values(r, 7)
                turn_back(r, 6)
                turn_back(r, 7)

            pe.wait_ge(s["consts"], 6)
            pe.wait_ge(s["warm_ready"], 1)
            pe.wait_ge(s["d_x"], 16)
            mean(0, xin[:, :])
            mean_square(0)
            pe.wait_ge(s["norm_ready"], 1)
            pe.wait_ge(s["d_wa0"], 16)
            mm1(PS[:, 2, 0:T], wa0[:, 0:D], xh[:, :]).then_inc(s["qp_done"], 1)
            for u in range(UNITS):
                if u == 0:
                    pe.wait_ge(s["consts"], 7)
                    pe.wait_ge(s["qp_copied"], 1)
                pe.wait_ge(s[f"d_ctx{u}"], 16)
                if u >= 2:
                    pe.wait_ge(s["rows_ready"], u - 1)
                for c in range(3):
                    n = min(512, S - c * 512)
                    for k in range(2):
                        b = 2 * u + k
                        last = mm1(PS[64 * k:64 * k + 64, 3 * (u % 2) + c, 0:n], qpT[:, b * L:b * L + 64],
                                   ctxT[:, b * S + c * 512:b * S + c * 512 + n])
                last.then_inc(s["cand_scores"], 1)
            for u in range(UNITS):
                pe.wait_ge(s[f"g{u}"], 16)
                last = nc.tensor.transpose(PS[:, 6, u * D:(u + 1) * D], mem[:, u, :], ident[:, :])
            last.then_inc(s["mem_turned"], 1)
            pe.wait_ge(s["memT_ready"], 1)
            mm1(PS[:, 7, 0:T], wa0[:, D:2 * D], memD[:, :, 0, :]).then_inc(s["kv_done"], 1)
            pe.wait_ge(s["rows_ready"], UNITS)
            for b in range(B):
                last = mm1(PS[0:PB, 2 + b // 4, (b % 4) * D:(b % 4 + 1) * D], memD[:, b, :, :].rearrange("p k l -> p (k l)"),
                           wa0[:, 2 * D:3 * D])
            last.then_inc(s["kv_done"], 1)
            pe.wait_ge(s["q4_ready"], 1)
            pe.wait_ge(s["kz_ready"], 1)
            attention(0, False)
            pe.wait_ge(s["o_ready"], B)
            mm1(PS[:, 0, 0:T], wa0[:, 3 * D:4 * D], o[:, :]).then_inc(s["wo_done"], 1)

            pe.wait_ge(s["x_ready"], 1)
            mean(1, x1[:, :])
            mean_square(1)
            mean_square(2)
            pe.wait_ge(s["norm_ready"], 3)
            pe.wait_ge(s["d_gw"], 32)
            for u in range(UNITS):
                last = mm1(PS[0:PB, 0, u * E:(u + 1) * E], h[:, u * PB:(u + 1) * PB], gw[:, :])
            last.then_inc(s["gate_done"], 1)
            pe.wait_ge(s["route_ready"], 1)
            for u in range(UNITS):
                last = nc.tensor.transpose(PS[0:E, 1, u * PB:(u + 1) * PB], ge[:, u, :], ident[0:PB, 0:PB])
            last.then_inc(s["route_turned"], 1)
            pe.wait_ge(s["rb_ready"], 1)
            pe.wait_ge(s["d_b2e"], 16)
            mm1(PS[:, 6, 0:T], b2e[:, :], routeT[:, :], stop=False)

            def expert_up(e, k, i, first):
                bank = 3 * (k % 2)
                pe.wait_ge(s[f"d_ew{k % RING}"], (i + 1) * 16)
                if not first or k >= 2:
                    pe.wait_ge(s["ww_ready"], e - 1)
                mm1(PS[:, bank, 0:T], ew[:, k % RING, 0:D], h[:, :])
                mm1(PS[:, bank + 1, 0:T], ew[:, k % RING, D:2 * D], h[:, :])
                mm1(PS[:, bank + 2, 0:T], sel[:, bass.ds(e, 1), :].rearrange("p e d -> p (e d)"), rb[:, :])\
                    .then_inc(s["e_glr"], 1)

            def expert_down(e, k, stop=False):
                pe.wait_ge(s["zz_ready"], e + 1)
                mm1(PS[:, 6, 0:T], ew[:, k, 2 * D:3 * D], zz[:, k % 2, :], start=False, stop=stop)\
                    .then_inc(s["y_done"], 1)

            expert_up(0, 0, 0, True)
            for k in range(RING):
                if k + 1 < RING:
                    expert_up(k + 1, k + 1, 0, True)
                else:
                    expert_up(RING, 0, 1, False)
                expert_down(k, k)
            with pe.Fori(1, E // RING - 1) as i:
                for k in range(RING):
                    if k + 1 < RING:
                        expert_up(i * RING + (k + 1), k + 1, i, False)
                    else:
                        expert_up(i * RING + RING, 0, i + 1, False)
                    expert_down(i * RING + k, k)
            for k in range(RING):
                e = E - RING + k
                if k + 1 < RING:
                    expert_up(e + 1, k + 1, E // RING - 1, False)
                expert_down(e, k, stop=e == E - 1)

            pe.wait_ge(s["x_ready"], 2)
            mean(2, x2[:, :])
            mean_square(3)
            pe.wait_ge(s["consts"], 15)
            pe.wait_ge(s["near_ready"], 1)
            pe.wait_ge(s["xbias_ready"], 1)
            pe.wait_ge(s["near_known"], 1)
            short = pe.value_load(near_i[0:1, 0:1], min_val=0, max_val=1)

            def cross_long(l):
                with pe.Fori(0, B) as b:
                    pe.wait_ge(s["far_step"], l * (B + 1) + b + 1)
                    lb = l * B + b
                    pe.wait_ge(s["d_gx"], (lb + 1) * 16)
                    for c in range(3):
                        mm1(PS[:, c, 0:SB], wA[:, WKC:WKC + D], gx[:, c * SB:(c + 1) * SB])
                        last = mm1(PS[:, 3 + c, 0:SB], wA[:, WVC:WVC + D], gx[:, c * SB:(c + 1) * SB])
                    last.then_inc(s["far_kv"], 1)
                    pe.wait_ge(s["gv_ready"], lb + 1)
                    for c in range(NK):
                        last = nc.tensor.transpose(PS[0:KC, 3 + c // 4, (c % 4) * D:(c % 4 + 1) * D],
                                                   gv[:, c * KC:(c + 1) * KC], ident[:, :])
                    last.then_inc(s["far_vt"], 1)
                    with pe.Fori(0, H) as hh_:
                        t = lb * H + hh_
                        pe.wait_ge(s["gq_ready"], t + 1)
                        for c in range(3):
                            last = mm1(PS[0:L, c, 0:SB], gqz, gk[:, c * SB:(c + 1) * SB])
                        last.then_inc(s["fs_ready"], 1)
                        pe.wait_ge(s["fe_ready"], t + 1)
                        for c in range(NK):
                            last = mm1(PS[0:KC, 6 + c // 8, (c % 8) * 64:(c % 8) * 64 + L],
                                       gp[:, c * KC:(c + 1) * KC], ident[0:L, 0:L])
                        last.then_inc(s["ft_ready"], 1)
                        pe.wait_ge(s["gV_ready"], lb + 1)
                        pe.wait_ge(s["fpt_ready"], t + 1)
                        for c in range(NK):
                            last = mm1(PS[0:L, 3, 0:DH], gPT[:, c, :], gV[:, c, bass.ds(hh_ * DH, DH)],
                                       start=c == 0, stop=c == NK - 1)
                        last.then_inc(s["fo_ready"], 1)
                    pe.wait_ge(s["fO_ready"], lb + 1)
                    mm1(PS[:, 4, 0:L], gOc, ident[0:L, 0:L]).then_inc(s["ff_ready"], 1)

            def half_product(bank, w, src, hf, ready):
                mm1(PS[:, bank, hf * HT:(hf + 1) * HT], w, src[:, hf * HT:(hf + 1) * HT]).then_inc(s[ready], 1)

            def half_mean_square(n, hf):
                pe.wait_ge(s["n_sq"], n + 1)
                if hf == 1:
                    pe.wait_ge(s["n_ln"], n)
                half_product(7, onesD[:, :], sq, hf, "n_ms")

            def near_scores(l, u):
                if u % 2 == 0:
                    pe.wait_ge(s["n_q4c"], l * 2 + (u // 2 + 1))
                if u >= 2:
                    pe.wait_ge(s["csub_done"], l * UNITS + (u - 1))
                mm1(PS[0:PB, u % 2, :], identb[0:PB, 0:PB],
                    xbias[:, 2 * u:2 * u + 2, :].unsqueeze(2).broadcast_to([PB, 2, 2, GR * NEAR]), stop=False)
                for k in range(2):
                    for jp in range(2):
                        b, col = 2 * u + k, (2 * k + jp) * GR * NEAR
                        last = mm1(PS[0:PB, u % 2, col:col + GR * NEAR],
                                   Q4c[:, b, 2 * jp:2 * jp + 2, :].rearrange("p j l -> p (j l)"),
                                   Kc[:, b, :, :].rearrange("p g k -> p (g k)"),
                                   start=False, stop=k + jp == 2)
                last.then_inc(s["cs_ready"], 1)

            def near_turn(l, u):
                pe.wait_ge(s["cexp_done"], l * UNITS + (u + 1))
                if u >= 2:
                    pe.wait_ge(s["cpt_ready"], l * UNITS + (u - 1))
                for c in range(4):
                    last = nc.tensor.transpose(PS[:, 2 + u % 2, c * PB:(c + 1) * PB],
                                               Pc[:, u, GR * c:GR * c + GR, :].rearrange("p g k -> p (g k)"),
                                               ident[0:PB, 0:PB])
                last.then_inc(s["cturned"], 1)

            def near_values(l, u):
                pe.wait_ge(s["cpt_ready"], l * UNITS + (u + 1))
                if u >= 2:
                    pe.wait_ge(s["near_out"], l * UNITS + (u - 1))
                for k in range(2):
                    for jp in range(2):
                        at = k * 2 * GR * CO
                        last = mm1(PS[0:PB, 4 + u % 2, at:at + 8 * CO]
                                   .rearrange("p (g j c) -> p g j c", g=GR, j=2)[:, :, jp, :],
                                   PTc[:, u, 2 * k + jp, :], Vc[:, 2 * u + k, jp, :, :])
                last.then_inc(s["cpv_done"], 1)

            def near_turn_back(l, u):
                pe.wait_ge(s["con_ready"], l * UNITS + (u + 1))
                for k in range(2):
                    last = mm1(PS[:, 4 + u % 2, 300 + k * L:300 + (k + 1) * L], O[:, u % 2, k, :], fold[:, :])
                last.then_inc(s["cot_done"], 1)

            def ffn_up(l, i):
                hf, c = i // FC, i % FC
                if c == 0:
                    pe.wait_ge(s["n_h"], l * 6 + (5 + hf))
                if i >= 2:
                    pe.wait_ge(s["n_m"], l * 2 * FC + (i - 1))
                x = h[:, hf * HT:(hf + 1) * HT]
                mm1(PS[:, i % 2, 0:HT], wF[:, WG + c * D:WG + (c + 1) * D], x)
                mm1(PS[:, 2 + i % 2, 0:HT], wF[:, WU + c * D:WU + (c + 1) * D], x).then_inc(s["n_up"], 1)

            def ffn_down(l, i):
                hf, c = i // FC, i % FC
                pe.wait_ge(s["n_m"], l * 2 * FC + (i + 1))
                last = mm1(PS[:, 4 + hf, hf * HT:(hf + 1) * HT], wF[:, WD + c * D:WD + (c + 1) * D],
                           mm[:, c, hf * HT:(hf + 1) * HT], start=c == 0, stop=c == FC - 1)
                if c == FC - 1:
                    last.then_inc(s["n_down"], 1)

            with pe.If(short == 1):
                half_mean_square(0, 0)
                with pe.Fori(0, NL) as l:
                    pe.wait_ge(s["d_wA"], (l + 1) * 16)
                    mm1(PS[:, 2, 0:B * NEAR], wA[:, WKC:WKC + D], near[:, :, :].rearrange("p b k -> p (b k)"))
                    for b in range(B):
                        mm1(PS[:, b // 4, (b % 4) * D:(b % 4 + 1) * D],
                            near4[:, b, :, :].rearrange("p g k -> p (g k)"), wA[:, WVC:WVC + D])
                    pe.wait_ge(s["pl_ready"], l + 1)
                    mm1(PS[:, 3, 0:1], wA[:, WO:WO + D], pl[:, BV:BV + 1]).then_inc(s["ckv_done"], 1)
                    half_mean_square(l * 6 + 1, 1)
                    for hf in range(2):
                        pe.wait_ge(s["n_h"], l * 6 + (hf + 1))
                        for i, pair in enumerate(((WQ, WQR), (WK, WKR))):
                            for j, w in enumerate(pair):
                                last = mm1(PS[:, 4 + 2 * hf + i, j * HT:(j + 1) * HT], wA[:, w:w + D],
                                           h[:, hf * HT:(hf + 1) * HT])
                            last.then_inc(s["n_proj"], 1)
                    pe.wait_ge(s["ckv_ready"], l + 1)
                    pe.wait_ge(s["bo_ready"], l + 1)
                    pe.wait_ge(s["n_hd"], l + 1)
                    for b in range(B):
                        last = mm1(PS[0:PB, 2 + b // 4, (b % 4) * D:(b % 4 + 1) * D],
                                   hd[:, b, :, :].rearrange("p k l -> p (k l)"), wA[:, WV:WV + D])
                    last.then_inc(s["proj_done"], 1)
                    pe.wait_ge(s["q4_ready"], l + 2)
                    pe.wait_ge(s["kz_ready"], l + 2)
                    r = l + 1
                    attention_start(r, True)
                    half_product(6, wA[:, WO:WO + D], o, 0, "n_wo")
                    turn(r, 7)
                    values(r, 6)
                    turn_back(r, 5)
                    half_mean_square(l * 6 + 2, 0)
                    values(r, 7)
                    turn_back(r, 6)
                    pe.wait_ge(s["n_h"], l * 6 + 3)
                    half_product(7, wA[:, WQC:WQC + D], h, 0, "n_qc")
                    turn_back(r, 7)
                    pe.wait_ge(s["o_ready"], r * B + B)
                    half_product(6, wA[:, WO:WO + D], o, 1, "n_wo")
                    near_scores(l, 0)
                    near_scores(l, 1)
                    half_mean_square(l * 6 + 3, 1)
                    near_turn(l, 0)
                    pe.wait_ge(s["n_h"], l * 6 + 4)
                    half_product(7, wA[:, WQC:WQC + D], h, 1, "n_qc")
                    near_turn(l, 1)
                    near_values(l, 0)
                    near_scores(l, 2)
                    near_values(l, 1)
                    near_turn_back(l, 0)
                    near_scores(l, 3)
                    near_turn(l, 2)
                    near_turn_back(l, 1)
                    pe.wait_ge(s["near_out"], l * UNITS + 2)
                    half_product(6, wA[:, WOC:WOC + D], o, 0, "n_woc")
                    near_turn(l, 3)
                    near_values(l, 2)
                    half_mean_square(l * 6 + 4, 0)
                    near_values(l, 3)
                    near_turn_back(l, 2)
                    near_turn_back(l, 3)
                    pe.wait_ge(s["near_out"], l * UNITS + 4)
                    half_product(6, wA[:, WOC:WOC + D], o, 1, "n_woc")
                    pe.wait_ge(s["d_wF"], (l + 1) * 16)
                    ffn_up(l, 0)
                    half_mean_square(l * 6 + 5, 1)
                    ffn_up(l, 1)
                    for i in range(2, 2 * FC):
                        ffn_down(l, i - 2)
                        ffn_up(l, i)
                    half_mean_square(l * 6 + 6, 0)
                    ffn_down(l, 6)
                    ffn_down(l, 7)

            with pe.If(short == 0):
                with pe.Fori(0, NL) as l:
                    mean_square(l * 3 + 4)
                    pe.wait_ge(s["norm_ready"], l * 3 + 5)
                    pe.wait_ge(s["d_wA"], (l + 1) * 16)
                    for i, w in enumerate((WQ, WQR, WK, WKR)):
                        mm1(PS[:, 4 + i, 0:T], wA[:, w:w + D], h[:, :]).then_inc(s["n_proj"], 1)
                    pe.wait_ge(s["n_hd"], l + 1)
                    for b in range(B):
                        last = mm1(PS[0:PB, 2 + b // 4, (b % 4) * D:(b % 4 + 1) * D],
                                   hd[:, b, :, :].rearrange("p k l -> p (k l)"), wA[:, WV:WV + D])
                    last.then_inc(s["proj_done"], 1)
                    pe.wait_ge(s["pl_ready"], l + 1)
                    mm1(PS[:, 1, 0:1], wA[:, WO:WO + D], pl[:, BV:BV + 1]).then_inc(s["ckv_done"], 1)
                    pe.wait_ge(s["bo_ready"], l + 1)
                    pe.wait_ge(s["q4_ready"], l + 2)
                    pe.wait_ge(s["kz_ready"], l + 2)
                    attention(l + 1, True)
                    pe.wait_ge(s["o_ready"], (l + 1) * B + B)
                    mm1(PS[:, 0, 0:T], wA[:, WO:WO + D], o[:, :]).then_inc(s["wo_done"], 1)
                    mean_square(l * 3 + 5)
                    pe.wait_ge(s["norm_ready"], l * 3 + 6)
                    mm1(PS[:, 1, 0:T], wA[:, WQC:WQC + D], h[:, :]).then_inc(s["qc_done"], 1)
                    cross_long(l)
                    pe.wait_ge(s["oc_ready"], l + 1)
                    mm1(PS[:, 0, 0:T], wA[:, WOC:WOC + D], o[:, :]).then_inc(s["woc_done"], 1)
                    mean_square(l * 3 + 6)
                    pe.wait_ge(s["norm_ready"], l * 3 + 7)
                    pe.wait_ge(s["d_wF"], (l + 1) * 16)
                    for c in range(FC):
                        if c >= 2:
                            pe.wait_ge(s["m_ready"], l * FC + (c - 1))
                        mm1(PS[:, 2 * (c % 2), 0:T], wF[:, WG + c * D:WG + (c + 1) * D], h[:, :])\
                            .then_inc(s["g_done"], 1)
                        mm1(PS[:, 2 * (c % 2) + 1, 0:T], wF[:, WU + c * D:WU + (c + 1) * D], h[:, :])\
                            .then_inc(s["u_done"], 1)
                    for c in range(FC):
                        pe.wait_ge(s["m_ready"], l * FC + (c + 1))
                        last = mm1(PS[:, 4, 0:T], wF[:, WD + c * D:WD + (c + 1) * D], mm[:, c, :],
                                   start=c == 0, stop=c == FC - 1)
                    last.then_inc(s["d_done"], 1)
            pe.wait_ge(s["sq_last"], 1)
            mm1(PS[:, 7, 0:T], onesD[:, :], sq[:, :]).then_inc(s["ms_last"], 1)

            pe.wait_ge(s["wq_ready"], 1)
            for c in range(FC):
                nc.tensor.transpose(PS[:, 0, c * 64:(c + 1) * 64].bitcast(BF16), wqb[:, 0, c * D:(c + 1) * D],
                                    identb[:, :])
            for c in range(FC):
                last = nc.tensor.transpose(PS[:, 1, c * 64:(c + 1) * 64].bitcast(BF16),
                                           wqb[:, 1, c * D:(c + 1) * D], identb[:, :])
            last.then_inc(s["wq_turned"], 1)

            pe.wait_ge(s["layers_done"], 2)
            mean(3, x3[:, :])
            pe.wait_ge(s["sq_last"], 2)
            mm1(PS[:, 7, 0:T], onesD[:, :], sq[:, :]).then_inc(s["ms_last"], 1)

            def largest(i):
                pe.wait_ge(s["max_in"], i + 1)
                nc.tensor.transpose(PS[0:1, 5, 0:D], s11[:, 0:1], ident[:, :]).then_inc(s["max_turned"], 1)
                pe.wait_ge(s["s_one"], i + 1)
                mm1(PS[:, 4, 0:1], ones1[:, :], s11[0:1, 2:3]).then_inc(s["s_bcast"], 1)

            largest(0)
            pe.wait_ge(s["yq_ready"], 1)
            pe.wait_ge(s["wqT_ready"], 1)
            for c in range(FC):
                mm1(PS[:, c, 0:T], w1qT[:, c * D:(c + 1) * D], yq[:, :]).then_inc(s["up_done"], 1)
            largest(1)
            pe.wait_ge(s["hq_ready"], 1)
            for c in range(FC):
                last = mm1(PS[:, 6, 0:T], w2qT[:, c, :], hq[:, c, :], start=c == 0, stop=c == FC - 1)
            last.then_inc(s["down_done"], 1)

        @block.scalar
        def _(act):
            def fn(dst, src, f, **kw):
                return nc.scalar.activation(dst, src, f, **kw)

            def norm(i, src, e):
                fn(sq[:, :], src, ACT.Square).then_inc(s["sq_ready"], 1)
                act.wait_ge(s["ms_ready"], i + 1)
                fn(rs[:, :], PS[:, 7, 0:T], ACT.Ln, bias=eps[:, e:e + 1]).then_inc(s["ln_done"], 1)
                act.wait_ge(s["ln_done"], i + 1)
                fn(rs[:, :], rs[:, :], ACT.Exp, scale=-0.5).then_inc(s["rstd_ready"], 1)

            def values_out(r):
                v = PS[0:PB, 2:4, :].rearrange("p k (b c) -> p (k b) c", c=D)
                for gg in range(2):
                    last = fn(VB[:, :, :, :, gg, 0:HV].rearrange("p b g j c -> p (b g) j c"),
                              v.rearrange("p b (g h c) -> p (b g) h c", g=2, h=4)[:, :, 2 * gg:2 * gg + 2, :],
                              ACT.Copy, scale=vec[0:PB, V_ROW + gg:V_ROW + gg + 1])
                last.then_inc(s["vb_ready"], 1)

            def keys_out(src):
                for g in range(GR):
                    last = fn(Kz[32 * g:32 * g + 32, :, g, :], heads3(src[32 * g:32 * g + 32]), ACT.Copy)
                last.then_inc(s["kz_ready"], 1)

            def exps(r, b):
                act.wait_ge(s["sub_done"], r * B + (b + 1))
                v = P[:, b // 2 % 2, b % 2, :, :].rearrange("p c l -> p (c l)")
                fn(v, v, ACT.Exp, scale=SCALE).then_inc(s["exp_done"], 1)

            def evac(r, b):
                act.wait_ge(s["turned"], r * B + (b + 1))
                if b >= 4:
                    act.wait_ge(s["pv_done"], r * B + (b - 3))
                fn(PT[:, b // 2 % 2, b % 2, :, :].rearrange("p c q -> p (c q)"), PS[0:PB, 2 + b % 2, 0:4 * PB],
                   ACT.Copy).then_inc(s["pt_ready"], 1)

            def out_part(r, b):
                act.wait_ge(s["ot_done"], r * B + (b + 1))
                fn(o[:, b * L:(b + 1) * L], PS[:, 4 + b % 2, 300:300 + L], ACT.Copy).then_inc(s["o_ready"], 1)

            def attention_start(r):
                exps(r, 0)
                exps(r, 1)
                evac(r, 0)
                exps(r, 2)
                evac(r, 1)
                exps(r, 3)
                evac(r, 2)
                out_part(r, 0)
                exps(r, 4)
                evac(r, 3)
                out_part(r, 1)
                exps(r, 5)
                evac(r, 4)
                out_part(r, 2)
                exps(r, 6)
                evac(r, 5)
                out_part(r, 3)
                exps(r, 7)
                evac(r, 6)

            def attention(r):
                attention_start(r)
                out_part(r, 4)
                evac(r, 7)
                out_part(r, 5)
                out_part(r, 6)
                out_part(r, 7)

            act.preload_act_table_set("natural_log_exp_and_others")
            act.wait_ge(s["consts"], 6)
            act.wait_ge(s["xc_ready"], 1)
            norm(0, xc[:, :], 0)
            act.wait_ge(s["qp_done"], 1)
            fn(qpT[:, 0:T], PS[:, 2, 0:T], ACT.Copy).then_inc(s["qp_copied"], 1)
            act.wait_ge(s["mem_turned"], 1)
            fn(memD[:, :, :, :], PS[:, 6, :].rearrange("p (b l) -> p b l", b=B)[:, :, 0:L].unsqueeze(2)
               .broadcast_to([D, B, 2, L]), ACT.Copy).then_inc(s["memT_ready"], 1)
            act.wait_ge(s["consts"], 12)
            act.wait_ge(s["d_vec"], 16)
            act.wait_ge(s["kv_done"], 1)
            keys_out(PS[:, 7, 0:T])
            act.wait_ge(s["kv_done"], 2)
            values_out(0)
            attention(0)
            act.wait_ge(s["xc_ready"], 2)
            norm(1, xc[:, :], 0)
            act.wait_ge(s["norm_ready"], 2)
            norm(2, xh[:, :], 0)
            act.wait_ge(s["gexp_in"], 1)
            fn(ge[:, :, :], ge[:, :, :], ACT.Exp).then_inc(s["gexp_done"], 1)

            def expert(e, k, first):
                bank = 3 * (k % 2)
                act.wait_ge(s["e_glr"], e + 1)
                if not first or k >= 2:
                    act.wait_ge(s["zz_ready"], e - 1)
                fn(l1[:, k % 2, :], PS[:, bank + 1, 0:T], ACT.Identity,
                   bias=vec[:, bass.ds(e + V_B1L, 1)]).then_inc(s["l1_ready"], 1)
                act.wait_ge(s["xg_ready"], e + 1)
                fn(sg[:, k % 2, :], xg[:, k % 2, :], ACT.Sigmoid, scale=ALPHA).then_inc(s["sg_ready"], 1)

            for k in range(RING):
                expert(k, k, True)
            with act.Fori(1, E // RING) as i:
                for k in range(RING):
                    expert(i * RING + k, k, False)
            act.preload_act_table_set("natural_log_exp_and_others")
            act.wait_ge(s["xc_ready"], 3)
            norm(3, xc[:, :], 0)
            act.wait_ge(s["near_known"], 1)
            short = act.value_load(near_i[0:1, 0:1], min_val=0, max_val=1)

            def near_exps(l, u):
                act.wait_ge(s["csub_done"], l * UNITS + (u + 1))
                v = Pc[:, u, :, :].rearrange("p c k -> p (c k)")
                fn(v, v, ACT.Exp, scale=SCALE).then_inc(s["cexp_done"], 1)

            def near_evac(l, u):
                act.wait_ge(s["cturned"], l * UNITS + (u + 1))
                fn(PTc[:, u, :, :].rearrange("p c q -> p (c q)"), PS[:, 2 + u % 2, 0:4 * PB],
                   ACT.Copy).then_inc(s["cpt_ready"], 1)

            def near_out(l, u):
                act.wait_ge(s["cot_done"], l * UNITS + (u + 1))
                fn(o[:, 2 * u * L:2 * (u + 1) * L], PS[:, 4 + u % 2, 300:300 + 2 * L], ACT.Copy)\
                    .then_inc(s["near_out"], 1)

            def half_squares(x, n, hf):
                act.wait_ge(s["n_x"], x)
                fn(sq[:, hf * HT:(hf + 1) * HT], xl[:, hf * HT:(hf + 1) * HT], ACT.Square).then_inc(s["n_sq"], 1)

            def half_rstd(n, hf):
                act.wait_ge(s["n_ms"], n + 1)
                c = slice(hf * HT, (hf + 1) * HT)
                fn(rs[:, c], PS[:, 7, c], ACT.Ln, bias=eps[:, 1:2]).then_inc(s["n_ln"], 1)
                act.wait_ge(s["n_ln"], n + 1)
                fn(rs[:, c], rs[:, c], ACT.Exp, scale=-0.5).then_inc(s["n_rs"], 1)

            def doubled(hf):
                return fn(hd[:, hf * HB:(hf + 1) * HB, :, :],
                          heads3(h[:, :])[:, hf * HB:(hf + 1) * HB, :].unsqueeze(2).broadcast_to([D, HB, 2, L]),
                          ACT.Copy)

            def cross_long(l):
                with act.Fori(0, B) as b:
                    lb = l * B + b
                    act.wait_ge(s["far_kv"], lb + 1)
                    fn(gv.rearrange("p (c n) -> p c n", c=3), PS[:, 3:6, 0:SB], ACT.Copy).then_inc(s["gv_ready"], 1)
                    act.wait_ge(s["far_vt"], lb + 1)
                    fn(gV.rearrange("p c d -> p (c d)"), PS[0:KC, 3:6, :].rearrange("p k c -> p (k c)"), ACT.Copy)\
                        .then_inc(s["gV_ready"], 1)
                    with act.Fori(0, H) as hh_:
                        t = lb * H + hh_
                        act.wait_ge(s["fm_ready"], t + 1)
                        fn(gp, gp, ACT.Exp, scale=SCALE, accum_out=fmx[:, 2:3])\
                            .then_inc(s["fe_ready"], 1)
                        act.wait_ge(s["ft_ready"], t + 1)
                        fn(gPT, PS[0:KC, 6:8, :].rearrange("p k (c n) -> p (k c) n", n=64)[:, 0:NK, 0:L], ACT.Copy)\
                            .then_inc(s["fpt_ready"], 1)

            with act.If(short == 1):
                act.wait_ge(s["near_ready"], 1)
                half_squares(1, 0, 0)
                with act.Fori(0, NL) as l:
                    act.preload_act_table_set("natural_log_exp_and_others")
                    half_rstd(l * 6, 0)
                    half_squares(l * 6 + 1, l * 6 + 1, 1)
                    act.wait_ge(s["ckv_done"], l + 1)
                    for g in range(GR):
                        fn(Kc[32 * g:32 * g + 32, :, g, :],
                           PS[32 * g:32 * g + 32, 2, 0:B * NEAR].rearrange("p (b k) -> p b k", b=B), ACT.Copy)
                    half_rstd(l * 6 + 1, 1)
                    v = PS[:, 0:2, :].rearrange("p k (b c) -> p (k b) c", c=D)
                    for g in range(GR):
                        last = fn(Vc[32 * g:32 * g + 32, :, :, g, 0:HV],
                                  v[32 * g:32 * g + 32, :, 32 * g:32 * g + 32].rearrange("p b (j c) -> p b j c", j=2),
                                  ACT.Copy)
                    last.then_inc(s["ckv_ready"], 1)
                    act.wait_ge(s["n_h"], l * 6 + 1)
                    doubled(0)
                    act.wait_ge(s["n_h"], l * 6 + 2)
                    doubled(1).then_inc(s["n_hd"], 1)
                    act.wait_ge(s["proj_done"], l + 1)
                    values_out(l + 1)
                    for hf in range(2):
                        act.wait_ge(s["n_k"], l * 2 + (hf + 1))
                        for g in range(GR):
                            q = slice(32 * g, 32 * g + 32)
                            last = fn(Kz[q, hf * HB:(hf + 1) * HB, g, :],
                                      heads3(qk[:, 1, :])[q, hf * HB:(hf + 1) * HB, :], ACT.Copy)
                    last.then_inc(s["kz_ready"], 1)
                    r = l + 1
                    attention_start(r)
                    half_squares(l * 6 + 2, l * 6 + 2, 0)
                    out_part(r, 4)
                    evac(r, 7)
                    out_part(r, 5)
                    half_rstd(l * 6 + 2, 0)
                    out_part(r, 6)
                    out_part(r, 7)
                    half_squares(l * 6 + 3, l * 6 + 3, 1)
                    near_exps(l, 0)
                    half_rstd(l * 6 + 3, 1)
                    near_exps(l, 1)
                    near_evac(l, 0)
                    near_evac(l, 1)
                    near_exps(l, 2)
                    near_out(l, 0)
                    near_exps(l, 3)
                    near_evac(l, 2)
                    near_out(l, 1)
                    half_squares(l * 6 + 4, l * 6 + 4, 0)
                    near_evac(l, 3)
                    half_rstd(l * 6 + 4, 0)
                    near_out(l, 2)
                    near_out(l, 3)
                    half_squares(l * 6 + 5, l * 6 + 5, 1)
                    half_rstd(l * 6 + 5, 1)
                    for i in range(2 * FC):
                        hf, c = i // FC, i % FC
                        act.wait_ge(s["n_up"], l * 2 * FC + (i + 1))
                        fn(sl[:, c, hf * HT:(hf + 1) * HT], PS[:, i % 2, 0:HT], ACT.Silu).then_inc(s["n_silu"], 1)
                        if i == 2 * FC - 2:
                            half_squares(l * 6 + 6, l * 6 + 6, 0)
                act.wait_ge(s["n_ms"], 6 * NL + 1)
            with act.If(short == 0):
                with act.Fori(0, NL) as l:
                    act.preload_act_table_set("natural_log_exp_and_others")
                    act.wait_ge(s["norm_ready"], l * 3 + 4)
                    act.wait_ge(s["x_ready"], l * 3 + 2)
                    norm(l * 3 + 4, xl[:, :], 1)
                    act.wait_ge(s["norm_ready"], l * 3 + 5)
                    doubled(0)
                    doubled(1).then_inc(s["n_hd"], 1)
                    act.wait_ge(s["proj_done"], l + 1)
                    values_out(l + 1)
                    act.wait_ge(s["k_ready"], l + 1)
                    keys_out(qk[:, 1, :])
                    attention(l + 1)
                    act.wait_ge(s["x_ready"], l * 3 + 3)
                    norm(l * 3 + 5, xl[:, :], 1)
                    cross_long(l)
                    act.wait_ge(s["x_ready"], l * 3 + 4)
                    norm(l * 3 + 6, xl[:, :], 1)
                    for c in range(FC):
                        act.wait_ge(s["g_done"], l * FC + (c + 1))
                        fn(sl[:, c, :], PS[:, 2 * (c % 2), 0:T], ACT.Silu).then_inc(s["silu_done"], 1)
                act.wait_ge(s["ms_ready"], 4 + 3 * NL)

            def last_norm(i, src, e):
                fn(sq[:, :], src, ACT.Square).then_inc(s["sq_last"], 1)
                act.wait_ge(s["ms_last"], i + 1)
                fn(rs[:, :], PS[:, 7, 0:T], ACT.Ln, bias=eps[:, e:e + 1]).then_inc(s["ln_last"], 1)
                act.wait_ge(s["ln_last"], i + 1)
                fn(rs[:, :], rs[:, :], ACT.Exp, scale=-0.5).then_inc(s["rs_last"], 1)

            act.preload_act_table_set("natural_log_exp_and_others")
            act.wait_ge(s["layers_done"], 1)
            last_norm(0, xl[:, :], 1)
            act.wait_ge(s["xc_ready"], 4)
            last_norm(1, xc[:, :], 0)
            for c in range(FC):
                act.wait_ge(s["up_done"], c + 1)
                fn(hh[:, c, :], PS[:, c, 0:T], ACT.Relu, bias=bq[:, c:c + 1], scale=ss[:, c:c + 1])\
                    .then_inc(s["relu_done"], 1)
            act.wait_ge(s["down_done"], 1)
            fn(yt[:, :], PS[:, 6, 0:T], ACT.Identity, bias=bq[:, 4:5], scale=ss[:, 4:5]).then_inc(s["out_scaled"], 1)

        @block.vector
        def _(dve):
            v_ = nc.vector

            def layer_norm(i, k, src, dst, rstd="rstd_ready", ready="norm_ready"):
                dve.wait_ge(s["mean_ready"], i + 1)
                v_.tensor_tensor(xc[:, :], src, PS[:, 6, 0:T], ALU.subtract).then_inc(s["xc_ready"], 1)
                dve.wait_ge(s["xc_ready"], i + 1)
                dve.wait_ge(s[rstd], k + 1)
                v_.tensor_tensor(dst, xc[:, :], rs[:, :], ALU.mult).then_inc(s[ready], 1)

            def rms_norm(k, src, w, dst):
                dve.wait_ge(s["rstd_ready"], k + 1)
                v_.scalar_tensor_tensor(dst, src, w, rs[:, :], ALU.mult, ALU.mult).then_inc(s["norm_ready"], 1)

            def queries_out(dst, src, ready):
                for j in range(HG):
                    last = v_.tensor_scalar(dst[:, :, j, :], heads3(src), colv(V_SEL + j), None, ALU.mult)
                last.then_inc(s[ready], 1)

            def normalise(v, nh, w, r, dst, own):
                v = v.rearrange("p (c x) -> p c x", x=CO)
                own(v_.reciprocal(r.unsqueeze(2), v[:, :, HV:CO]))
                own(v_.tensor_tensor(w, r.unsqueeze(2).broadcast_to([PB, nh, 2]),
                                     vec[0:PB, V_ROW:V_ROW + 2].unsqueeze(1).broadcast_to([PB, nh, 2]), ALU.mult))
                return v_.tensor_tensor(dst, v[:, :, 0:HV].rearrange("p c (j d) -> p c j d", j=2),
                                        w.unsqueeze(3).broadcast_to([PB, nh, 2, DH]), ALU.mult)

            def softmax(r, b, own):
                dve.wait_ge(s["s_ready"], r * B + (b + 1))
                src = PS[0:PB, b % 2, 0:8 * L].rearrange("p (c l) -> p c l", l=L)
                m = mxs[:, b // 2 % 2, 8 * (b % 2):8 * (b % 2) + 8]
                own(v_.tensor_reduce(m, src, AX.X, ALU.max))
                if b >= 4:
                    dve.wait_ge(s["turned"], r * B + (b - 3))
                v_.tensor_tensor(P[:, b // 2 % 2, b % 2, :, :], src, m.unsqueeze(2).broadcast_to([PB, 8, L]),
                                 ALU.subtract).then_inc(s["sub_done"], 1)

            def out_norm(r, b, own):
                dve.wait_ge(s["pv_done"], r * B + (b + 1))
                if b >= 4:
                    dve.wait_ge(s["ot_done"], r * B + (b - 3))
                u, k = b // 2 % 2, b % 2
                normalise(PS[0:PB, 4 + b % 2, 0:8 * CO], 8, wgt[:, u, 8 * k:8 * k + 8, :], rcp[:, u, 8 * k:8 * k + 8],
                          O[:, u, k, :].rearrange("p (c j d) -> p c j d", j=2, d=DH), own).then_inc(s["on_ready"], 1)

            def attention_start(r, own):
                softmax(r, 0, own)
                softmax(r, 1, own)
                softmax(r, 2, own)
                for b in range(B - 3):
                    out_norm(r, b, own)
                    softmax(r, b + 3, own)
                out_norm(r, 5, own)

            def attention(r, own):
                attention_start(r, own)
                out_norm(r, 6, own)
                out_norm(r, 7, own)

            own = Chain(dve, s["dve_a"])
            dve.wait_ge(s["d_x"], 16)
            dve.wait_ge(s["d_vec"], 16)
            layer_norm(0, 0, xin[:, :], xh[:, :])
            dve.wait_ge(s["qp_copied"], 1)
            queries_out(Q4, qpT[:, 0:T], "q4_ready")
            for u in range(UNITS):
                dve.wait_ge(s["cand_scores"], u + 1)
                src = PS[:, 3 * (u % 2):3 * (u % 2) + 3, :].rearrange("p k c -> p (k c)")[:, 0:S]
                own(v_.max(mx8[:, :], src))
                own(v_.max_index(idx8[:, :], mx8[:, :], src))
                v_.tensor_tensor(rows[:, u:u + 1], idx8[:, 0:1], colv(V_BASE + u), ALU.add)\
                    .then_inc(s["rows_ready"], 1)
            dve.wait_ge(s["d_wq"], 32)
            v_.tensor_reduce(sw[:, 0:FC], w1n[:, :, :], AX.X, ALU.max, apply_absolute_value=True)
            own(v_.tensor_reduce(sw[:, FC:FC + 1], w2n[:, :], AX.X, ALU.max, apply_absolute_value=True))
            own(v_.tensor_scalar(sw[:, 0:5], sw[:, 0:5], 1e-8, 1.0 / 127.0, ALU.max, ALU.mult))
            own(v_.reciprocal(swi[:, 0:5], sw[:, 0:5]))
            for c in range(FC):
                v_.tensor_scalar(wt[:, 0, c * D:(c + 1) * D], w1n[:, c, :], swi[:, c:c + 1], MAGIC, ALU.mult, ALU.add)
            own(v_.tensor_scalar(wt[:, 1, :], w2n[:, :], swi[:, FC:FC + 1], MAGIC, ALU.mult, ALU.add))
            own(v_.tensor_scalar(wt[:, :, :], wt[:, :, :], -MAGIC, -128.0, ALU.add, ALU.max))
            v_.tensor_scalar(wqb[:, :, :], wt[:, :, :], 127.0, None, ALU.min).then_inc(s["wq_ready"], 1)
            attention(0, own)
            dve.wait_ge(s["wo_done"], 1)
            v_.tensor_tensor(x1[:, :], xin[:, :], PS[:, 0, 0:T], ALU.add).then_inc(s["x_ready"], 1)

            layer_norm(1, 1, x1[:, :], xh[:, :])
            dve.wait_ge(s["norm_ready"], 2)
            rms_norm(2, xh[:, :], colv(V_SCALE), h[:, :])
            dve.wait_ge(s["gate_done"], 1)
            dve.wait_ge(s["d_gw"], 32)
            own(v_.tensor_tensor(gl[:, :, :], PS[0:PB, 0, 0:UNITS * E].rearrange("p (u e) -> p u e", e=E),
                                 gb[:, :].unsqueeze(1).broadcast_to([PB, UNITS, E]), ALU.add))
            for u in range(UNITS):
                v = v_.max(gm8[:, u, :], gl[:, u, :])
            own(v)
            for u in range(UNITS):
                v = v_.max_index(gi8[:, u, :], gm8[:, u, :], gl[:, u, :])
            own(v)
            dve.wait_ge(s["consts"], 13)
            own(v_.tensor_copy(gif[:, :, :], gi8[:, :, 0:TOPK]))
            v_.tensor_tensor(ge[:, :, :], gl[:, :, :], gm8[:, :, 0:1].broadcast_to([PB, UNITS, E]), ALU.subtract)\
                .then_inc(s["gexp_in"], 1)
            own(v_.tensor_tensor(eq[:, :, :, :],
                                 eiof[:, :].unsqueeze(1).unsqueeze(3).broadcast_to([PB, UNITS, E, TOPK]),
                                 gif[:, :, :].unsqueeze(2).broadcast_to([PB, UNITS, E, TOPK]), ALU.is_equal))
            own(v_.tensor_reduce(gl[:, :, :], eq[:, :, :, :], AX.X, ALU.add))
            dve.wait_ge(s["gexp_done"], 1)
            own(v_.tensor_tensor(gl[:, :, :], gl[:, :, :], ge[:, :, :], ALU.mult))
            own(v_.tensor_reduce(gsum[:, :], gl[:, :, :], AX.X, ALU.add))
            own(v_.reciprocal(gsum[:, :], gsum[:, :]))
            v_.tensor_tensor(ge[:, :, :], gl[:, :, :], gsum[:, :].unsqueeze(2).broadcast_to([PB, UNITS, E]),
                             ALU.mult).then_inc(s["route_ready"], 1)
            dve.wait_ge(s["route_turned"], 1)
            ps = PS[0:E, 1, 0:T]
            own(v_.tensor_copy(rb[0:E, :], ps))
            own(v_.tensor_tensor(rpart[:, 0, :], ps, rb[0:E, :], ALU.subtract))
            v_.tensor_copy(routeT[:, :], ps)
            v_.tensor_copy(rb[32:32 + E, :], rpart[:, 0, :])
            own(v_.tensor_copy(rmid[:, :], rpart[:, 0, :]))
            own(v_.tensor_tensor(rpart[:, 1, :], rpart[:, 0, :], rmid[:, :], ALU.subtract))
            v_.tensor_copy(rb[64:64 + E, :], rpart[:, 1, :]).then_inc(s["rb_ready"], 1)

            def expert(e, k, first):
                bank = 3 * (k % 2)
                dve.wait_ge(s["e_glr"], e + 1)
                v_.tensor_scalar(xg[:, k % 2, :], PS[:, bank, 0:T], vec[:, bass.ds(e + V_B1G, 1)], LIMIT,
                                 ALU.add, ALU.min).then_inc(s["xg_ready"], 1)
                dve.wait_ge(s["l1_ready"], e + 1)
                v_.tensor_scalar(l2[:, k % 2, :], l1[:, k % 2, :], LIMIT, LIMIT, ALU.max, ALU.min)\
                    .then_inc(s["l2_ready"], 1)
                dve.wait_ge(s["l2_ready"], e + 1)
                v_.scalar_tensor_tensor(ww[:, k % 2, :], l2[:, k % 2, :], 1.0, PS[:, bank + 2, 0:T],
                                        ALU.add, ALU.mult).then_inc(s["ww_ready"], 1)
                dve.wait_ge(s["sg_ready"], e + 1)
                v_.tensor_tensor(vv[:, k % 2, :], xg[:, k % 2, :], sg[:, k % 2, :], ALU.mult)\
                    .then_inc(s["vv_ready"], 1)
                dve.wait_ge(s["ww_ready"], e + 1)
                dve.wait_ge(s["vv_ready"], e + 1)
                if not first or k >= 2:
                    dve.wait_ge(s["y_done"], e - 1)
                v_.tensor_tensor(zz[:, k % 2, :], ww[:, k % 2, :], vv[:, k % 2, :], ALU.mult)\
                    .then_inc(s["zz_ready"], 1)

            for k in range(RING):
                expert(k, k, True)
            with dve.Fori(1, E // RING) as i:
                for k in range(RING):
                    expert(i * RING + k, k, False)
            own(v_.tensor_tensor(x2[:, :], x1[:, :], xh[:, :], ALU.add))
            dve.wait_ge(s["y_done"], E)
            v_.tensor_tensor(x2[:, :], x2[:, :], PS[:, 6, 0:T], ALU.add).then_inc(s["x_ready"], 1)

            layer_norm(2, 3, x2[:, :], xl[:, :])
            dve.wait_ge(s["d_seg"], 16)
            dve.wait_ge(s["consts"], 15)
            own(v_.tensor_copy(segf[:, 0, :], seg[:, :]))
            own(v_.tensor_scalar(segf[:, 1, :], segf[:, 0, :], -float(LOOKBACK), None, ALU.add))
            for b in range(B):
                v_.tensor_scalar(xm[:, 0, :], krowf[:, :], segf[:, 0, b:b + 1], NEG, ALU.is_gt, ALU.mult)
                own(v_.tensor_scalar(xm[:, 1, :], krowf[:, :], segf[:, 1, b:b + 1], NEG, ALU.is_le, ALU.mult))
                last = v_.tensor_tensor(xbias[:, b, :].rearrange("p (g k) -> p g k", g=GR),
                                        xm[:, 0, :].unsqueeze(1).broadcast_to([PB, GR, NEAR]),
                                        xm[:, 1, :].unsqueeze(1).broadcast_to([PB, GR, NEAR]), ALU.add)
                own(last)
            v_.tensor_copy(cz[:, 0, 0:B], segf[:, 0, :]).then_inc(s["xbias_ready"], 1)
            dve.wait_ge(s["d_par"], 16)
            dve.wait_ge(s["d_cs"], 16)
            dve.wait_ge(s["d_segrow"], 16)
            own(v_.tensor_copy(segrf[:, :], segrow[:, :]))
            own(v_.tensor_reduce(lim[:, 0:1], segrf[:, :], AX.X, ALU.max))
            own(v_.tensor_reduce(lim[:, 1:2], segrf[:, :], AX.X, ALU.min))
            own(v_.tensor_scalar(lim[:, 2:3], lim[:, 0:1], NEAR - 0.5, None, ALU.is_lt))
            own(v_.tensor_scalar(lim[:, 3:4], lim[:, 1:2], 0.0, lim[:, 2:3], ALU.is_ge, ALU.mult))
            v_.tensor_copy(near_i[:, :], lim[:, 3:4]).then_inc(s["near_known"], 1)
            dve.wait_ge(s["near_known"], 1)
            short = dve.value_load(near_i[0:1, 0:1], min_val=0, max_val=1)

            def near_softmax(l, u, own):
                dve.wait_ge(s["cs_ready"], l * UNITS + (u + 1))
                src = PS[0:PB, u % 2, :].rearrange("p (c k) -> p c k", k=NEAR)
                own(v_.tensor_reduce(mxs[:, u % 2, :], src, AX.X, ALU.max))
                v_.tensor_tensor(Pc[:, u, :, :], src, mxs[:, u % 2, :].unsqueeze(2).broadcast_to([PB, 16, NEAR]),
                                 ALU.subtract).then_inc(s["csub_done"], 1)

            def near_out_norm(l, u, own):
                dve.wait_ge(s["cpv_done"], l * UNITS + (u + 1))
                if u >= 2:
                    dve.wait_ge(s["cot_done"], l * UNITS + (u - 1))
                normalise(PS[0:PB, 4 + u % 2, 0:16 * CO], 16, wgt[:, u % 2, :, :], rcp[:, u % 2, :],
                          O[:, u % 2, :, :].rearrange("p k (c j d) -> p (k c) j d", j=2, d=DH), own)\
                    .then_inc(s["con_ready"], 1)

            def half(ap, hf):
                return ap[:, hf * HT:(hf + 1) * HT]

            def half_norm(n, w, hf):
                dve.wait_ge(s["n_rs"], n + 1)
                v_.scalar_tensor_tensor(half(h, hf), half(xl, hf), w, half(rs, hf), ALU.mult, ALU.mult)\
                    .then_inc(s["n_h"], 1)

            def half_add(done, n, hf, x, bias=False, bank=6):
                dve.wait_ge(s[done], n)
                if bias:
                    v_.scalar_tensor_tensor(half(xl, hf), PS[:, bank, hf * HT:(hf + 1) * HT], bo2[:, 0:1], half(xl, hf),
                                            ALU.add, ALU.add).then_inc(s["n_x"], 1)
                else:
                    v_.tensor_tensor(half(xl, hf), PS[:, bank, hf * HT:(hf + 1) * HT], half(xl, hf), ALU.add)\
                        .then_inc(s["n_x"], 1)
                dve.wait_ge(s["n_x"], x)

            def near_queries_out(l, hf):
                dve.wait_ge(s["n_qc"], l * 2 + (hf + 1))
                for j in range(HG):
                    last = v_.tensor_scalar(Q4c[:, hf * HB:(hf + 1) * HB, j, :],
                                            heads3(PS[:, 7, 0:T])[:, hf * HB:(hf + 1) * HB, :], colv(V_SEL + j),
                                            None, ALU.mult)
                last.then_inc(s["n_q4c"], 1)

            def cross_long(l):
                dve.wait_ge(s["qc_done"], l + 1)
                v_.tensor_copy(tq[:, 0, :], PS[:, 1, 0:T]).then_inc(s["far_step"], 1)
                with dve.Fori(0, B) as b:
                    lb = l * B + b
                    fb = Chain(dve, s["dve_fb"], lb * 7)
                    dve.wait_ge(s["far_step"], l * (B + 1) + b + 1)
                    fb(v_.tensor_copy(gq, tq[:, 0, bass.ds(b * L, L)]))
                    for k in range(3):
                        fb(v_.tensor_scalar(gi[:, k * SB:(k + 1) * SB], frow[:, :], float(k * SB), None, ALU.add))
                    fb(v_.tensor_scalar(gb_, gi, segf[0:L, 0, bass.ds(b, 1)], NEG, ALU.is_gt, ALU.mult))
                    fb(v_.tensor_scalar(gi, gi, segf[0:L, 1, bass.ds(b, 1)], NEG, ALU.is_le, ALU.mult))
                    fb(v_.tensor_tensor(gb_, gb_, gi, ALU.add))
                    dve.wait_ge(s["far_kv"], lb + 1)
                    v_.tensor_copy(gk.rearrange("p (c n) -> p c n", c=3), PS[:, 0:3, 0:SB]).then_inc(s["gk_ready"], 1)
                    with dve.Fori(0, H) as hh_:
                        t = lb * H + hh_
                        fh = Chain(dve, s["dve_fh"], t * 4)
                        dve.wait_ge(s["gk_ready"], lb + 1)
                        v_.tensor_scalar(gqz, gq, vec[:, bass.ds(hh_ + V_HEAD, 1)], None, ALU.mult)\
                            .then_inc(s["gq_ready"], 1)
                        dve.wait_ge(s["fs_ready"], t + 1)
                        fh(v_.tensor_tensor(gp.rearrange("p (c n) -> p c n", c=3), PS[0:L, 0:3, 0:SB],
                                            gb_.rearrange("p (c n) -> p c n", c=3), ALU.add))
                        fh(v_.tensor_reduce(fmx[:, 0:1], gp, AX.X, ALU.max))
                        v_.tensor_scalar(gp, gp, fmx[:, 0:1], None, ALU.subtract).then_inc(s["fm_ready"], 1)
                        dve.wait_ge(s["fo_ready"], t + 1)
                        fh(v_.reciprocal(fmx[:, 0:1], fmx[:, 2:3]))
                        fh(v_.tensor_scalar(gO[:, bass.ds(hh_ * DH, DH)], PS[0:L, 3, 0:DH], fmx[:, 0:1], None,
                                            ALU.mult))
                    v_.tensor_copy(gOc, gO).then_inc(s["fO_ready"], 1)
                    dve.wait_ge(s["ff_ready"], lb + 1)
                    v_.tensor_copy(o[:, bass.ds(b * L, L)], PS[:, 4, 0:L]).then_inc(s["far_step"], 1)
                dve.wait_ge(s["far_step"], l * (B + 1) + (B + 1))
                v_.tensor_copy(tq[:, 1, 0:1], o[:, 0:1]).then_inc(s["oc_ready"], 1)

            with dve.If(short == 1):
                dve.wait_ge(s["norm_ready"], 4)
                v_.tensor_copy(tq[:, 1, 0:1], xl[:, 0:1]).then_inc(s["n_x"], 1)
                with dve.Fori(0, NL) as l:
                    own = Chain(dve, s["n_dve"], l * NDVE)
                    v_.tensor_copy(pl[:, :], par[:, bass.ds(l, 1), :].rearrange("p l n -> p (l n)"))\
                        .then_inc(s["pl_ready"], 1)
                    dve.wait_ge(s["pl_ready"], l + 1)
                    half_norm(l * 6, pl[:, N1:N1 + 1], 0)
                    half_norm(l * 6 + 1, pl[:, N1:N1 + 1], 1)
                    dve.wait_ge(s["ckv_done"], l + 1)
                    v_.tensor_tensor(bo2[:, :], pl[:, BO:BO + 1], PS[:, 3, 0:1], ALU.add).then_inc(s["bo_ready"], 1)
                    dve.wait_ge(s["bo_ready"], l + 1)
                    for hf in range(2):
                        c = slice(hf * HT, (hf + 1) * HT)
                        for i, (t, b1, b2) in enumerate(((tq, BQ, BQR), (tk, BK, BKR))):
                            dve.wait_ge(s["n_proj"], l * 4 + (2 * hf + i + 1))
                            bank = 4 + 2 * hf + i
                            v_.scalar_tensor_tensor(t[:, 0, c], PS[:, bank, 0:HT], pl[:, b1:b1 + 1], cs[:, 0, c],
                                                    ALU.add, ALU.mult)
                            own(v_.scalar_tensor_tensor(t[:, 1, c], PS[:, bank, HT:T], pl[:, b2:b2 + 1],
                                                        cs[:, 1, c], ALU.add, ALU.mult))
                            add = v_.tensor_tensor(qk[:, i, c], t[:, 0, c], t[:, 1, c], ALU.add)
                            if i == 1:
                                add.then_inc(s["n_k"], 1)
                            else:
                                own(add)
                        for j in range(HG):
                            last = v_.tensor_scalar(Q4[:, hf * HB:(hf + 1) * HB, j, :],
                                                    heads3(qk[:, 0, :])[:, hf * HB:(hf + 1) * HB, :],
                                                    colv(V_SEL + j), None, ALU.mult)
                    last.then_inc(s["q4_ready"], 1)
                    r = l + 1
                    attention_start(r, own)
                    half_add("n_wo", l * 2 + 1, 0, l * 6 + 2, True)
                    out_norm(r, 6, own)
                    half_norm(l * 6 + 2, pl[:, N2:N2 + 1], 0)
                    out_norm(r, 7, own)
                    near_queries_out(l, 0)
                    half_add("n_wo", l * 2 + 2, 1, l * 6 + 3, True)
                    near_softmax(l, 0, own)
                    half_norm(l * 6 + 3, pl[:, N2:N2 + 1], 1)
                    near_softmax(l, 1, own)
                    near_queries_out(l, 1)
                    near_out_norm(l, 0, own)
                    near_softmax(l, 2, own)
                    near_out_norm(l, 1, own)
                    near_softmax(l, 3, own)
                    half_add("n_woc", l * 2 + 1, 0, l * 6 + 4)
                    near_out_norm(l, 2, own)
                    half_norm(l * 6 + 4, pl[:, N3:N3 + 1], 0)
                    near_out_norm(l, 3, own)
                    half_add("n_woc", l * 2 + 2, 1, l * 6 + 5)
                    half_norm(l * 6 + 5, pl[:, N3:N3 + 1], 1)
                    for i in range(2 * FC):
                        hf, c = i // FC, i % FC
                        dve.wait_ge(s["n_silu"], l * 2 * FC + (i + 1))
                        v_.tensor_tensor(mm[:, c, hf * HT:(hf + 1) * HT], sl[:, c, hf * HT:(hf + 1) * HT],
                                         PS[:, 2 + i % 2, 0:HT], ALU.mult).then_inc(s["n_m"], 1)
                        if i == FC + 1:
                            half_add("n_down", l * 2 + 1, 0, l * 6 + 6, bank=4)
                    half_add("n_down", l * 2 + 2, 1, l * 6 + 7, bank=5)
                    v_.tensor_copy(tq[:, 1, 0:1], xl[:, 0:1])
                    assert own.n == NDVE, own.n
                v_.tensor_copy(tq[:, 1, 1:2], xl[:, 0:1]).then_inc(s["layers_done"], 1)
            with dve.If(short == 0):
                with dve.Fori(0, NL) as l:
                    own = Chain(dve, s["dve_l"], l * NDVE_LONG)
                    v_.tensor_copy(pl[:, :], par[:, bass.ds(l, 1), :].rearrange("p l n -> p (l n)"))\
                        .then_inc(s["pl_ready"], 1)
                    dve.wait_ge(s["pl_ready"], l + 1)
                    dve.wait_ge(s["norm_ready"], l * 3 + 4)
                    dve.wait_ge(s["x_ready"], l * 3 + 2)
                    rms_norm(l * 3 + 4, xl[:, :], pl[:, N1:N1 + 1], h[:, :])
                    for i, (t, b1, b2) in enumerate(((tq, BQ, BQR), (tk, BK, BKR))):
                        dve.wait_ge(s["n_proj"], l * 4 + (2 * i + 1))
                        v_.scalar_tensor_tensor(t[:, 0, :], PS[:, 4 + 2 * i, 0:T], pl[:, b1:b1 + 1], cs[:, 0, :],
                                                ALU.add, ALU.mult)
                        dve.wait_ge(s["n_proj"], l * 4 + (2 * i + 2))
                        own(v_.scalar_tensor_tensor(t[:, 1, :], PS[:, 5 + 2 * i, 0:T], pl[:, b2:b2 + 1], cs[:, 1, :],
                                                    ALU.add, ALU.mult))
                        add = v_.tensor_tensor(qk[:, i, :], t[:, 0, :], t[:, 1, :], ALU.add)
                        if i == 1:
                            add.then_inc(s["k_ready"], 1)
                        else:
                            own(add)
                            queries_out(Q4, qk[:, 0, :], "q4_ready")
                    dve.wait_ge(s["ckv_done"], l + 1)
                    v_.tensor_tensor(bo2[:, :], pl[:, BO:BO + 1], PS[:, 1, 0:1], ALU.add).then_inc(s["bo_ready"], 1)
                    dve.wait_ge(s["bo_ready"], l + 1)
                    attention(l + 1, own)
                    dve.wait_ge(s["wo_done"], l + 2)
                    v_.scalar_tensor_tensor(xl[:, :], PS[:, 0, 0:T], bo2[:, 0:1], xl[:, :], ALU.add, ALU.add)\
                        .then_inc(s["x_ready"], 1)
                    dve.wait_ge(s["x_ready"], l * 3 + 3)
                    rms_norm(l * 3 + 5, xl[:, :], pl[:, N2:N2 + 1], h[:, :])
                    cross_long(l)
                    dve.wait_ge(s["woc_done"], l + 1)
                    v_.tensor_tensor(xl[:, :], xl[:, :], PS[:, 0, 0:T], ALU.add).then_inc(s["x_ready"], 1)
                    dve.wait_ge(s["x_ready"], l * 3 + 4)
                    rms_norm(l * 3 + 6, xl[:, :], pl[:, N3:N3 + 1], h[:, :])
                    for c in range(FC):
                        dve.wait_ge(s["silu_done"], l * FC + (c + 1))
                        dve.wait_ge(s["u_done"], l * FC + (c + 1))
                        v_.tensor_tensor(mm[:, c, :], sl[:, c, :], PS[:, 2 * (c % 2) + 1, 0:T], ALU.mult)\
                            .then_inc(s["m_ready"], 1)
                    dve.wait_ge(s["d_done"], l + 1)
                    v_.tensor_tensor(xl[:, :], xl[:, :], PS[:, 4, 0:T], ALU.add).then_inc(s["x_ready"], 1)
                    assert own.n == NDVE_LONG, own.n
                dve.wait_ge(s["x_ready"], 2 + 3 * NL)
                v_.tensor_copy(tq[:, 1, 0:1], xl[:, 0:1]).then_inc(s["layers_done"], 1)
            own = Chain(dve, s["dve_d"])
            dve.wait_ge(s["rs_last"], 1)
            own(v_.scalar_tensor_tensor(h[:, :], xl[:, :], colv(V_NF), rs[:, :], ALU.mult, ALU.mult))
            v_.tensor_tensor(x3[:, :], x2[:, :], h[:, :], ALU.add).then_inc(s["layers_done"], 1)
            dve.wait_ge(s["layers_done"], 2)

            dve.wait_ge(s["wq_turned"], 1)
            v_.tensor_copy(w1qT[:, :], PS[:, 0, 0:256].bitcast(BF16))
            v_.tensor_copy(w2qT[:, :, :].rearrange("p c d -> p (c d)"), PS[:, 1, 0:256].bitcast(BF16))\
                .then_inc(s["wqT_ready"], 1)
            layer_norm(3, 1, x3[:, :], yt[:, :], "rs_last", "yt_ready")
            dve.wait_ge(s["yt_ready"], 1)

            def scale_of(i, c):
                dve.wait_ge(s["max_turned"], i + 1)
                own(v_.tensor_reduce(s11[0:1, 1:2], PS[0:1, 5, 0:D], AX.X, ALU.max))
                v_.tensor_scalar(s11[0:1, 2:3], s11[0:1, 1:2], 1e-8, 1.0 / 255.0, ALU.max, ALU.mult)\
                    .then_inc(s["s_one"], 1)
                dve.wait_ge(s["s_bcast"], i + 1)
                own(v_.tensor_copy(s11[:, c:c + 1], PS[:, 4, 0:1]))
                own(v_.reciprocal(s11[:, c + 1:c + 2], s11[:, c:c + 1]))

            def bias_of(c0, n, src, sc):
                own(v_.tensor_scalar(ss[:, c0:c0 + n], sw[:, c0:c0 + n], s11[:, sc:sc + 1], None, ALU.mult))
                own(v_.reciprocal(swi[:, c0:c0 + n], ss[:, c0:c0 + n]))
                own(v_.tensor_tensor(bq[:, c0:c0 + n], src, swi[:, c0:c0 + n], ALU.mult))
                own(v_.tensor_scalar(bq[:, c0:c0 + n], bq[:, c0:c0 + n], MAGIC, -MAGIC, ALU.add, ALU.add))
                own(v_.tensor_tensor(bq[:, c0:c0 + n], bq[:, c0:c0 + n], ss[:, c0:c0 + n], ALU.mult))

            v_.tensor_reduce(s11[:, 0:1], yt[:, :], AX.X, ALU.max).then_inc(s["max_in"], 1)
            scale_of(0, 3)
            own(v_.tensor_scalar(sq2[:, :], yt[:, :], s11[:, 4:5], MAGIC, ALU.mult, ALU.add))
            own(v_.tensor_scalar(sq2[:, :], sq2[:, :], -MAGIC, 0.0, ALU.add, ALU.max))
            own(v_.tensor_scalar(yq[:, :], sq2[:, :], 255.0, None, ALU.min))
            bias_of(0, FC, colv(V_B1, FC), 3)
            v_.tensor_copy(s11[:, 5:6], s11[:, 3:4]).then_inc(s["yq_ready"], 1)
            for c in range(FC):
                dve.wait_ge(s["relu_done"], c + 1)
                v = v_.tensor_reduce(s11[:, 8 + c:9 + c], hh[:, c, :], AX.X, ALU.max)
            own(v)
            v_.tensor_reduce(s11[:, 0:1], s11[:, 8:8 + FC], AX.X, ALU.max).then_inc(s["max_in"], 1)
            scale_of(1, 6)
            own(v_.tensor_scalar(ht[:, :, :], hh[:, :, :], s11[:, 7:8], MAGIC, ALU.mult, ALU.add))
            own(v_.tensor_scalar(ht[:, :, :], ht[:, :, :], -MAGIC, 0.0, ALU.add, ALU.max))
            own(v_.tensor_scalar(hq[:, :, :], ht[:, :, :], 255.0, None, ALU.min))
            bias_of(FC, 1, colv(V_B2), 6)
            v_.tensor_copy(s11[:, 5:6], s11[:, 6:7]).then_inc(s["hq_ready"], 1)
            dve.wait_ge(s["out_scaled"], 1)
            v_.tensor_tensor(yt[:, :], yt[:, :], x3[:, :], ALU.add).then_inc(s["out_ready"], 1)


def kernel(**inputs):
    import concourse.bacc as _bacc
    from concourse.bass_utils import run_bass_kernel_spmd as _run

    g = {n: np.asarray(v) for n, v in inputs.items()}
    f32 = np.float32
    x, ctxt = g["x"], g["ctx_1024"]
    arr = {}
    arr["xT"] = x.reshape(T, D).T
    arr["ctx"] = ctxt.reshape(B * S, D)
    arr["ctxT"] = ctxt.reshape(B * S, D).T
    wkv = g["L0_xattn_Wkv"]
    arr["wa0"] = np.concatenate([g["L0_xattn_Wq"].T, np.tile(wkv[:DH], (H, 1)).T, np.tile(wkv[DH:], (H, 1)).T,
                                 g["L0_xattn_Wc"].T], axis=1)
    arr["gw"] = g["L0_ffn_gate_w"].T
    arr["gb"] = np.tile(g["L0_ffn_gate_b"][None], (PB, 1))
    m1, m1b = g["L0_ffn_mlp1_w"], g["L0_ffn_mlp1_b"]
    arr["ew"] = np.concatenate([m1[:, ::2].transpose(2, 0, 1), m1[:, 1::2].transpose(2, 0, 1),
                                g["L0_ffn_mlp2_w"].transpose(2, 0, 1)], axis=2).reshape(D, E * 3 * D)
    arr["b2e"] = g["L0_ffn_mlp2_b"]
    seg = g["itok_BxS_0_255"]
    arr["seg"] = np.tile(seg.T, (2, 1)).astype(np.int32)
    arr["segrow"] = seg.reshape(1, T).astype(np.int32)
    arr["w1n"] = g["L1_ffn_w1"].reshape(FC, D, D).transpose(1, 0, 2)
    arr["w2n"] = g["L1_ffn_w2"]
    inv = (1.0 / f32(10000.0) ** (np.arange(0, DH, 2, dtype=f32) / f32(DH))).astype(f32)
    ang = np.arange(L, dtype=f32)[:, None] * inv[None]
    half = DH // 2
    dim = np.arange(D) % DH
    cos, sin = np.cos(ang).astype(f32)[:, dim % half].T, np.sin(ang).astype(f32)[:, dim % half].T
    sin = np.where(dim[:, None] < half, -sin, sin)
    arr["cs"] = np.stack([np.tile(cos, (1, B)), np.tile(sin, (1, B))], axis=1).astype(f32)
    swap = np.arange(D) - dim + (dim + half) % DH
    wqkv, bqkv = g["L1_xattn_Wqkv"], g["L1_xattn_bqkv"]
    wq, wk, wv = wqkv[:, 0:D], wqkv[:, D:2 * D], wqkv[:, 2 * D:]
    bq_, bk_, bv_ = bqkv[:, 0:D], bqkv[:, D:2 * D], bqkv[:, 2 * D:]
    wkvc = g["L1_xattn_Wkv_c"]
    blocks = [wq, wq[:, swap], wk, wk[:, swap], wv, g["L1_xattn_Wo"], g["L1_xattn_Wq_c"], wkvc[:, :D], wkvc[:, D:],
              g["L1_xattn_Wo_c"]]
    arr["wA"] = np.concatenate([w.transpose(2, 0, 1) for w in blocks], axis=2).reshape(D, NL * WATT)
    down = g["L1_xattn_Wd"].reshape(NL, D, FC, D).transpose(3, 0, 2, 1).reshape(D, NL, FF)
    arr["wF"] = np.concatenate([g["L1_xattn_Wg"].transpose(2, 0, 1), g["L1_xattn_Wu"].transpose(2, 0, 1), down],
                               axis=2).reshape(D, NL * WFFN)
    arr["par"] = np.stack([bq_, bq_[:, swap], bk_, bk_[:, swap], bv_, g["L1_xattn_bo"], g["L1_xattn_n1"],
                           g["L1_xattn_n2"], g["L1_xattn_n3"]], axis=0).transpose(2, 1, 0)
    p = np.arange(D)
    sel = (p[:, None] // DH % HG == np.arange(HG)[None]).astype(f32)
    row = np.stack([p < L, (p >= L) & (p < PB)], axis=1).astype(f32)
    base = (2 * np.arange(UNITS)[None] + p[:, None] // 64).astype(f32) * f32(S)
    heads = (p[:, None] // DH == np.arange(H)[None]).astype(f32)
    arr["vec"] = np.concatenate([g["L0_ffn_scale"][:, None], g["L1_xattn_nf"][:, None], g["L1_ffn_b2"][:, None],
                                 g["L1_ffn_b1"].reshape(FC, D).T, sel, row, base, m1b[:, ::2].T, m1b[:, 1::2].T,
                                 heads], axis=1)
    nc = _bacc.Bacc("TRN2", target_bir_lowering=False, num_devices=1)
    feed, aps = {}, {}
    for name, v in arr.items():
        v = np.ascontiguousarray(v)
        feed[f"in_{name}"] = v
        aps[name] = nc.dram_tensor(f"in_{name}", v.shape, mybir.dt.from_np(v.dtype), kind="ExternalInput").ap()
    out = nc.dram_tensor("out_0", (D, T), F32, kind="ExternalOutput").ap()
    build(nc, aps, out)
    r = _run(nc, [feed], core_ids=[0])
    return r.results[0]["out_0"].T.reshape(B, L, D)
```

```python
from contextlib import ExitStack

import numpy as np

import concourse.bass as bass
from concourse import mybir

F32 = mybir.dt.float32
BF16 = mybir.dt.bfloat16
I32 = mybir.dt.int32
U32 = mybir.dt.uint32
ALU = mybir.AluOpType
ACT = mybir.ActivationFunctionType
AX = mybir.AxisListType

D = 128
B = 8
L = 56
T = B * L
H = 16
DH = D // H
GR = 4
HG = H // GR
S = 1500
NL = 4
E = 16
TOPK = 4
FF = 512
FC = FF // D
HV = 2 * DH
CO = HV + 1
NEAR = 32
LOOKBACK = 128
KC = 125
NK = S // KC
SB = 500
UNITS = 4
PB = 2 * L
SCALE = float(1.0 / np.sqrt(np.float32(DH)))
WARM_SQ = 3
WARM_NORM = 8
WARM_SCORES = 3
WARM_HALF = 3
WARM_OUT = 3
WARM_FFN = 8
WARM_LAST = 8
NEG = -1e30
MAGIC = 12582912.0
LIMIT = 7.0
ALPHA = 1.702

WQ, WQR, WK, WKR, WV, WO, WQC, WKC, WVC, WOC = (i * D for i in range(10))
WATT = 10 * D
WG, WU, WD = 0, FF, 2 * FF
WFFN = 3 * FF
BQ, BQR, BK, BKR, BV, BO, N1, N2, N3 = range(9)
NP_ = 9
HT = T // 2
HB = B // 2
NDVE_LONG = 27
NDVE = 41
V_SCALE, V_NF, V_B2 = 0, 1, 2
V_B1 = 3
V_SEL = V_B1 + FC
V_ROW = V_SEL + HG
V_BASE = V_ROW + 2
V_B1G = V_BASE + UNITS
V_B1L = V_B1G + E
V_HEAD = V_B1L + E
NV = V_HEAD + H


class Chain:

    def __init__(self, eng, sem, start=0):
        self.eng, self.sem, self.start, self.n = eng, sem, start, 0

    def __call__(self, ins):
        self.n += 1
        ins.then_inc(self.sem, 1)
        self.eng.wait_ge(self.sem, self.start + self.n)


def build(nc, a, out):
    ctx = ExitStack()
    with ctx:
        def sb(name, shape, dt=F32):
            return ctx.enter_context(nc.sbuf_tensor(name, shape, dt))

        def sem(name):
            return ctx.enter_context(nc.semaphore(name))

        ctxT = sb("ctxT", [D, B * S])
        arena = [0]

        def carve(*shape):
            n = int(np.prod(shape))
            assert arena[0] + n <= B * S
            flat = ctxT[:, arena[0]:arena[0] + n]
            arena[0] += n
            if len(shape) == 1:
                return flat
            names = "abcde"[:len(shape)]
            return flat.rearrange("p (" + " ".join(names) + ") -> p " + " ".join(names),
                                  **{c: m for c, m in zip(names[1:], shape[1:])})

        xin = sb("xin", [D, T])
        xc = sb("xc", [D, T])
        sq = sb("sq", [D, T])
        rs = sb("rs", [D, T])
        xh = sb("xh", [D, T])
        h = sb("h", [D, T])
        x1 = sb("x1", [D, T])
        x2 = sb("x2", [D, T])
        xl = sb("xl", [D, T])
        wa0 = sb("wa0", [D, 4 * D])
        wA = sb("wA", [D, WATT])
        wF = sb("wF", [D, WFFN])
        par = sb("par", [D, NL, NP_])
        pl = sb("pl", [D, NP_])
        vec = sb("vec", [D, NV])
        cs = sb("cs", [D, 2, T])
        seg = sb("seg", [PB, B], I32)
        segrow = sb("segrow", [1, T], I32)
        segrf = sb("segrf", [1, T])
        lim = sb("lim", [1, 4])
        near_i = sb("near_i", [1, 1], I32)
        fmx = sb("fmx", [L, 3])
        segf = sb("segf", [PB, 2, B])
        ident = sb("ident", [D, D])
        identb = sb("identb", [D, D], BF16)
        one = sb("one", [D, 1])
        warm = sb("warm", [D, 8 * L], BF16)
        onesD = sb("onesD", [D, D])
        ones1 = sb("ones1", [1, D])
        eps = sb("eps", [D, 3])
        causal = sb("causal", [PB, 8, L], BF16)
        frow = sb("frow", [L, SB])
        cz = sb("cz", [PB, 4, L])
        krow = sb("krow", [PB, NEAR], I32)
        krowf = sb("krowf", [PB, NEAR])
        xm = sb("xm", [PB, 2, B, NEAR])
        xbias = sb("xbias", [PB, B, GR * NEAR], BF16)
        qpT = sb("qpT", [D, T + 8])
        mx8 = sb("mx8", [D, 8])
        idx8 = sb("idx8", [D, 8], U32)
        rows = sb("rows", [D, UNITS], U32)
        mem = sb("mem", [D, UNITS, D])
        tq = sb("tq", [D, 2, T])
        memD = tq[:, :, :].rearrange("p a t -> p (a t)").rearrange("p (b k l) -> p b k l", b=B, k=2)
        Q4 = sb("Q4", [D, B, HG, L])
        Kz = sb("Kz", [D, B, GR, L])
        VB = sb("VB", [PB, B, 2, 2, 2, HV + 1])
        O = sb("O", [PB, 2, 2, D])
        rcp = sb("rcp", [PB, 2, 16])
        wgt = sb("wgt", [PB, 2, 16, 2])
        fold = sb("fold", [PB, L])
        P = sb("P", [PB, 2, 2, 8, L])
        PT = sb("PT", [PB, 2, 2, 4, PB])
        mxs = sb("mxs", [PB, 2, 16])
        o = sb("o", [D, T])
        Kc = sb("Kc", [D, B, GR, NEAR])
        Vc = sb("Vc", [D, B, 2, GR, HV + 1])
        near = sb("near", [D, B, NEAR])
        bo2 = sb("bo2", [D, 1])
        gw = sb("gw", [D, E])
        gb = sb("gb", [PB, E])
        gl = sb("gl", [PB, UNITS, E])
        gm8 = sb("gm8", [PB, UNITS, 8])
        gi8 = sb("gi8", [PB, UNITS, 8], U32)
        gif = sb("gif", [PB, UNITS, TOPK])
        eio = sb("eio", [PB, E], I32)
        eiof = sb("eiof", [PB, E])
        gsplit = sb("gsplit", [PB, UNITS, 96], BF16)
        grest = sb("grest", [PB, 2, UNITS, E])
        eq = sb("eq", [PB, UNITS, E, TOPK])
        ge = sb("ge", [PB, UNITS, E])
        gsum = sb("gsum", [PB, UNITS])
        b2e = sb("b2e", [E, D])
        RING = 4
        ew = sb("ew", [D, RING, 3 * D])
        wn = sb("wn", [D, 2, FF])
        w1n = wn[:, 0, :].rearrange("p (c d) -> p c d", c=FC)
        w2n = wn[:, 1, :]
        wt = wn
        wqb = sb("wqb", [D, 2, FF], BF16)
        w1qT = sb("w1qT", [D, FF], BF16)
        w2qT = sb("w2qT", [D, FC, D], BF16)
        sw = sb("sw", [D, 8])
        swi = sb("swi", [D, 8])
        ss = sb("ss", [D, 8])
        bq = sb("bq", [D, 8])
        s11 = sb("s11", [D, 12])
        yt = sb("yt", [D, T])
        yq = sb("yq", [D, T], BF16)
        def bf16(ap):
            return ap.bitcast(BF16)

        sel = bf16(carve(E * D // 2)[0:96]).rearrange("p (e d) -> p e d", e=E)
        routeT = carve(T)[0:E]
        rb = bf16(carve(T // 2)[0:96])
        xg, sg, l1, l2, vv, ww, zz = (carve(2, T) for _ in range(7))
        arena[0] = 0
        Q4c = carve(B, HG, L)
        Pc = carve(UNITS, 16, NEAR)[0:PB]
        PTc = carve(UNITS, 4, PB)
        sl = carve(FC, T)
        mm = sl
        hd = carve(B, 2, L)
        near4 = carve(B, GR, NEAR)
        tk = carve(2, T)
        qk = carve(2, T)
        x3 = x1
        arena[0] = 0
        gx = carve(S)
        gk = carve(S)
        gv = carve(S)
        gV = carve(NK, D)[0:KC]
        gp = carve(S)[0:L]
        gPT = carve(NK, L)[0:KC]
        assert arena[0] <= 8320
        gb_ = P[:, :, :, :, :].rearrange("p a b c l -> p (a b c l)")[0:L, 0:S]
        gi = PT[:, :, :, :, :].rearrange("p a b c l -> p (a b c l)")[0:L, 0:S]
        gq, gqz = tk[:, 0, 0:L], tk[:, 0, 64:64 + L]
        gO, gOc = qk[0:L, 0, 0:D], qk[0:L, 1, 0:D]
        arena[0] = 0
        sq2 = carve(T)
        hh = carve(FC, T)
        ht = carve(FC, T)
        hq = carve(FC * T // 2).bitcast(BF16).rearrange("p (c t) -> p c t", c=FC)

        PS = ctx.enter_context(nc.psum_tensor("PS", [D, 8, 512], F32))

        names = """krow_ready n_kz n_q n_q4 n_x n_sq n_ms n_rs n_h n_hd n_proj n_k n_wo n_qc n_woc n_q4c n_up n_silu n_m n_down
        layers_done n_ln ln_last sq_last ms_last rs_last yt_ready warm_ready d_x d_vec d_wa0 d_ctx0 d_ctx1 d_ctx2 d_ctx3 d_gw d_seg d_cs d_par d_wA d_wF d_wq d_b2e
        ln_done on_ready ot_done con_ready cot_done near_out near_ready d_segrow near_known far_step d_gx far_kv gk_ready gv_ready far_vt gV_ready gq_ready fs_ready fm_ready fe_ready ft_ready fpt_ready fo_ready fO_ready ff_ready dve_fb dve_fh ww_ready x_ready xbias_ready bo_ready d_near d_ew0 d_ew1 d_ew2 d_ew3 d_out g0 g1 g2 g3
        consts pool_own dve_a dve_l dve_d         mean_ready xc_ready sq_ready ms_ready rstd_ready norm_ready
        qp_done qp_copied cand_scores rows_ready mem_turned memT_ready kv_done
        proj_done q4_ready kz_ready vb_ready s_ready sub_done exp_done turned pt_ready pv_done o_ready
        wo_done ckv_done ckv_ready cs_ready csub_done cexp_done cturned cpt_ready cpv_done oc_ready
        g_done u_done pl_ready
        gate_done route_ready gexp_in gexp_done route_turned rb_ready
        e_gate e_glr g1_ready xg_ready sg_ready l1_ready l2_ready vv_ready zz_ready y_done         wq_ready wq_turned wqT_ready max_in max_turned s_one s_bcast yq_ready up_done relu_done hq_ready down_done bias1_ready bias2_ready out_ready""".split()
        s = {n: sem(n) for n in names}

        ctx.enter_context(nc.allow_non_contiguous_dma(reason="small vectors"))
        block = ctx.enter_context(nc.Block())

        def colv(c, n=1, p=D):
            return vec[0:p, c:c + n]

        def heads3(ap):
            return ap.rearrange("p (b l) -> p b l", b=B)

        @block.sync
        def _(sp):
            sp.dma_start(xin[:, :], a["xT"]).then_inc(s["d_x"], 16)
            sp.dma_start(vec[:, :], a["vec"]).then_inc(s["d_vec"], 16)
            sp.dma_start(wa0[:, :], a["wa0"]).then_inc(s["d_wa0"], 16)
            for u in range(UNITS):
                sp.dma_start(ctxT[:, u * 2 * S:(u + 1) * 2 * S],
                             a["ctxT"][:, u * 2 * S:(u + 1) * 2 * S]).then_inc(s[f"d_ctx{u}"], 16)
            sp.dma_start(gw[:, :], a["gw"]).then_inc(s["d_gw"], 16)
            sp.dma_start(gb[:, :], a["gb"]).then_inc(s["d_gw"], 16)
            sp.dma_start(b2e[:, :], a["b2e"]).then_inc(s["d_b2e"], 16)
            sp.wait_ge(s[f"g{UNITS - 1}"], 16)
            for e in range(RING):
                sp.dma_start(ew[:, e, :], a["ew"][:, e * 3 * D:(e + 1) * 3 * D]).then_inc(s[f"d_ew{e}"], 16)
            sp.dma_start(seg[:, :], a["seg"]).then_inc(s["d_seg"], 16)
            sp.dma_start(segrow[:, :], a["segrow"]).then_inc(s["d_segrow"], 16)
            sp.dma_start(near[:, :, :], a["ctxT"].rearrange("p (b s) -> p b s", b=B)[:, :, 0:NEAR]).then_inc(s["d_near"], 16)
            sp.dma_start(w1n[:, :, :], a["w1n"]).then_inc(s["d_wq"], 16)
            sp.dma_start(w2n[:, :], a["w2n"]).then_inc(s["d_wq"], 16)
            sp.dma_start(cs[:, :, :], a["cs"]).then_inc(s["d_cs"], 16)
            sp.dma_start(par[:, :, :], a["par"]).then_inc(s["d_par"], 16)
            sp.dma_start(wA[:, :], a["wA"][:, 0:WATT]).then_inc(s["d_wA"], 16)
            sp.dma_start(wF[:, :], a["wF"][:, 0:WFFN]).then_inc(s["d_wF"], 16)
            with sp.Fori(0, E // RING - 1) as i:
                for k in range(RING):
                    sp.wait_ge(s["y_done"], i * RING + (k + 1))
                    sp.dma_start(ew[:, k, :], a["ew"][:, bass.ds((i + 1) * (RING * 3 * D) + k * 3 * D, 3 * D)])\
                        .then_inc(s[f"d_ew{k}"], 16)
            sp.wait_ge(s["near_known"], 1)
            short = sp.value_load(near_i[0:1, 0:1], min_val=0, max_val=1)

            def contexts(l):
                with sp.Fori(0, B) as b:
                    sp.wait_ge(s["far_step"], l * (B + 1) + b + 1)
                    sp.dma_start(gx, a["ctxT"][:, bass.ds(b * S, S)]).then_inc(s["d_gx"], 16)

            def next_weights(l, attention_done, ffn_done, n):
                sp.wait_ge(s[attention_done], (l + 1) * n)
                sp.dma_start(wA[:, :], a["wA"][:, bass.ds((l + 1) * WATT, WATT)]).then_inc(s["d_wA"], 16)
                sp.wait_ge(s[ffn_done], (l + 1) * n)
                sp.dma_start(wF[:, :], a["wF"][:, bass.ds((l + 1) * WFFN, WFFN)]).then_inc(s["d_wF"], 16)

            with sp.If(short == 1):
                with sp.Fori(0, NL - 1) as l:
                    next_weights(l, "n_woc", "n_down", 2)
            with sp.If(short == 0):
                with sp.Fori(0, NL - 1) as l:
                    contexts(l)
                    next_weights(l, "n_woc", "n_down", 1)
                contexts(NL - 1)
            sp.wait_ge(s["out_ready"], 1)
            sp.dma_start(out, yt[:, :]).then_inc(s["d_out"], 16)
            sp.wait_ge(s["d_out"], 16)


        @block.gpsimd
        def _(pool):
            own = Chain(pool, s["pool_own"])
            pool.memset(onesD[:, :], 1.0 / D).then_inc(s["consts"], 1)
            pool.memset(eps[:, 0:1], 1e-5).then_inc(s["consts"], 1)
            pool.memset(eps[:, 1:2], 1e-6).then_inc(s["consts"], 1)
            own(pool.memset(eps[:, 2:3], 1e-10))
            pool.memset(ones1[:, :], 1.0).then_inc(s["consts"], 1)
            pool.memset(warm[:, :], 1.0).then_inc(s["warm_ready"], 1)
            own(pool.memset(ident[:, :], 0.0))
            pool.affine_select(out=ident[:, :], in_=ident[:, :], compare_op=ALU.not_equal, fill=1.0,
                               base=0, pattern=[[-1, D]], channel_multiplier=1).then_inc(s["consts"], 1)
            pool.wait_ge(s["consts"], 5)
            pool.tensor_copy(identb[:, :], ident[:, :]).then_inc(s["consts"], 1)
            pool.memset(qpT[:, T:T + 8], 0.0).then_inc(s["consts"], 1)
            pool.memset(Kz[:, :, :, :], 0.0).then_inc(s["consts"], 1)
            own(pool.memset(VB[:, :, :, :, :, :], 0.0))
            pool.wait_ge(s["d_vec"], 16)
            for gg in range(2):
                pool.tensor_copy(VB[:, :, :, :, gg, HV:CO].rearrange("p b g j c -> p (b g j) c"),
                                 vec[0:PB, V_ROW + gg:V_ROW + gg + 1].unsqueeze(1).broadcast_to([PB, 4 * B, 1]))\
                    .then_inc(s["consts"], 1)
            own(pool.memset(one[:, :], 1.0))
            own(pool.memset(fold[:, :], 0.0))
            for k in range(2):
                pool.affine_select(out=fold[:, :], in_=fold[:, :], compare_op=ALU.not_equal, fill=1.0, base=-k * L,
                                   pattern=[[-1, L]], channel_multiplier=1).then_inc(s["consts"], 1)
                pool.wait_ge(s["consts"], 11 + k)
            own(pool.iota(krow[:, :], pattern=[[1, NEAR]], base=0, channel_multiplier=0))
            own(pool.tensor_copy(krowf[:, :], krow[:, :]))
            pool.memset(gsplit[:, :, :], 0.0).then_inc(s["krow_ready"], 1)
            for u in range(UNITS):
                pool.wait_ge(s["rows_ready"], u + 1)
                pool.indirect_dma_start(out=mem[:, u, :], out_offset=None, in_=a["ctx"],
                                        in_offset=bass.IndirectOffsetOnAxis(ap=rows[:, u:u + 1], axis=0))\
                    .then_inc(s[f"g{u}"], 16)
            for u in range(UNITS):
                pool.wait_ge(s[f"g{u}"], 16)
            own(pool.memset(sel[:, :, :], 0.0))
            for k in range(3):
                own(pool.affine_select(out=sel[32 * k:32 * k + E, :, :], in_=sel[32 * k:32 * k + E, :, :],
                                       compare_op=ALU.not_equal, fill=1.0, base=0,
                                       pattern=[[-1, E], [0, D]], channel_multiplier=1))
            own(pool.iota(eio[:, :], pattern=[[1, E]], base=0, channel_multiplier=0))
            pool.tensor_copy(eiof[:, :], eio[:, :]).then_inc(s["consts"], 1)
            own(pool.memset(causal[:, :, :], 0.0))
            own(pool.memset(Kc[:, :, :, :], 0.0))
            own(pool.memset(Vc[:, :, :, :, :], 0.0))
            for g in range(GR):
                own(pool.memset(Vc[32 * g:32 * g + 32, :, :, g, HV:CO], 1.0))
            pool.iota(frow[:, :], pattern=[[1, SB]], base=0, channel_multiplier=0,
                      allow_small_or_imprecise_dtypes=True).then_inc(s["consts"], 1)
            own(pool.memset(cz[:, :, :], 0.0))
            own(pool.affine_select(out=cz[:, 0, :], in_=cz[:, 0, :], compare_op=ALU.is_ge, fill=NEG,
                                   base=0, pattern=[[-1, L]], channel_multiplier=1))
            own(pool.affine_select(out=cz[:, 1, :], in_=cz[:, 1, :], compare_op=ALU.is_ge, fill=NEG,
                                   base=-L, pattern=[[-1, L]], channel_multiplier=1))
            own(pool.tensor_scalar(cz[:, 2, :], cz[:, 1, :], vec[0:PB, V_ROW + 1:V_ROW + 2], None, ALU.mult))
            own(pool.tensor_tensor(cz[:, 3, :], cz[:, 0, :], cz[:, 2, :], ALU.add))
            pool.tensor_copy(causal[:, :, :], cz[:, 3, :].unsqueeze(1).broadcast_to([PB, 8, L]))\
                .then_inc(s["consts"], 1)

            pool.wait_ge(s["d_near"], 16)
            pool.wait_ge(s["x_ready"], 2)
            pool.tensor_copy(near4[:, :, :, :], near[:, :, :].unsqueeze(2).broadcast_to([D, B, GR, NEAR]))\
                .then_inc(s["near_ready"], 1)
            pool.wait_ge(s["near_known"], 1)
            short = pool.value_load(near_i[0:1, 0:1], min_val=0, max_val=1)

            def doubled(hf):
                pool.tensor_tensor(hd[:, hf * HB:(hf + 1) * HB, :, :],
                                   heads3(h[:, :])[:, hf * HB:(hf + 1) * HB, :].unsqueeze(2).broadcast_to([D, HB, 2, L]),
                                   one[:, :].unsqueeze(2).unsqueeze(3).broadcast_to([D, HB, 2, L]),
                                   ALU.mult).then_inc(s["n_hd"], 1)

            with pool.If(short == 1):
                with pool.Fori(0, NL) as l:
                    pool.wait_ge(s["n_h"], l * 6 + 1)
                    doubled(0)
                    pool.wait_ge(s["n_h"], l * 6 + 2)
                    doubled(1)
                    pool.wait_ge(s["n_q"], l + 1)
                    pool.tensor_tensor(Q4[:, HB:B, :, :],
                                       heads3(qk[:, 0, :])[:, HB:B, :].unsqueeze(2).broadcast_to([D, HB, HG, L]),
                                       colv(V_SEL, HG).unsqueeze(1).unsqueeze(3).broadcast_to([D, HB, HG, L]),
                                       ALU.mult).then_inc(s["n_q4"], 1)
            with pool.If(short == 0):
                with pool.Fori(0, NL) as l:
                    pool.wait_ge(s["norm_ready"], l * 3 + 5)
                    doubled(0)
                    doubled(1)

        @block.tensor
        def _(pe):
            def mm1(dst, w, x, start=True, stop=True):
                return nc.tensor.matmul(dst, w, x, start=start, stop=stop)

            def stay_warm(n, bank=5):
                for _ in range(n):
                    mm1(PS[:, bank, 0:8 * L], identb[:, :], warm[:, :])

            def mean(i, src):
                mm1(PS[:, 6, 0:T], onesD[:, :], src).then_inc(s["mean_ready"], 1)

            def mean_square(i):
                stay_warm(WARM_SQ)
                pe.wait_ge(s["sq_ready"], i + 1)
                mm1(PS[:, 7, 0:T], onesD[:, :], sq[:, :]).then_inc(s["ms_ready"], 1)
                stay_warm(WARM_NORM)

            def scores(r, b, masked, l=None):
                if l is not None and b == 0:
                    pe.wait_ge(s["q4_ready"], l + 2)
                    pe.wait_ge(s["n_kz"], l * 2 + 1)
                if not masked and b == HB:
                    pe.wait_ge(s["kz_ready"], 2)
                if l is not None and b == HB:
                    pe.wait_ge(s["n_q4"], l + 1)
                    pe.wait_ge(s["n_kz"], l * 2 + 2)
                if b >= 2:
                    pe.wait_ge(s["sub_done"], r * B + (b - 1))
                if masked:
                    mm1(PS[0:PB, b % 2, 0:8 * L], identb[0:PB, 0:PB],
                        causal[:, :, :].rearrange("p c l -> p (c l)"), stop=False)
                for jp in range(2):
                    last = mm1(PS[0:PB, b % 2, jp * GR * L:(jp + 1) * GR * L],
                               Q4[:, b, 2 * jp:2 * jp + 2, :].rearrange("p j l -> p (j l)"),
                               Kz[:, b, :, :].rearrange("p g l -> p (g l)"),
                               start=not masked, stop=not masked or jp == 1)
                last.then_inc(s["s_ready"], 1)

            def turn(r, b, masked=True):
                if b == 0 and masked:
                    pe.wait_ge(s["vb_ready"], r + 2)
                pe.wait_ge(s["exp_done"], r * B + (b + 1))
                if b >= 2:
                    pe.wait_ge(s["pt_ready"], r * B + (b - 1))
                for jp in range(2):
                    for G in range(2):
                        src = P[:, b // 2 % 2, b % 2, jp * GR + 2 * G:jp * GR + 2 * G + 2, :]
                        last = nc.tensor.transpose(PS[0:PB, 2 + b % 2, (jp * 2 + G) * PB:(jp * 2 + G + 1) * PB],
                                                   src.rearrange("p g l -> p (g l)"), ident[0:PB, 0:PB])
                last.then_inc(s["turned"], 1)

            def values(r, b, masked=True):
                if not masked and b % HB == 0:
                    pe.wait_ge(s["vb_ready"], b // HB + 1)
                pe.wait_ge(s["pt_ready"], r * B + (b + 1))
                if b >= 2:
                    pe.wait_ge(s["o_ready"], r * B + (b - 1))
                for G in range(2):
                    for jp in range(2):
                        at = (G * GR + jp) * CO
                        last = mm1(PS[0:PB, 4 + b % 2, at - jp * CO:at - jp * CO + 4 * CO]
                                   .rearrange("p (g j c) -> p g j c", g=2, j=2)[:, :, jp, :],
                                   PT[:, b // 2 % 2, b % 2, jp * 2 + G, :], VB[:, b, G, jp, :, :])
                last.then_inc(s["pv_done"], 1)

            def turn_back(r, b):
                pe.wait_ge(s["on_ready"], r * B + (b + 1))
                mm1(PS[:, 4 + b % 2, 300:300 + L], O[:, b // 2 % 2, b % 2, :], fold[:, :]).then_inc(s["ot_done"], 1)

            def turn_memory(hf):
                if hf == 1:
                    pe.wait_ge(s["vb_ready"], 1)
                for u in range(2 * hf, 2 * hf + 2):
                    pe.wait_ge(s[f"g{u}"], 16)
                    last = nc.tensor.transpose(PS[:, 6, (u % 2) * D:(u % 2 + 1) * D], mem[:, u, :], ident[:, :])
                last.then_inc(s["mem_turned"], 1)

            def memory_products(hf):
                if hf == 1:
                    pe.wait_ge(s["kz_ready"], 1)
                pe.wait_ge(s["memT_ready"], hf + 1)
                mm1(PS[:, 7, 0:HT], wa0[:, D:2 * D], memD[:, hf * HB:(hf + 1) * HB, 0, :]).then_inc(s["kv_done"], 1)
                for b in range(HB):
                    last = mm1(PS[0:PB, 6, b * D:(b + 1) * D],
                               memD[:, hf * HB + b, :, :].rearrange("p k l -> p (k l)"), wa0[:, 2 * D:3 * D])
                last.then_inc(s["kv_done"], 1)

            def attention_start(r, masked, l=None):
                scores(r, 0, masked, l)
                scores(r, 1, masked, l)
                turn(r, 0, masked)
                scores(r, 2, masked, l)
                if not masked:
                    turn_memory(1)
                turn(r, 1, masked)
                values(r, 0, masked)
                scores(r, 3, masked, l)
                if not masked:
                    memory_products(1)
                turn(r, 2, masked)
                values(r, 1, masked)
                turn_back(r, 0)
                scores(r, 4, masked, l)
                turn(r, 3, masked)
                values(r, 2, masked)
                turn_back(r, 1)
                scores(r, 5, masked, l)
                turn(r, 4, masked)
                values(r, 3, masked)
                turn_back(r, 2)
                scores(r, 6, masked, l)
                turn(r, 5, masked)
                values(r, 4, masked)
                turn_back(r, 3)
                scores(r, 7, masked, l)
                turn(r, 6, masked)
                values(r, 5, masked)
                turn_back(r, 4)

            def attention(r, masked):
                attention_start(r, masked)
                turn(r, 7, masked)
                values(r, 6, masked)
                turn_back(r, 5)
                values(r, 7, masked)
                turn_back(r, 6)
                turn_back(r, 7)

            pe.wait_ge(s["consts"], 6)
            pe.wait_ge(s["warm_ready"], 1)
            pe.wait_ge(s["d_x"], 16)
            mean(0, xin[:, :])
            pe.wait_ge(s["d_wa0"], 16)
            pe.wait_ge(s["xc_ready"], 1)
            mm1(PS[:, 2, 0:T], wa0[:, 0:D], xc[:, :]).then_inc(s["qp_done"], 1)
            pe.wait_ge(s["sq_ready"], 1)
            mm1(PS[:, 7, 0:T], onesD[:, :], sq[:, :]).then_inc(s["ms_ready"], 1)

            def candidates(u):
                pe.wait_ge(s[f"d_ctx{u}"], 16)
                if u >= 2:
                    pe.wait_ge(s["rows_ready"], u - 1)
                for c in range(3):
                    n = min(512, S - c * 512)
                    for k in range(2):
                        b = 2 * u + k
                        last = mm1(PS[64 * k:64 * k + 64, 3 * (u % 2) + c, 0:n], qpT[:, b * L:b * L + 64],
                                   ctxT[:, b * S + c * 512:b * S + c * 512 + n])
                last.then_inc(s["cand_scores"], 1)

            pe.wait_ge(s["consts"], 7)
            pe.wait_ge(s["qp_copied"], 1)
            candidates(0)
            candidates(1)
            candidates(2)
            candidates(3)
            turn_memory(0)
            memory_products(0)
            pe.wait_ge(s["rows_ready"], UNITS)
            pe.wait_ge(s["q4_ready"], 1)
            pe.wait_ge(s["kz_ready"], 1)
            attention(0, False)
            pe.wait_ge(s["o_ready"], B)
            mm1(PS[:, 0, 0:T], wa0[:, 3 * D:4 * D], o[:, :]).then_inc(s["wo_done"], 1)

            pe.wait_ge(s["x_ready"], 1)
            mean(1, x1[:, :])
            mean_square(1)
            pe.wait_ge(s["norm_ready"], 2)
            pe.wait_ge(s["d_gw"], 32)
            for u in range(UNITS):
                last = mm1(PS[0:PB, 7, u * E:(u + 1) * E], h[:, u * PB:(u + 1) * PB], gw[:, :])
            last.then_inc(s["gate_done"], 1)
            def expert_up(e, k, i, first, route=True):
                bank = 3 * (k % 2)
                reused = not first or k >= 2
                pe.wait_ge(s[f"d_ew{k % RING}"], (i + 1) * 16)
                if reused:
                    pe.wait_ge(s["g1_ready"], e - 1)
                mm1(PS[:, bank, 0:T], ew[:, k % RING, 0:D], h[:, :]).then_inc(s["e_gate"], 1)
                if reused:
                    pe.wait_ge(s["l1_ready"], e - 1)
                mm1(PS[:, bank + 1, 0:T], ew[:, k % RING, D:2 * D], h[:, :])
                if reused:
                    pe.wait_ge(s["ww_ready"], e - 1)
                if route:
                    expert_route(e, k)

            def expert_route(e, k):
                mm1(PS[:, 3 * (k % 2) + 2, 0:T], sel[:, bass.ds(e, 1), :].rearrange("p e d -> p (e d)"), rb[:, :])\
                    .then_inc(s["e_glr"], 1)

            expert_up(0, 0, 0, True, route=False)
            expert_up(1, 1, 0, True, route=False)
            pe.wait_ge(s["route_ready"], 1)
            for u in range(UNITS):
                last = mm1(PS[0:96, 7, u * PB:(u + 1) * PB], gsplit[:, u, :], identb[0:PB, 0:PB])
            last.then_inc(s["route_turned"], 1)
            for u in range(UNITS):
                last = nc.tensor.transpose(PS[0:E, 6, u * PB:(u + 1) * PB], ge[:, u, :], ident[0:PB, 0:PB])
            last.then_inc(s["route_turned"], 1)
            pe.wait_ge(s["rb_ready"], 1)
            expert_route(0, 0)
            expert_route(1, 1)
            pe.wait_ge(s["rb_ready"], 2)
            pe.wait_ge(s["d_b2e"], 16)
            mm1(PS[:, 6, 0:T], b2e[:, :], routeT[:, :], stop=False)

            def expert_down(e, k, stop=False):
                pe.wait_ge(s["zz_ready"], e + 1)
                mm1(PS[:, 6, 0:T], ew[:, k, 2 * D:3 * D], zz[:, k % 2, :], start=False, stop=stop)\
                    .then_inc(s["y_done"], 1)

            for k in range(RING):
                expert_up(k + 2, (k + 2) % RING, (k + 2) // RING, k + 2 < RING)
                expert_down(k, k)
            with pe.Fori(1, E // RING - 1) as i:
                for k in range(RING):
                    expert_up(i * RING + (k + 2), (k + 2) % RING, i + (k + 2) // RING, False)
                    expert_down(i * RING + k, k)
            for k in range(RING):
                e = E - RING + k
                if k + 2 < RING:
                    expert_up(e + 2, k + 2, E // RING - 1, False)
                expert_down(e, k, stop=e == E - 1)

            pe.wait_ge(s["x_ready"], 2)
            mean(2, x2[:, :])
            mean_square(2)
            pe.wait_ge(s["consts"], 15)
            pe.wait_ge(s["xbias_ready"], 1)
            pe.wait_ge(s["near_known"], 1)
            short = pe.value_load(near_i[0:1, 0:1], min_val=0, max_val=1)

            def cross_long(l):
                with pe.Fori(0, B) as b:
                    pe.wait_ge(s["far_step"], l * (B + 1) + b + 1)
                    lb = l * B + b
                    pe.wait_ge(s["d_gx"], (lb + 1) * 16)
                    for c in range(3):
                        mm1(PS[:, c, 0:SB], wA[:, WKC:WKC + D], gx[:, c * SB:(c + 1) * SB])
                        last = mm1(PS[:, 3 + c, 0:SB], wA[:, WVC:WVC + D], gx[:, c * SB:(c + 1) * SB])
                    last.then_inc(s["far_kv"], 1)
                    pe.wait_ge(s["gv_ready"], lb + 1)
                    for c in range(NK):
                        last = nc.tensor.transpose(PS[0:KC, 3 + c // 4, (c % 4) * D:(c % 4 + 1) * D],
                                                   gv[:, c * KC:(c + 1) * KC], ident[:, :])
                    last.then_inc(s["far_vt"], 1)
                    with pe.Fori(0, H) as hh_:
                        t = lb * H + hh_
                        pe.wait_ge(s["gq_ready"], t + 1)
                        for c in range(3):
                            last = mm1(PS[0:L, c, 0:SB], gqz, gk[:, c * SB:(c + 1) * SB])
                        last.then_inc(s["fs_ready"], 1)
                        pe.wait_ge(s["fe_ready"], t + 1)
                        for c in range(NK):
                            last = mm1(PS[0:KC, 6 + c // 8, (c % 8) * 64:(c % 8) * 64 + L],
                                       gp[:, c * KC:(c + 1) * KC], ident[0:L, 0:L])
                        last.then_inc(s["ft_ready"], 1)
                        pe.wait_ge(s["gV_ready"], lb + 1)
                        pe.wait_ge(s["fpt_ready"], t + 1)
                        for c in range(NK):
                            last = mm1(PS[0:L, 3, 0:DH], gPT[:, c, :], gV[:, c, bass.ds(hh_ * DH, DH)],
                                       start=c == 0, stop=c == NK - 1)
                        last.then_inc(s["fo_ready"], 1)
                    pe.wait_ge(s["fO_ready"], lb + 1)
                    mm1(PS[:, 4, 0:L], gOc, ident[0:L, 0:L]).then_inc(s["ff_ready"], 1)

            def half_product(bank, w, src, hf, ready):
                mm1(PS[:, bank, hf * HT:(hf + 1) * HT], w, src[:, hf * HT:(hf + 1) * HT]).then_inc(s[ready], 1)

            def near_value_products(b0):
                pe.wait_ge(s["near_ready"], 1)
                for b in range(b0, b0 + HB):
                    last = mm1(PS[:, b // 4, (b % 4) * D:(b % 4 + 1) * D],
                               near4[:, b, :, :].rearrange("p g k -> p (g k)"), wA[:, WVC:WVC + D])
                return last

            def half_mean_square(n, hf):
                pe.wait_ge(s["n_sq"], n + 1)
                if hf == 1:
                    pe.wait_ge(s["n_ln"], n)
                half_product(7, onesD[:, :], sq, hf, "n_ms")

            def near_scores(l, u):
                if u % 2 == 0:
                    pe.wait_ge(s["n_q4c"], l * 2 + (u // 2 + 1))
                if u == 0:
                    pe.wait_ge(s["ckv_ready"], l * 2 + 2)
                if u >= 2:
                    pe.wait_ge(s["csub_done"], l * UNITS + (u - 1))
                mm1(PS[0:PB, u % 2, :], identb[0:PB, 0:PB],
                    xbias[:, 2 * u:2 * u + 2, :].unsqueeze(2).broadcast_to([PB, 2, 2, GR * NEAR]), stop=False)
                for k in range(2):
                    for jp in range(2):
                        b, col = 2 * u + k, (2 * k + jp) * GR * NEAR
                        last = mm1(PS[0:PB, u % 2, col:col + GR * NEAR],
                                   Q4c[:, b, 2 * jp:2 * jp + 2, :].rearrange("p j l -> p (j l)"),
                                   Kc[:, b, :, :].rearrange("p g k -> p (g k)"),
                                   start=False, stop=k + jp == 2)
                last.then_inc(s["cs_ready"], 1)

            def near_turn(l, u):
                pe.wait_ge(s["cexp_done"], l * UNITS + (u + 1))
                if u >= 2:
                    pe.wait_ge(s["cpt_ready"], l * UNITS + (u - 1))
                for c in range(4):
                    last = nc.tensor.transpose(PS[:, 2 + u % 2, c * PB:(c + 1) * PB],
                                               Pc[:, u, GR * c:GR * c + GR, :].rearrange("p g k -> p (g k)"),
                                               ident[0:PB, 0:PB])
                last.then_inc(s["cturned"], 1)

            def near_values(l, u):
                pe.wait_ge(s["cpt_ready"], l * UNITS + (u + 1))
                if u >= 2:
                    pe.wait_ge(s["near_out"], l * UNITS + (u - 1))
                for k in range(2):
                    for jp in range(2):
                        at = k * 2 * GR * CO
                        last = mm1(PS[0:PB, 4 + u % 2, at:at + 8 * CO]
                                   .rearrange("p (g j c) -> p g j c", g=GR, j=2)[:, :, jp, :],
                                   PTc[:, u, 2 * k + jp, :], Vc[:, 2 * u + k, jp, :, :])
                last.then_inc(s["cpv_done"], 1)

            def near_turn_back(l, u):
                pe.wait_ge(s["con_ready"], l * UNITS + (u + 1))
                for k in range(2):
                    last = mm1(PS[:, 4 + u % 2, 300 + k * L:300 + (k + 1) * L], O[:, u % 2, k, :], fold[:, :])
                last.then_inc(s["cot_done"], 1)

            def ffn_up(l, i):
                hf, c = i // FC, i % FC
                if c == 0:
                    pe.wait_ge(s["n_h"], l * 6 + (5 + hf))
                if i >= 2:
                    pe.wait_ge(s["n_m"], l * 2 * FC + (i - 1))
                x = h[:, hf * HT:(hf + 1) * HT]
                mm1(PS[:, i % 2, 0:HT], wF[:, WG + c * D:WG + (c + 1) * D], x)
                mm1(PS[:, 2 + i % 2, 0:HT], wF[:, WU + c * D:WU + (c + 1) * D], x).then_inc(s["n_up"], 1)

            def ffn_down(l, i):
                hf, c = i // FC, i % FC
                pe.wait_ge(s["n_m"], l * 2 * FC + (i + 1))
                last = mm1(PS[:, 4 + hf, hf * HT:(hf + 1) * HT], wF[:, WD + c * D:WD + (c + 1) * D],
                           mm[:, c, hf * HT:(hf + 1) * HT], start=c == 0, stop=c == FC - 1)
                if c == FC - 1:
                    last.then_inc(s["n_down"], 1)

            with pe.If(short == 1):
                half_mean_square(0, 0)
                with pe.Fori(0, NL) as l:
                    pe.wait_ge(s["d_wA"], (l + 1) * 16)
                    mm1(PS[:, 0, 0:B * NEAR], wA[:, WKC:WKC + D], near[:, :, :].rearrange("p b k -> p (b k)"))
                    pe.wait_ge(s["pl_ready"], l + 1)
                    mm1(PS[:, 1, 0:1], wA[:, WO:WO + D], pl[:, BV:BV + 1]).then_inc(s["ckv_done"], 1)
                    half_mean_square(l * 6 + 1, 1)
                    for hf in range(2):
                        pe.wait_ge(s["n_h"], l * 6 + (hf + 1))
                        for i, pair in enumerate(((WK, WKR), (WQ, WQR))):
                            for j, w in enumerate(pair):
                                last = mm1(PS[:, 4 + 2 * hf + i, j * HT:(j + 1) * HT], wA[:, w:w + D],
                                           h[:, hf * HT:(hf + 1) * HT])
                            last.then_inc(s["n_proj"], 1)
                        pe.wait_ge(s["n_hd"], l * 2 + (hf + 1))
                        for b in range(hf * HB, (hf + 1) * HB):
                            last = mm1(PS[0:PB, 2 + b // 4, (b % 4) * D:(b % 4 + 1) * D],
                                       hd[:, b, :, :].rearrange("p k l -> p (k l)"), wA[:, WV:WV + D])
                    last.then_inc(s["proj_done"], 1)
                    pe.wait_ge(s["ckv_ready"], l * 2 + 1)
                    pe.wait_ge(s["bo_ready"], l + 1)
                    stay_warm(WARM_SCORES, 1)
                    r = l + 1
                    attention_start(r, True, l)
                    half_product(6, wA[:, WO:WO + D], o, 0, "n_wo")
                    turn(r, 7)
                    near_value_products(0)
                    values(r, 6)
                    turn_back(r, 5)
                    half_mean_square(l * 6 + 2, 0)
                    near_value_products(HB).then_inc(s["ckv_done"], 1)
                    values(r, 7)
                    turn_back(r, 6)
                    pe.wait_ge(s["n_h"], l * 6 + 3)
                    half_product(7, wA[:, WQC:WQC + D], h, 0, "n_qc")
                    turn_back(r, 7)
                    pe.wait_ge(s["o_ready"], r * B + B)
                    half_product(6, wA[:, WO:WO + D], o, 1, "n_wo")
                    near_scores(l, 0)
                    near_scores(l, 1)
                    half_mean_square(l * 6 + 3, 1)
                    near_turn(l, 0)
                    stay_warm(WARM_HALF, 6)
                    pe.wait_ge(s["n_h"], l * 6 + 4)
                    half_product(7, wA[:, WQC:WQC + D], h, 1, "n_qc")
                    near_turn(l, 1)
                    near_values(l, 0)
                    near_scores(l, 2)
                    near_values(l, 1)
                    near_turn_back(l, 0)
                    near_scores(l, 3)
                    near_turn(l, 2)
                    near_turn_back(l, 1)
                    stay_warm(WARM_OUT, 7)
                    near_turn(l, 3)
                    pe.wait_ge(s["near_out"], l * UNITS + 2)
                    half_product(6, wA[:, WOC:WOC + D], o, 0, "n_woc")
                    near_values(l, 2)
                    half_mean_square(l * 6 + 4, 0)
                    near_values(l, 3)
                    near_turn_back(l, 2)
                    near_turn_back(l, 3)
                    stay_warm(WARM_OUT, 2)
                    pe.wait_ge(s["near_out"], l * UNITS + 4)
                    half_product(6, wA[:, WOC:WOC + D], o, 1, "n_woc")
                    pe.wait_ge(s["d_wF"], (l + 1) * 16)
                    ffn_up(l, 0)
                    half_mean_square(l * 6 + 5, 1)
                    ffn_up(l, 1)
                    stay_warm(WARM_FFN, 5)
                    for i in range(2, 2 * FC):
                        ffn_down(l, i - 2)
                        ffn_up(l, i)
                    half_mean_square(l * 6 + 6, 0)
                    ffn_down(l, 6)
                    ffn_down(l, 7)

            with pe.If(short == 0):
                with pe.Fori(0, NL) as l:
                    mean_square(l * 3 + 3)
                    pe.wait_ge(s["norm_ready"], l * 3 + 5)
                    pe.wait_ge(s["d_wA"], (l + 1) * 16)
                    for i, w in enumerate((WQ, WQR, WK, WKR)):
                        mm1(PS[:, 4 + i, 0:T], wA[:, w:w + D], h[:, :]).then_inc(s["n_proj"], 1)
                    pe.wait_ge(s["n_hd"], l * 2 + 2)
                    for b in range(B):
                        last = mm1(PS[0:PB, 2 + b // 4, (b % 4) * D:(b % 4 + 1) * D],
                                   hd[:, b, :, :].rearrange("p k l -> p (k l)"), wA[:, WV:WV + D])
                    last.then_inc(s["proj_done"], 1)
                    pe.wait_ge(s["pl_ready"], l + 1)
                    mm1(PS[:, 1, 0:1], wA[:, WO:WO + D], pl[:, BV:BV + 1]).then_inc(s["ckv_done"], 1)
                    pe.wait_ge(s["bo_ready"], l + 1)
                    pe.wait_ge(s["q4_ready"], l + 2)
                    pe.wait_ge(s["kz_ready"], l + 3)
                    attention(l + 1, True)
                    pe.wait_ge(s["o_ready"], (l + 1) * B + B)
                    mm1(PS[:, 0, 0:T], wA[:, WO:WO + D], o[:, :]).then_inc(s["wo_done"], 1)
                    mean_square(l * 3 + 4)
                    pe.wait_ge(s["norm_ready"], l * 3 + 6)
                    mm1(PS[:, 1, 0:T], wA[:, WQC:WQC + D], h[:, :]).then_inc(s["n_qc"], 1)
                    cross_long(l)
                    pe.wait_ge(s["oc_ready"], l + 1)
                    mm1(PS[:, 0, 0:T], wA[:, WOC:WOC + D], o[:, :]).then_inc(s["n_woc"], 1)
                    mean_square(l * 3 + 5)
                    pe.wait_ge(s["norm_ready"], l * 3 + 7)
                    pe.wait_ge(s["d_wF"], (l + 1) * 16)
                    for c in range(FC):
                        if c >= 2:
                            pe.wait_ge(s["n_m"], l * FC + (c - 1))
                        mm1(PS[:, 2 * (c % 2), 0:T], wF[:, WG + c * D:WG + (c + 1) * D], h[:, :])\
                            .then_inc(s["g_done"], 1)
                        mm1(PS[:, 2 * (c % 2) + 1, 0:T], wF[:, WU + c * D:WU + (c + 1) * D], h[:, :])\
                            .then_inc(s["u_done"], 1)
                    for c in range(FC):
                        pe.wait_ge(s["n_m"], l * FC + (c + 1))
                        last = mm1(PS[:, 4, 0:T], wF[:, WD + c * D:WD + (c + 1) * D], mm[:, c, :],
                                   start=c == 0, stop=c == FC - 1)
                    last.then_inc(s["n_down"], 1)
            pe.wait_ge(s["sq_last"], 1)
            mm1(PS[:, 7, 0:T], onesD[:, :], sq[:, :]).then_inc(s["ms_last"], 1)

            pe.wait_ge(s["wq_ready"], 1)
            for c in range(FC):
                nc.tensor.transpose(PS[:, 0, c * 64:(c + 1) * 64].bitcast(BF16), wqb[:, 0, c * D:(c + 1) * D],
                                    identb[:, :])
            for c in range(FC):
                last = nc.tensor.transpose(PS[:, 1, c * 64:(c + 1) * 64].bitcast(BF16),
                                           wqb[:, 1, c * D:(c + 1) * D], identb[:, :])
            last.then_inc(s["wq_turned"], 1)

            stay_warm(WARM_LAST)
            pe.wait_ge(s["layers_done"], 2)
            mean(3, x3[:, :])
            stay_warm(WARM_SQ)
            pe.wait_ge(s["sq_last"], 2)
            mm1(PS[:, 7, 0:T], onesD[:, :], sq[:, :]).then_inc(s["ms_last"], 1)

            def largest(i):
                pe.wait_ge(s["max_in"], i + 1)
                nc.tensor.transpose(PS[0:1, 5, 0:D], s11[:, 0:1], ident[:, :]).then_inc(s["max_turned"], 1)
                pe.wait_ge(s["s_one"], i + 1)
                mm1(PS[:, 4, 0:1], ones1[:, :], s11[0:1, 2:3]).then_inc(s["s_bcast"], 1)

            largest(0)
            pe.wait_ge(s["yq_ready"], 1)
            pe.wait_ge(s["wqT_ready"], 1)
            for c in range(FC):
                mm1(PS[:, c, 0:T], w1qT[:, c * D:(c + 1) * D], yq[:, :]).then_inc(s["up_done"], 1)
            largest(1)
            for c in range(FC):
                pe.wait_ge(s["hq_ready"], c + 1)
                last = mm1(PS[:, 6, 0:T], w2qT[:, c, :], hq[:, c, :], start=c == 0, stop=c == FC - 1)
            last.then_inc(s["down_done"], 1)

        @block.scalar
        def _(act):
            def fn(dst, src, f, **kw):
                return nc.scalar.activation(dst, src, f, **kw)

            def norm(i, src, e, extra=0):
                fn(sq[:, :], src, ACT.Square).then_inc(s["sq_ready"], 1)
                act.wait_ge(s["ms_ready"], i + 1)
                fn(rs[:, :], PS[:, 7, 0:T], ACT.Ln, bias=eps[:, e:e + 1]).then_inc(s["ln_done"], 1)
                act.wait_ge(s["ln_done"], i + 1 + extra)
                fn(rs[:, :], rs[:, :], ACT.Exp, scale=-0.5).then_inc(s["rstd_ready"], 1)

            def values_out(r):
                v = PS[0:PB, 2:4, :].rearrange("p k (b c) -> p (k b) c", c=D)
                for gg in range(2):
                    last = fn(VB[:, :, :, :, gg, 0:HV].rearrange("p b g j c -> p (b g) j c"),
                              v.rearrange("p b (g h c) -> p (b g) h c", g=2, h=4)[:, :, 2 * gg:2 * gg + 2, :],
                              ACT.Copy, scale=vec[0:PB, V_ROW + gg:V_ROW + gg + 1])
                last.then_inc(s["vb_ready"], 1)

            def keys_out(src):
                for g in range(GR):
                    last = fn(Kz[32 * g:32 * g + 32, :, g, :], heads3(src[32 * g:32 * g + 32]), ACT.Copy)
                last.then_inc(s["kz_ready"], 1)

            def exps(r, b):
                act.wait_ge(s["sub_done"], r * B + (b + 1))
                v = P[:, b // 2 % 2, b % 2, :, :].rearrange("p c l -> p (c l)")
                fn(v, v, ACT.Exp, scale=SCALE).then_inc(s["exp_done"], 1)

            def evac(r, b):
                act.wait_ge(s["turned"], r * B + (b + 1))
                if b >= 4:
                    act.wait_ge(s["pv_done"], r * B + (b - 3))
                fn(PT[:, b // 2 % 2, b % 2, :, :].rearrange("p c q -> p (c q)"), PS[0:PB, 2 + b % 2, 0:4 * PB],
                   ACT.Copy).then_inc(s["pt_ready"], 1)

            def out_part(r, b):
                act.wait_ge(s["ot_done"], r * B + (b + 1))
                fn(o[:, b * L:(b + 1) * L], PS[:, 4 + b % 2, 300:300 + L], ACT.Copy).then_inc(s["o_ready"], 1)

            def memory_out(hf):
                act.wait_ge(s["mem_turned"], hf + 1)
                fn(memD[:, hf * HB:(hf + 1) * HB, :, :],
                   PS[:, 6, 0:2 * D].rearrange("p (b l) -> p b l", b=HB)[:, :, 0:L].unsqueeze(2)
                   .broadcast_to([D, HB, 2, L]), ACT.Copy).then_inc(s["memT_ready"], 1)

            def memory_keys_values_out(hf):
                rows_ = slice(hf * HB, (hf + 1) * HB)
                act.wait_ge(s["kv_done"], 2 * hf + 1)
                for g in range(GR):
                    last = fn(Kz[32 * g:32 * g + 32, rows_, g, :],
                              PS[32 * g:32 * g + 32, 7, 0:HT].rearrange("p (b l) -> p b l", b=HB), ACT.Copy)
                last.then_inc(s["kz_ready"], 1)
                act.wait_ge(s["kv_done"], 2 * hf + 2)
                v = PS[0:PB, 6, :].rearrange("p (b g h c) -> p (b g) h c", b=HB, g=2, h=4)
                for gg in range(2):
                    last = fn(VB[:, rows_, :, :, gg, 0:HV].rearrange("p b g j c -> p (b g) j c"),
                              v[:, :, 2 * gg:2 * gg + 2, :], ACT.Copy, scale=vec[0:PB, V_ROW + gg:V_ROW + gg + 1])
                last.then_inc(s["vb_ready"], 1)

            def attention_start(r, stage_a=False):
                exps(r, 0)
                exps(r, 1)
                evac(r, 0)
                exps(r, 2)
                if stage_a:
                    memory_out(1)
                evac(r, 1)
                exps(r, 3)
                if stage_a:
                    memory_keys_values_out(1)
                evac(r, 2)
                out_part(r, 0)
                exps(r, 4)
                evac(r, 3)
                out_part(r, 1)
                exps(r, 5)
                evac(r, 4)
                out_part(r, 2)
                exps(r, 6)
                evac(r, 5)
                out_part(r, 3)
                exps(r, 7)
                evac(r, 6)

            def attention(r):
                attention_start(r)
                out_part(r, 4)
                evac(r, 7)
                out_part(r, 5)
                out_part(r, 6)
                out_part(r, 7)

            act.preload_act_table_set("natural_log_exp_and_others")
            act.wait_ge(s["consts"], 6)
            act.wait_ge(s["xc_ready"], 1)
            fn(sq[:, :], xc[:, :], ACT.Square).then_inc(s["sq_ready"], 1)
            act.wait_ge(s["qp_done"], 1)
            fn(qpT[:, 0:T], PS[:, 2, 0:T], ACT.Copy).then_inc(s["qp_copied"], 1)
            act.wait_ge(s["ms_ready"], 1)
            fn(rs[:, :], PS[:, 7, 0:T], ACT.Ln, bias=eps[:, 0:1]).then_inc(s["ln_done"], 1)
            act.wait_ge(s["ln_done"], 1)
            fn(rs[:, :], rs[:, :], ACT.Exp, scale=-0.5).then_inc(s["rstd_ready"], 1)
            act.wait_ge(s["consts"], 12)
            act.wait_ge(s["d_vec"], 16)

            memory_out(0)
            memory_keys_values_out(0)
            attention_start(0, True)
            out_part(0, 4)
            evac(0, 7)
            out_part(0, 5)
            out_part(0, 6)
            out_part(0, 7)
            act.wait_ge(s["xc_ready"], 2)
            fn(sq[:, :], xc[:, :], ACT.Square).then_inc(s["sq_ready"], 1)
            act.wait_ge(s["ms_ready"], 2)
            fn(tq[:, 0, :], PS[:, 7, 0:T], ACT.Ln, scale=1.0 + 1e-5, bias=eps[:, 2:3]).then_inc(s["ln_done"], 1)
            fn(rs[:, :], PS[:, 7, 0:T], ACT.Ln, bias=eps[:, 0:1]).then_inc(s["ln_done"], 1)
            act.wait_ge(s["ln_done"], 2)
            fn(tq[:, 1, :], tq[:, 0, :], ACT.Exp, scale=-0.5).then_inc(s["rstd_ready"], 1)
            act.wait_ge(s["ln_done"], 3)
            fn(rs[:, :], rs[:, :], ACT.Exp, scale=-0.5).then_inc(s["rstd_ready"], 1)
            act.wait_ge(s["gexp_in"], 1)
            fn(ge[:, :, :], ge[:, :, :], ACT.Exp).then_inc(s["gexp_done"], 1)

            def expert(e, k, first):
                bank = 3 * (k % 2)
                act.wait_ge(s["e_gate"], e + 1)
                if not first or k >= 2:
                    act.wait_ge(s["zz_ready"], e - 1)
                fn(xg[:, k % 2, :], PS[:, bank, 0:T], ACT.Identity,
                   bias=vec[:, bass.ds(e + V_B1G, 1)]).then_inc(s["g1_ready"], 1)
                act.wait_ge(s["e_glr"], e + 1)
                fn(l1[:, k % 2, :], PS[:, bank + 1, 0:T], ACT.Identity,
                   bias=vec[:, bass.ds(e + V_B1L, 1)]).then_inc(s["l1_ready"], 1)
                act.wait_ge(s["xg_ready"], e + 1)
                fn(sg[:, k % 2, :], xg[:, k % 2, :], ACT.Sigmoid, scale=ALPHA).then_inc(s["sg_ready"], 1)

            for k in range(RING):
                expert(k, k, True)
            with act.Fori(1, E // RING) as i:
                for k in range(RING):
                    expert(i * RING + k, k, False)
            act.preload_act_table_set("natural_log_exp_and_others")
            act.wait_ge(s["xc_ready"], 3)
            norm(2, xc[:, :], 0, 1)
            act.wait_ge(s["near_known"], 1)
            short = act.value_load(near_i[0:1, 0:1], min_val=0, max_val=1)

            def half_keys_out(l, hf):
                act.wait_ge(s["n_k"], l * 2 + (hf + 1))
                for g in range(GR):
                    q = slice(32 * g, 32 * g + 32)
                    last = fn(Kz[q, hf * HB:(hf + 1) * HB, g, :],
                              heads3(qk[:, 1, :])[q, hf * HB:(hf + 1) * HB, :], ACT.Copy)
                last.then_inc(s["n_kz"], 1)

            def near_exps(l, u):
                act.wait_ge(s["csub_done"], l * UNITS + (u + 1))
                v = Pc[:, u, :, :].rearrange("p c k -> p (c k)")
                fn(v, v, ACT.Exp, scale=SCALE).then_inc(s["cexp_done"], 1)

            def near_evac(l, u):
                act.wait_ge(s["cturned"], l * UNITS + (u + 1))
                fn(PTc[:, u, :, :].rearrange("p c q -> p (c q)"), PS[:, 2 + u % 2, 0:4 * PB],
                   ACT.Copy).then_inc(s["cpt_ready"], 1)

            def near_out(l, u):
                act.wait_ge(s["cot_done"], l * UNITS + (u + 1))
                fn(o[:, 2 * u * L:2 * (u + 1) * L], PS[:, 4 + u % 2, 300:300 + 2 * L], ACT.Copy)\
                    .then_inc(s["near_out"], 1)

            def half_squares(x, n, hf):
                act.wait_ge(s["n_x"], x)
                fn(sq[:, hf * HT:(hf + 1) * HT], xl[:, hf * HT:(hf + 1) * HT], ACT.Square).then_inc(s["n_sq"], 1)

            def half_rstd(n, hf):
                act.wait_ge(s["n_ms"], n + 1)
                c = slice(hf * HT, (hf + 1) * HT)
                fn(rs[:, c], PS[:, 7, c], ACT.Ln, bias=eps[:, 1:2]).then_inc(s["n_ln"], 1)
                act.wait_ge(s["n_ln"], n + 1)
                fn(rs[:, c], rs[:, c], ACT.Exp, scale=-0.5).then_inc(s["n_rs"], 1)

            def cross_long(l):
                with act.Fori(0, B) as b:
                    lb = l * B + b
                    act.wait_ge(s["far_kv"], lb + 1)
                    fn(gv.rearrange("p (c n) -> p c n", c=3), PS[:, 3:6, 0:SB], ACT.Copy).then_inc(s["gv_ready"], 1)
                    act.wait_ge(s["far_vt"], lb + 1)
                    fn(gV.rearrange("p c d -> p (c d)"), PS[0:KC, 3:6, :].rearrange("p k c -> p (k c)"), ACT.Copy)\
                        .then_inc(s["gV_ready"], 1)
                    with act.Fori(0, H) as hh_:
                        t = lb * H + hh_
                        act.wait_ge(s["fm_ready"], t + 1)
                        fn(gp, gp, ACT.Exp, scale=SCALE, accum_out=fmx[:, 2:3])\
                            .then_inc(s["fe_ready"], 1)
                        act.wait_ge(s["ft_ready"], t + 1)
                        fn(gPT, PS[0:KC, 6:8, :].rearrange("p k (c n) -> p (k c) n", n=64)[:, 0:NK, 0:L], ACT.Copy)\
                            .then_inc(s["fpt_ready"], 1)

            with act.If(short == 1):
                act.wait_ge(s["near_ready"], 1)
                half_squares(1, 0, 0)
                with act.Fori(0, NL) as l:
                    act.preload_act_table_set("natural_log_exp_and_others")
                    half_rstd(l * 6, 0)
                    half_squares(l * 6 + 1, l * 6 + 1, 1)
                    half_rstd(l * 6 + 1, 1)
                    act.wait_ge(s["ckv_done"], l * 2 + 1)
                    for g in range(GR):
                        last = fn(Kc[32 * g:32 * g + 32, :, g, :],
                                  PS[32 * g:32 * g + 32, 0, 0:B * NEAR].rearrange("p (b k) -> p b k", b=B), ACT.Copy)
                    last.then_inc(s["ckv_ready"], 1)
                    half_keys_out(l, 0)
                    act.wait_ge(s["proj_done"], l + 1)
                    values_out(l + 1)
                    half_keys_out(l, 1)
                    r = l + 1
                    attention_start(r)
                    half_squares(l * 6 + 2, l * 6 + 2, 0)
                    out_part(r, 4)
                    evac(r, 7)
                    out_part(r, 5)
                    half_rstd(l * 6 + 2, 0)
                    out_part(r, 6)
                    act.wait_ge(s["ckv_done"], l * 2 + 2)
                    v = PS[:, 0:2, :].rearrange("p k (b c) -> p (k b) c", c=D)
                    for g in range(GR):
                        last = fn(Vc[32 * g:32 * g + 32, :, :, g, 0:HV],
                                  v[32 * g:32 * g + 32, :, 32 * g:32 * g + 32].rearrange("p b (j c) -> p b j c", j=2),
                                  ACT.Copy)
                    last.then_inc(s["ckv_ready"], 1)
                    out_part(r, 7)
                    half_squares(l * 6 + 3, l * 6 + 3, 1)
                    near_exps(l, 0)
                    half_rstd(l * 6 + 3, 1)
                    near_evac(l, 0)
                    near_exps(l, 1)
                    act.wait_ge(s["n_qc"], l * 2 + 2)
                    for j in range(HG):
                        last = fn(Q4c[:, HB:B, j, :], heads3(PS[:, 7, 0:T])[:, HB:B, :], ACT.Copy,
                                  scale=colv(V_SEL + j))
                    last.then_inc(s["n_q4c"], 1)
                    near_evac(l, 1)
                    near_exps(l, 2)
                    near_out(l, 0)
                    near_exps(l, 3)
                    near_evac(l, 2)
                    near_out(l, 1)
                    half_squares(l * 6 + 4, l * 6 + 4, 0)
                    near_evac(l, 3)
                    half_rstd(l * 6 + 4, 0)
                    near_out(l, 2)
                    near_out(l, 3)
                    half_squares(l * 6 + 5, l * 6 + 5, 1)
                    half_rstd(l * 6 + 5, 1)
                    for i in range(2 * FC):
                        hf, c = i // FC, i % FC
                        act.wait_ge(s["n_up"], l * 2 * FC + (i + 1))
                        fn(sl[:, c, hf * HT:(hf + 1) * HT], PS[:, i % 2, 0:HT], ACT.Silu).then_inc(s["n_silu"], 1)
                        if i == 2 * FC - 2:
                            half_squares(l * 6 + 6, l * 6 + 6, 0)
                act.wait_ge(s["n_ms"], 6 * NL + 1)
            with act.If(short == 0):
                with act.Fori(0, NL) as l:
                    act.preload_act_table_set("natural_log_exp_and_others")
                    act.wait_ge(s["norm_ready"], l * 3 + 4)
                    act.wait_ge(s["x_ready"], l * 3 + 2)
                    norm(l * 3 + 3, xl[:, :], 1, 1)
                    act.wait_ge(s["proj_done"], l + 1)
                    values_out(l + 1)
                    act.wait_ge(s["n_k"], l + 1)
                    keys_out(qk[:, 1, :])
                    attention(l + 1)
                    act.wait_ge(s["x_ready"], l * 3 + 3)
                    norm(l * 3 + 4, xl[:, :], 1, 1)
                    cross_long(l)
                    act.wait_ge(s["x_ready"], l * 3 + 4)
                    norm(l * 3 + 5, xl[:, :], 1, 1)
                    for c in range(FC):
                        act.wait_ge(s["g_done"], l * FC + (c + 1))
                        fn(sl[:, c, :], PS[:, 2 * (c % 2), 0:T], ACT.Silu).then_inc(s["n_silu"], 1)
                act.wait_ge(s["ms_ready"], 3 + 3 * NL)

            def last_norm(i, src, e):
                fn(sq[:, :], src, ACT.Square).then_inc(s["sq_last"], 1)
                act.wait_ge(s["ms_last"], i + 1)
                fn(rs[:, :], PS[:, 7, 0:T], ACT.Ln, bias=eps[:, e:e + 1]).then_inc(s["ln_last"], 1)
                act.wait_ge(s["ln_last"], i + 1)
                fn(rs[:, :], rs[:, :], ACT.Exp, scale=-0.5).then_inc(s["rs_last"], 1)

            act.preload_act_table_set("natural_log_exp_and_others")
            act.wait_ge(s["layers_done"], 1)
            last_norm(0, xl[:, :], 1)
            act.wait_ge(s["xc_ready"], 4)
            last_norm(1, xc[:, :], 0)
            act.wait_ge(s["bias1_ready"], 1)
            for c in range(FC):
                act.wait_ge(s["up_done"], c + 1)
                fn(hh[:, c, :], PS[:, c, 0:T], ACT.Relu, bias=bq[:, c:c + 1], scale=ss[:, c:c + 1])\
                    .then_inc(s["relu_done"], 1)

        @block.vector
        def _(dve):
            v_ = nc.vector

            def layer_norm(i, k, src, dst, rstd="rstd_ready", ready="norm_ready"):
                dve.wait_ge(s["mean_ready"], i + 1)
                v_.tensor_tensor(xc[:, :], src, PS[:, 6, 0:T], ALU.subtract).then_inc(s["xc_ready"], 1)
                dve.wait_ge(s["xc_ready"], i + 1)
                dve.wait_ge(s[rstd], k + 1)
                v_.tensor_tensor(dst, xc[:, :], rs[:, :], ALU.mult).then_inc(s[ready], 1)

            def rms_norm(k, src, w, dst):
                dve.wait_ge(s["rstd_ready"], k + 1)
                v_.scalar_tensor_tensor(dst, src, w, rs[:, :], ALU.mult, ALU.mult).then_inc(s["norm_ready"], 1)

            def queries_out(dst, src, ready):
                for j in range(HG):
                    last = v_.tensor_scalar(dst[:, :, j, :], heads3(src), colv(V_SEL + j), None, ALU.mult)
                last.then_inc(s[ready], 1)

            def normalise(v, nh, w, r, dst, own):
                v = v.rearrange("p (c x) -> p c x", x=CO)
                own(v_.reciprocal(r.unsqueeze(2), v[:, :, HV:CO]))
                own(v_.tensor_tensor(w, r.unsqueeze(2).broadcast_to([PB, nh, 2]),
                                     vec[0:PB, V_ROW:V_ROW + 2].unsqueeze(1).broadcast_to([PB, nh, 2]), ALU.mult))
                return v_.tensor_tensor(dst, v[:, :, 0:HV].rearrange("p c (j d) -> p c j d", j=2),
                                        w.unsqueeze(3).broadcast_to([PB, nh, 2, DH]), ALU.mult)

            def softmax(r, b, own):
                dve.wait_ge(s["s_ready"], r * B + (b + 1))
                src = PS[0:PB, b % 2, 0:8 * L].rearrange("p (c l) -> p c l", l=L)
                m = mxs[:, b // 2 % 2, 8 * (b % 2):8 * (b % 2) + 8]
                own(v_.tensor_reduce(m, src, AX.X, ALU.max))
                if b >= 4:
                    dve.wait_ge(s["turned"], r * B + (b - 3))
                v_.tensor_tensor(P[:, b // 2 % 2, b % 2, :, :], src, m.unsqueeze(2).broadcast_to([PB, 8, L]),
                                 ALU.subtract).then_inc(s["sub_done"], 1)

            def out_norm(r, b, own):
                dve.wait_ge(s["pv_done"], r * B + (b + 1))
                if b >= 4:
                    dve.wait_ge(s["ot_done"], r * B + (b - 3))
                u, k = b // 2 % 2, b % 2
                normalise(PS[0:PB, 4 + b % 2, 0:8 * CO], 8, wgt[:, u, 8 * k:8 * k + 8, :], rcp[:, u, 8 * k:8 * k + 8],
                          O[:, u, k, :].rearrange("p (c j d) -> p c j d", j=2, d=DH), own).then_inc(s["on_ready"], 1)

            def attention_start(r, own):
                softmax(r, 0, own)
                softmax(r, 1, own)
                softmax(r, 2, own)
                for b in range(B - 3):
                    out_norm(r, b, own)
                    softmax(r, b + 3, own)
                out_norm(r, 5, own)

            def attention(r, own):
                attention_start(r, own)
                out_norm(r, 6, own)
                out_norm(r, 7, own)

            own = Chain(dve, s["dve_a"])
            dve.wait_ge(s["d_x"], 16)
            dve.wait_ge(s["d_vec"], 16)
            dve.wait_ge(s["mean_ready"], 1)
            v_.tensor_tensor(xc[:, :], xin[:, :], PS[:, 6, 0:T], ALU.subtract).then_inc(s["xc_ready"], 1)
            dve.wait_ge(s["qp_copied"], 1)
            dve.wait_ge(s["rstd_ready"], 1)
            v_.tensor_tensor(h[:, :], qpT[:, 0:T], rs[:, :], ALU.mult).then_inc(s["norm_ready"], 1)
            dve.wait_ge(s["norm_ready"], 1)
            queries_out(Q4, h[:, :], "q4_ready")
            for u in range(UNITS):
                dve.wait_ge(s["cand_scores"], u + 1)
                src = PS[:, 3 * (u % 2):3 * (u % 2) + 3, :].rearrange("p k c -> p (k c)")[:, 0:S]
                own(v_.max(mx8[:, :], src))
                own(v_.max_index(idx8[:, :], mx8[:, :], src))
                v_.tensor_tensor(rows[:, u:u + 1], idx8[:, 0:1], colv(V_BASE + u), ALU.add)\
                    .then_inc(s["rows_ready"], 1)
            attention_start(0, own)
            dve.wait_ge(s["d_segrow"], 16)
            own(v_.tensor_copy(segrf[:, :], segrow[:, :]))
            v_.tensor_reduce(lim[:, 0:1], segrf[:, :], AX.X, ALU.max)
            own(v_.tensor_reduce(lim[:, 1:2], segrf[:, :], AX.X, ALU.min))
            own(v_.tensor_scalar(lim[:, 2:3], lim[:, 0:1], NEAR - 0.5, None, ALU.is_lt))
            own(v_.tensor_scalar(lim[:, 3:4], lim[:, 1:2], 0.0, lim[:, 2:3], ALU.is_ge, ALU.mult))
            v_.tensor_copy(near_i[:, :], lim[:, 3:4]).then_inc(s["near_known"], 1)
            out_norm(0, 6, own)
            out_norm(0, 7, own)
            dve.wait_ge(s["d_seg"], 16)
            dve.wait_ge(s["krow_ready"], 1)
            own(v_.tensor_copy(segf[:, 0, :], seg[:, :]))
            own(v_.tensor_scalar(segf[:, 1, :], segf[:, 0, :], -float(LOOKBACK), None, ALU.add))
            keys = krowf[:, :].unsqueeze(1).broadcast_to([PB, B, NEAR])
            v_.tensor_tensor(xm[:, 0, :, :], keys, segf[:, 0, :].unsqueeze(2).broadcast_to([PB, B, NEAR]), ALU.is_gt)
            own(v_.tensor_tensor(xm[:, 1, :, :], keys, segf[:, 1, :].unsqueeze(2).broadcast_to([PB, B, NEAR]),
                                 ALU.is_le))
            own(v_.tensor_tensor(xm[:, 0, :, :], xm[:, 0, :, :], xm[:, 1, :, :], ALU.add))
            v_.tensor_scalar(xbias[:, :, :].rearrange("p b (g k) -> p b g k", g=GR),
                             xm[:, 0, :, :].unsqueeze(2).broadcast_to([PB, B, GR, NEAR]), NEG, None, ALU.mult)\
                .then_inc(s["xbias_ready"], 1)
            dve.wait_ge(s["wo_done"], 1)
            v_.tensor_tensor(x1[:, :], xin[:, :], PS[:, 0, 0:T], ALU.add).then_inc(s["x_ready"], 1)

            dve.wait_ge(s["mean_ready"], 2)
            v_.tensor_tensor(xc[:, :], x1[:, :], PS[:, 6, 0:T], ALU.subtract).then_inc(s["xc_ready"], 1)
            dve.wait_ge(s["xc_ready"], 2)
            dve.wait_ge(s["d_wq"], 32)
            v_.tensor_reduce(sw[:, 0:FC], w1n[:, :, :], AX.X, ALU.max, apply_absolute_value=True)
            own(v_.tensor_reduce(sw[:, FC:FC + 1], w2n[:, :], AX.X, ALU.max, apply_absolute_value=True))
            own(v_.tensor_scalar(sw[:, 0:5], sw[:, 0:5], 1e-8, 1.0 / 127.0, ALU.max, ALU.mult))
            own(v_.reciprocal(swi[:, 0:5], sw[:, 0:5]))
            for c in range(FC):
                v_.tensor_scalar(wt[:, 0, c * D:(c + 1) * D], w1n[:, c, :], swi[:, c:c + 1], MAGIC, ALU.mult, ALU.add)
            own(v_.tensor_scalar(wt[:, 1, :], w2n[:, :], swi[:, FC:FC + 1], MAGIC, ALU.mult, ALU.add))
            own(v_.tensor_scalar(wt[:, :, :], wt[:, :, :], -MAGIC, -128.0, ALU.add, ALU.max))
            v_.tensor_scalar(wqb[:, :, :], wt[:, :, :], 127.0, None, ALU.min).then_inc(s["wq_ready"], 1)
            dve.wait_ge(s["rstd_ready"], 2)
            v_.scalar_tensor_tensor(h[:, :], xc[:, :], colv(V_SCALE), tq[:, 1, :], ALU.mult, ALU.mult)\
                .then_inc(s["norm_ready"], 1)
            dve.wait_ge(s["rstd_ready"], 3)
            v_.tensor_tensor(xh[:, :], xc[:, :], rs[:, :], ALU.mult).then_inc(s["norm_ready"], 1)
            dve.wait_ge(s["gate_done"], 1)
            dve.wait_ge(s["d_gw"], 32)
            own(v_.tensor_tensor(gl[:, :, :], PS[0:PB, 7, 0:UNITS * E].rearrange("p (u e) -> p u e", e=E),
                                 gb[:, :].unsqueeze(1).broadcast_to([PB, UNITS, E]), ALU.add))
            for u in range(UNITS):
                v = v_.max(gm8[:, u, :], gl[:, u, :])
            own(v)
            for u in range(UNITS):
                v = v_.max_index(gi8[:, u, :], gm8[:, u, :], gl[:, u, :])
            own(v)
            dve.wait_ge(s["consts"], 13)
            own(v_.tensor_copy(gif[:, :, :], gi8[:, :, 0:TOPK]))
            v_.tensor_tensor(ge[:, :, :], gl[:, :, :], gm8[:, :, 0:1].broadcast_to([PB, UNITS, E]), ALU.subtract)\
                .then_inc(s["gexp_in"], 1)
            own(v_.tensor_tensor(eq[:, :, :, :],
                                 eiof[:, :].unsqueeze(1).unsqueeze(3).broadcast_to([PB, UNITS, E, TOPK]),
                                 gif[:, :, :].unsqueeze(2).broadcast_to([PB, UNITS, E, TOPK]), ALU.is_equal))
            own(v_.tensor_reduce(gl[:, :, :], eq[:, :, :, :], AX.X, ALU.add))
            dve.wait_ge(s["gexp_done"], 1)
            own(v_.tensor_tensor(gl[:, :, :], gl[:, :, :], ge[:, :, :], ALU.mult))
            own(v_.tensor_reduce(gsum[:, :], gl[:, :, :], AX.X, ALU.add))
            own(v_.reciprocal(gsum[:, :], gsum[:, :]))
            own(v_.tensor_tensor(ge[:, :, :], gl[:, :, :], gsum[:, :].unsqueeze(2).broadcast_to([PB, UNITS, E]),
                                 ALU.mult))
            dve.wait_ge(s["krow_ready"], 1)
            own(v_.tensor_copy(gsplit[:, :, 0:E], ge[:, :, :]))
            own(v_.tensor_tensor(grest[:, 0, :, :], ge[:, :, :], gsplit[:, :, 0:E], ALU.subtract))
            own(v_.tensor_copy(gsplit[:, :, 32:32 + E], grest[:, 0, :, :]))
            own(v_.tensor_tensor(grest[:, 1, :, :], grest[:, 0, :, :], gsplit[:, :, 32:32 + E], ALU.subtract))
            v_.tensor_copy(gsplit[:, :, 64:64 + E], grest[:, 1, :, :]).then_inc(s["route_ready"], 1)
            dve.wait_ge(s["route_turned"], 1)
            v_.tensor_copy(rb[:, :], PS[0:96, 7, 0:T]).then_inc(s["rb_ready"], 1)
            dve.wait_ge(s["route_turned"], 2)
            v_.tensor_copy(routeT[:, :], PS[0:E, 6, 0:T]).then_inc(s["rb_ready"], 1)

            def gate_clamp(e, k):
                dve.wait_ge(s["g1_ready"], e + 1)
                v_.tensor_scalar(xg[:, k % 2, :], xg[:, k % 2, :], LIMIT, None, ALU.min).then_inc(s["xg_ready"], 1)

            def expert(e, k, first, last=False):
                bank = 3 * (k % 2)
                dve.wait_ge(s["l1_ready"], e + 1)
                v_.tensor_scalar(l2[:, k % 2, :], l1[:, k % 2, :], LIMIT, LIMIT, ALU.max, ALU.min)\
                    .then_inc(s["l2_ready"], 1)
                dve.wait_ge(s["l2_ready"], e + 1)
                v_.scalar_tensor_tensor(ww[:, k % 2, :], l2[:, k % 2, :], 1.0, PS[:, bank + 2, 0:T],
                                        ALU.add, ALU.mult).then_inc(s["ww_ready"], 1)
                dve.wait_ge(s["sg_ready"], e + 1)
                v_.tensor_tensor(vv[:, k % 2, :], xg[:, k % 2, :], sg[:, k % 2, :], ALU.mult)\
                    .then_inc(s["vv_ready"], 1)
                if not last:
                    gate_clamp(e + 1, k + 1)
                dve.wait_ge(s["ww_ready"], e + 1)
                dve.wait_ge(s["vv_ready"], e + 1)
                if not first or k >= 2:
                    dve.wait_ge(s["y_done"], e - 1)
                v_.tensor_tensor(zz[:, k % 2, :], ww[:, k % 2, :], vv[:, k % 2, :], ALU.mult)\
                    .then_inc(s["zz_ready"], 1)

            gate_clamp(0, 0)
            for k in range(RING):
                expert(k, k, True)
            with dve.Fori(1, E // RING - 1) as i:
                for k in range(RING):
                    expert(i * RING + k, k, False)
            for k in range(RING):
                expert(E - RING + k, k, False, last=k == RING - 1)
            own(v_.tensor_tensor(x2[:, :], x1[:, :], xh[:, :], ALU.add))
            dve.wait_ge(s["y_done"], E)
            v_.tensor_tensor(x2[:, :], x2[:, :], PS[:, 6, 0:T], ALU.add).then_inc(s["x_ready"], 1)

            layer_norm(2, 3, x2[:, :], xl[:, :])
            dve.wait_ge(s["d_par"], 16)
            dve.wait_ge(s["d_cs"], 16)
            dve.wait_ge(s["near_known"], 1)
            short = dve.value_load(near_i[0:1, 0:1], min_val=0, max_val=1)

            def near_softmax(l, u, own):
                dve.wait_ge(s["cs_ready"], l * UNITS + (u + 1))
                src = PS[0:PB, u % 2, :].rearrange("p (c k) -> p c k", k=NEAR)
                own(v_.tensor_reduce(mxs[:, u % 2, :], src, AX.X, ALU.max))
                v_.tensor_tensor(Pc[:, u, :, :], src, mxs[:, u % 2, :].unsqueeze(2).broadcast_to([PB, 16, NEAR]),
                                 ALU.subtract).then_inc(s["csub_done"], 1)

            def near_out_norm(l, u, own):
                dve.wait_ge(s["cpv_done"], l * UNITS + (u + 1))
                if u >= 2:
                    dve.wait_ge(s["cot_done"], l * UNITS + (u - 1))
                normalise(PS[0:PB, 4 + u % 2, 0:16 * CO], 16, wgt[:, u % 2, :, :], rcp[:, u % 2, :],
                          O[:, u % 2, :, :].rearrange("p k (c j d) -> p (k c) j d", j=2, d=DH), own)\
                    .then_inc(s["con_ready"], 1)

            def half(ap, hf):
                return ap[:, hf * HT:(hf + 1) * HT]

            def half_norm(n, w, hf):
                dve.wait_ge(s["n_rs"], n + 1)
                v_.scalar_tensor_tensor(half(h, hf), half(xl, hf), w, half(rs, hf), ALU.mult, ALU.mult)\
                    .then_inc(s["n_h"], 1)

            def half_add(done, n, hf, x, bias=False, bank=6):
                dve.wait_ge(s[done], n)
                if bias:
                    v_.scalar_tensor_tensor(half(xl, hf), PS[:, bank, hf * HT:(hf + 1) * HT], bo2[:, 0:1], half(xl, hf),
                                            ALU.add, ALU.add).then_inc(s["n_x"], 1)
                else:
                    v_.tensor_tensor(half(xl, hf), PS[:, bank, hf * HT:(hf + 1) * HT], half(xl, hf), ALU.add)\
                        .then_inc(s["n_x"], 1)
                dve.wait_ge(s["n_x"], x)

            def cross_long(l):
                dve.wait_ge(s["n_qc"], l + 1)
                v_.tensor_copy(tq[:, 0, :], PS[:, 1, 0:T]).then_inc(s["far_step"], 1)
                with dve.Fori(0, B) as b:
                    lb = l * B + b
                    fb = Chain(dve, s["dve_fb"], lb * 7)
                    dve.wait_ge(s["far_step"], l * (B + 1) + b + 1)
                    fb(v_.tensor_copy(gq, tq[:, 0, bass.ds(b * L, L)]))
                    for k in range(3):
                        fb(v_.tensor_scalar(gi[:, k * SB:(k + 1) * SB], frow[:, :], float(k * SB), None, ALU.add))
                    fb(v_.tensor_scalar(gb_, gi, segf[0:L, 0, bass.ds(b, 1)], NEG, ALU.is_gt, ALU.mult))
                    fb(v_.tensor_scalar(gi, gi, segf[0:L, 1, bass.ds(b, 1)], NEG, ALU.is_le, ALU.mult))
                    fb(v_.tensor_tensor(gb_, gb_, gi, ALU.add))
                    dve.wait_ge(s["far_kv"], lb + 1)
                    v_.tensor_copy(gk.rearrange("p (c n) -> p c n", c=3), PS[:, 0:3, 0:SB]).then_inc(s["gk_ready"], 1)
                    with dve.Fori(0, H) as hh_:
                        t = lb * H + hh_
                        fh = Chain(dve, s["dve_fh"], t * 4)
                        dve.wait_ge(s["gk_ready"], lb + 1)
                        v_.tensor_scalar(gqz, gq, vec[:, bass.ds(hh_ + V_HEAD, 1)], None, ALU.mult)\
                            .then_inc(s["gq_ready"], 1)
                        dve.wait_ge(s["fs_ready"], t + 1)
                        fh(v_.tensor_tensor(gp.rearrange("p (c n) -> p c n", c=3), PS[0:L, 0:3, 0:SB],
                                            gb_.rearrange("p (c n) -> p c n", c=3), ALU.add))
                        fh(v_.tensor_reduce(fmx[:, 0:1], gp, AX.X, ALU.max))
                        v_.tensor_scalar(gp, gp, fmx[:, 0:1], None, ALU.subtract).then_inc(s["fm_ready"], 1)
                        dve.wait_ge(s["fo_ready"], t + 1)
                        fh(v_.reciprocal(fmx[:, 0:1], fmx[:, 2:3]))
                        fh(v_.tensor_scalar(gO[:, bass.ds(hh_ * DH, DH)], PS[0:L, 3, 0:DH], fmx[:, 0:1], None,
                                            ALU.mult))
                    v_.tensor_copy(gOc, gO).then_inc(s["fO_ready"], 1)
                    dve.wait_ge(s["ff_ready"], lb + 1)
                    v_.tensor_copy(o[:, bass.ds(b * L, L)], PS[:, 4, 0:L]).then_inc(s["far_step"], 1)
                dve.wait_ge(s["far_step"], l * (B + 1) + (B + 1))
                v_.tensor_copy(tq[:, 1, 0:1], o[:, 0:1]).then_inc(s["oc_ready"], 1)

            with dve.If(short == 1):
                dve.wait_ge(s["norm_ready"], 4)
                v_.tensor_copy(tq[:, 1, 0:1], xl[:, 0:1]).then_inc(s["n_x"], 1)
                with dve.Fori(0, NL) as l:
                    own = Chain(dve, s["dve_l"], l * NDVE)
                    v_.tensor_copy(pl[:, :], par[:, bass.ds(l, 1), :].rearrange("p l n -> p (l n)"))\
                        .then_inc(s["pl_ready"], 1)
                    dve.wait_ge(s["pl_ready"], l + 1)
                    half_norm(l * 6, pl[:, N1:N1 + 1], 0)

                    def rotary(hf, i, tmp, b1, b2):
                        c, bank = slice(hf * HT, (hf + 1) * HT), 4 + 2 * hf + i
                        dve.wait_ge(s["n_proj"], l * 4 + (2 * hf + i + 1))
                        v_.scalar_tensor_tensor(tmp[:, 0, c], PS[:, bank, 0:HT], pl[:, b1:b1 + 1], cs[:, 0, c],
                                                ALU.add, ALU.mult)
                        own(v_.scalar_tensor_tensor(tmp[:, 1, c], PS[:, bank, HT:T], pl[:, b2:b2 + 1],
                                                    cs[:, 1, c], ALU.add, ALU.mult))
                        return v_.tensor_tensor(qk[:, 1 - i, c], tmp[:, 0, c], tmp[:, 1, c], ALU.add)

                    rotary(0, 0, tk, BK, BKR).then_inc(s["n_k"], 1)
                    half_norm(l * 6 + 1, pl[:, N1:N1 + 1], 1)
                    dve.wait_ge(s["ckv_done"], l * 2 + 1)
                    v_.tensor_tensor(bo2[:, :], pl[:, BO:BO + 1], PS[:, 1, 0:1], ALU.add).then_inc(s["bo_ready"], 1)
                    dve.wait_ge(s["bo_ready"], l + 1)
                    own(rotary(0, 1, tq, BQ, BQR))
                    for j in range(HG):
                        last = v_.tensor_scalar(Q4[:, 0:HB, j, :], heads3(qk[:, 0, :])[:, 0:HB, :],
                                                colv(V_SEL + j), None, ALU.mult)
                    last.then_inc(s["q4_ready"], 1)
                    rotary(1, 1, tq, BQ, BQR).then_inc(s["n_q"], 1)
                    rotary(1, 0, tk, BK, BKR).then_inc(s["n_k"], 1)
                    r = l + 1
                    attention_start(r, own)
                    half_add("n_wo", l * 2 + 1, 0, l * 6 + 2, True)
                    out_norm(r, 6, own)
                    half_norm(l * 6 + 2, pl[:, N2:N2 + 1], 0)
                    out_norm(r, 7, own)
                    dve.wait_ge(s["n_qc"], l * 2 + 1)
                    for j in range(HG):
                        last = v_.tensor_scalar(Q4c[:, 0:HB, j, :], heads3(PS[:, 7, 0:T])[:, 0:HB, :],
                                                colv(V_SEL + j), None, ALU.mult)
                    last.then_inc(s["n_q4c"], 1)
                    half_add("n_wo", l * 2 + 2, 1, l * 6 + 3, True)
                    near_softmax(l, 0, own)
                    near_softmax(l, 1, own)
                    half_norm(l * 6 + 3, pl[:, N2:N2 + 1], 1)
                    near_out_norm(l, 0, own)
                    near_softmax(l, 2, own)
                    near_out_norm(l, 1, own)
                    near_softmax(l, 3, own)
                    half_add("n_woc", l * 2 + 1, 0, l * 6 + 4)
                    near_out_norm(l, 2, own)
                    half_norm(l * 6 + 4, pl[:, N3:N3 + 1], 0)
                    near_out_norm(l, 3, own)
                    half_add("n_woc", l * 2 + 2, 1, l * 6 + 5)
                    half_norm(l * 6 + 5, pl[:, N3:N3 + 1], 1)
                    for i in range(2 * FC):
                        hf, c = i // FC, i % FC
                        dve.wait_ge(s["n_silu"], l * 2 * FC + (i + 1))
                        v_.tensor_tensor(mm[:, c, hf * HT:(hf + 1) * HT], sl[:, c, hf * HT:(hf + 1) * HT],
                                         PS[:, 2 + i % 2, 0:HT], ALU.mult).then_inc(s["n_m"], 1)
                        if i == FC + 1:
                            half_add("n_down", l * 2 + 1, 0, l * 6 + 6, bank=4)
                    half_add("n_down", l * 2 + 2, 1, l * 6 + 7, bank=5)
                    v_.tensor_copy(tq[:, 1, 0:1], xl[:, 0:1])
                    assert own.n == NDVE, own.n
                v_.tensor_copy(tq[:, 1, 1:2], xl[:, 0:1]).then_inc(s["layers_done"], 1)
            with dve.If(short == 0):
                with dve.Fori(0, NL) as l:
                    own = Chain(dve, s["dve_l"], l * NDVE_LONG)
                    v_.tensor_copy(pl[:, :], par[:, bass.ds(l, 1), :].rearrange("p l n -> p (l n)"))\
                        .then_inc(s["pl_ready"], 1)
                    dve.wait_ge(s["pl_ready"], l + 1)
                    dve.wait_ge(s["norm_ready"], l * 3 + 4)
                    dve.wait_ge(s["x_ready"], l * 3 + 2)
                    rms_norm(l * 3 + 4, xl[:, :], pl[:, N1:N1 + 1], h[:, :])
                    for i, (t, b1, b2) in enumerate(((tq, BQ, BQR), (tk, BK, BKR))):
                        dve.wait_ge(s["n_proj"], l * 4 + (2 * i + 1))
                        v_.scalar_tensor_tensor(t[:, 0, :], PS[:, 4 + 2 * i, 0:T], pl[:, b1:b1 + 1], cs[:, 0, :],
                                                ALU.add, ALU.mult)
                        dve.wait_ge(s["n_proj"], l * 4 + (2 * i + 2))
                        own(v_.scalar_tensor_tensor(t[:, 1, :], PS[:, 5 + 2 * i, 0:T], pl[:, b2:b2 + 1], cs[:, 1, :],
                                                    ALU.add, ALU.mult))
                        add = v_.tensor_tensor(qk[:, i, :], t[:, 0, :], t[:, 1, :], ALU.add)
                        if i == 1:
                            add.then_inc(s["n_k"], 1)
                        else:
                            own(add)
                            queries_out(Q4, qk[:, 0, :], "q4_ready")
                    dve.wait_ge(s["ckv_done"], l + 1)
                    v_.tensor_tensor(bo2[:, :], pl[:, BO:BO + 1], PS[:, 1, 0:1], ALU.add).then_inc(s["bo_ready"], 1)
                    dve.wait_ge(s["bo_ready"], l + 1)
                    attention(l + 1, own)
                    dve.wait_ge(s["wo_done"], l + 2)
                    v_.scalar_tensor_tensor(xl[:, :], PS[:, 0, 0:T], bo2[:, 0:1], xl[:, :], ALU.add, ALU.add)\
                        .then_inc(s["x_ready"], 1)
                    dve.wait_ge(s["x_ready"], l * 3 + 3)
                    rms_norm(l * 3 + 5, xl[:, :], pl[:, N2:N2 + 1], h[:, :])
                    cross_long(l)
                    dve.wait_ge(s["n_woc"], l + 1)
                    v_.tensor_tensor(xl[:, :], xl[:, :], PS[:, 0, 0:T], ALU.add).then_inc(s["x_ready"], 1)
                    dve.wait_ge(s["x_ready"], l * 3 + 4)
                    rms_norm(l * 3 + 6, xl[:, :], pl[:, N3:N3 + 1], h[:, :])
                    for c in range(FC):
                        dve.wait_ge(s["n_silu"], l * FC + (c + 1))
                        dve.wait_ge(s["u_done"], l * FC + (c + 1))
                        v_.tensor_tensor(mm[:, c, :], sl[:, c, :], PS[:, 2 * (c % 2) + 1, 0:T], ALU.mult)\
                            .then_inc(s["n_m"], 1)
                    dve.wait_ge(s["n_down"], l + 1)
                    v_.tensor_tensor(xl[:, :], xl[:, :], PS[:, 4, 0:T], ALU.add).then_inc(s["x_ready"], 1)
                    assert own.n == NDVE_LONG, own.n
                dve.wait_ge(s["x_ready"], 2 + 3 * NL)
                v_.tensor_copy(tq[:, 1, 0:1], xl[:, 0:1]).then_inc(s["layers_done"], 1)
            own = Chain(dve, s["dve_d"])
            dve.wait_ge(s["rs_last"], 1)
            own(v_.scalar_tensor_tensor(h[:, :], xl[:, :], colv(V_NF), rs[:, :], ALU.mult, ALU.mult))
            v_.tensor_tensor(x3[:, :], x2[:, :], h[:, :], ALU.add).then_inc(s["layers_done"], 1)
            dve.wait_ge(s["layers_done"], 2)

            dve.wait_ge(s["wq_turned"], 1)
            v_.tensor_copy(w1qT[:, :], PS[:, 0, 0:256].bitcast(BF16))
            v_.tensor_copy(w2qT[:, :, :].rearrange("p c d -> p (c d)"), PS[:, 1, 0:256].bitcast(BF16))\
                .then_inc(s["wqT_ready"], 1)
            layer_norm(3, 1, x3[:, :], yt[:, :], "rs_last", "yt_ready")
            dve.wait_ge(s["yt_ready"], 1)

            def scale_of(i, c):
                dve.wait_ge(s["max_turned"], i + 1)
                own(v_.tensor_reduce(s11[0:1, 1:2], PS[0:1, 5, 0:D], AX.X, ALU.max))
                v_.tensor_scalar(s11[0:1, 2:3], s11[0:1, 1:2], 1e-8, 1.0 / 255.0, ALU.max, ALU.mult)\
                    .then_inc(s["s_one"], 1)
                dve.wait_ge(s["s_bcast"], i + 1)
                v_.tensor_copy(s11[:, c:c + 1], PS[:, 4, 0:1])
                own(v_.reciprocal(s11[:, c + 1:c + 2], PS[:, 4, 0:1]))

            def bias_of(c0, n, src, sc, ready):
                own(v_.tensor_scalar(ss[:, c0:c0 + n], sw[:, c0:c0 + n], s11[:, sc:sc + 1], None, ALU.mult))
                own(v_.reciprocal(swi[:, c0:c0 + n], ss[:, c0:c0 + n]))
                own(v_.tensor_tensor(bq[:, c0:c0 + n], src, swi[:, c0:c0 + n], ALU.mult))
                own(v_.tensor_scalar(bq[:, c0:c0 + n], bq[:, c0:c0 + n], MAGIC, -MAGIC, ALU.add, ALU.add))
                v_.tensor_tensor(bq[:, c0:c0 + n], bq[:, c0:c0 + n], ss[:, c0:c0 + n], ALU.mult).then_inc(s[ready], 1)

            v_.tensor_reduce(s11[:, 0:1], yt[:, :], AX.X, ALU.max).then_inc(s["max_in"], 1)
            scale_of(0, 3)
            own(v_.tensor_scalar(sq2[:, :], yt[:, :], s11[:, 4:5], MAGIC, ALU.mult, ALU.add))
            own(v_.tensor_scalar(sq2[:, :], sq2[:, :], -MAGIC, 0.0, ALU.add, ALU.max))
            v_.tensor_scalar(yq[:, :], sq2[:, :], 255.0, None, ALU.min).then_inc(s["yq_ready"], 1)
            bias_of(0, FC, colv(V_B1, FC), 3, "bias1_ready")
            for c in range(FC):
                dve.wait_ge(s["relu_done"], c + 1)
                v = v_.tensor_reduce(s11[:, 8 + c:9 + c], hh[:, c, :], AX.X, ALU.max)
            own(v)
            v_.tensor_reduce(s11[:, 0:1], s11[:, 8:8 + FC], AX.X, ALU.max).then_inc(s["max_in"], 1)
            scale_of(1, 6)
            own(v_.tensor_scalar(ht[:, :, :], hh[:, :, :], s11[:, 7:8], MAGIC, ALU.mult, ALU.add))
            for c in range(FC):
                v_.tensor_scalar(hq[:, c, :], ht[:, c, :], MAGIC + 255.0, -MAGIC, ALU.min, ALU.add)\
                    .then_inc(s["hq_ready"], 1)
            bias_of(FC, 1, colv(V_B2), 6, "bias2_ready")
            dve.wait_ge(s["bias2_ready"], 1)
            own(v_.tensor_scalar(yt[:, :], x3[:, :], bq[:, 4:5], None, ALU.add))
            dve.wait_ge(s["down_done"], 1)
            v_.scalar_tensor_tensor(yt[:, :], PS[:, 6, 0:T], ss[:, 4:5], yt[:, :], ALU.mult, ALU.add)\
                .then_inc(s["out_ready"], 1)


def kernel(**inputs):
    import concourse.bacc as _bacc
    from concourse.bass_utils import run_bass_kernel_spmd as _run

    g = {n: np.asarray(v) for n, v in inputs.items()}
    f32 = np.float32
    x, ctxt = g["x"], g["ctx_1024"]
    arr = {}
    arr["xT"] = x.reshape(T, D).T
    arr["ctx"] = ctxt.reshape(B * S, D)
    arr["ctxT"] = ctxt.reshape(B * S, D).T
    wkv = g["L0_xattn_Wkv"]
    arr["wa0"] = np.concatenate([g["L0_xattn_Wq"].T, np.tile(wkv[:DH], (H, 1)).T, np.tile(wkv[DH:], (H, 1)).T,
                                 g["L0_xattn_Wc"].T], axis=1)
    arr["gw"] = g["L0_ffn_gate_w"].T
    arr["gb"] = np.tile(g["L0_ffn_gate_b"][None], (PB, 1))
    m1, m1b = g["L0_ffn_mlp1_w"], g["L0_ffn_mlp1_b"]
    arr["ew"] = np.concatenate([m1[:, ::2].transpose(2, 0, 1), m1[:, 1::2].transpose(2, 0, 1),
                                g["L0_ffn_mlp2_w"].transpose(2, 0, 1)], axis=2).reshape(D, E * 3 * D)
    arr["b2e"] = g["L0_ffn_mlp2_b"]
    seg = g["itok_BxS_0_255"]
    arr["seg"] = np.tile(seg.T, (2, 1)).astype(np.int32)
    arr["segrow"] = seg.reshape(1, T).astype(np.int32)
    arr["w1n"] = g["L1_ffn_w1"].reshape(FC, D, D).transpose(1, 0, 2)
    arr["w2n"] = g["L1_ffn_w2"]
    inv = (1.0 / f32(10000.0) ** (np.arange(0, DH, 2, dtype=f32) / f32(DH))).astype(f32)
    ang = np.arange(L, dtype=f32)[:, None] * inv[None]
    half = DH // 2
    dim = np.arange(D) % DH
    cos, sin = np.cos(ang).astype(f32)[:, dim % half].T, np.sin(ang).astype(f32)[:, dim % half].T
    sin = np.where(dim[:, None] < half, -sin, sin)
    arr["cs"] = np.stack([np.tile(cos, (1, B)), np.tile(sin, (1, B))], axis=1).astype(f32)
    swap = np.arange(D) - dim + (dim + half) % DH
    wqkv, bqkv = g["L1_xattn_Wqkv"], g["L1_xattn_bqkv"]
    wq, wk, wv = wqkv[:, 0:D], wqkv[:, D:2 * D], wqkv[:, 2 * D:]
    bq_, bk_, bv_ = bqkv[:, 0:D], bqkv[:, D:2 * D], bqkv[:, 2 * D:]
    wkvc = g["L1_xattn_Wkv_c"]
    blocks = [wq, wq[:, swap], wk, wk[:, swap], wv, g["L1_xattn_Wo"], g["L1_xattn_Wq_c"], wkvc[:, :D], wkvc[:, D:],
              g["L1_xattn_Wo_c"]]
    arr["wA"] = np.concatenate([w.transpose(2, 0, 1) for w in blocks], axis=2).reshape(D, NL * WATT)
    down = g["L1_xattn_Wd"].reshape(NL, D, FC, D).transpose(3, 0, 2, 1).reshape(D, NL, FF)
    arr["wF"] = np.concatenate([g["L1_xattn_Wg"].transpose(2, 0, 1), g["L1_xattn_Wu"].transpose(2, 0, 1), down],
                               axis=2).reshape(D, NL * WFFN)
    arr["par"] = np.stack([bq_, bq_[:, swap], bk_, bk_[:, swap], bv_, g["L1_xattn_bo"], g["L1_xattn_n1"],
                           g["L1_xattn_n2"], g["L1_xattn_n3"]], axis=0).transpose(2, 1, 0)
    p = np.arange(D)
    sel = (p[:, None] // DH % HG == np.arange(HG)[None]).astype(f32)
    row = np.stack([p < L, (p >= L) & (p < PB)], axis=1).astype(f32)
    base = (2 * np.arange(UNITS)[None] + p[:, None] // 64).astype(f32) * f32(S)
    heads = (p[:, None] // DH == np.arange(H)[None]).astype(f32)
    arr["vec"] = np.concatenate([g["L0_ffn_scale"][:, None], g["L1_xattn_nf"][:, None], g["L1_ffn_b2"][:, None],
                                 g["L1_ffn_b1"].reshape(FC, D).T, sel, row, base, m1b[:, ::2].T, m1b[:, 1::2].T,
                                 heads], axis=1)
    nc = _bacc.Bacc("TRN2", target_bir_lowering=False, num_devices=1)
    feed, aps = {}, {}
    for name, v in arr.items():
        v = np.ascontiguousarray(v)
        feed[f"in_{name}"] = v
        aps[name] = nc.dram_tensor(f"in_{name}", v.shape, mybir.dt.from_np(v.dtype), kind="ExternalInput").ap()
    out = nc.dram_tensor("out_0", (D, T), F32, kind="ExternalOutput").ap()
    build(nc, aps, out)
    r = _run(nc, [feed], core_ids=[0])
    return r.results[0]["out_0"].T.reshape(B, L, D)
```
